# Optimizing a Trainium2 kernel written in Bass

```python
import numpy as np
import jax
import jax.numpy as jnp

def _softmax(x, axis=-1):
    return jax.nn.softmax(x, axis=axis)

def _gelu(x):
    return jax.nn.gelu(x, approximate=True)

def _silu(x):
    return jax.nn.silu(x)

def _sigmoid(x):
    return jax.nn.sigmoid(x)

def _layernorm(x, axis=-1, eps=1e-05):
    m = jnp.mean(x, axis=axis, keepdims=True)
    v = jnp.var(x, axis=axis, keepdims=True)
    return (x - m) / jnp.sqrt(v + eps)

def _scatter_add(tgt, idx, src, axis=0):
    return tgt.at[idx].add(src)

def _segment_sum(src, seg, n):
    return jax.ops.segment_sum(src, seg, n)
kernel_name = 'mk_cond_seq_d2_seqx_r8_87d913'

def setup_inputs(seed: int=0):
    np.random.seed(seed)
    _w = jnp.asarray

    def _rec_inputs():
        import jax
        import jax.numpy as jnp
        _rk = jax.random.key(seed)
        x = 7.22e-05 + 1 * jax.random.normal(jax.random.fold_in(_rk, 1), (16, 128, 256), jnp.float32)
        _lenS = 128 - jax.random.randint(jax.random.fold_in(_rk, 7), (16,), 0, max(1, 128 // 4) + 1, jnp.int32)
        _lenS2 = 128 - jax.random.randint(jax.random.fold_in(_rk, 8), (16,), 0, max(1, 128 // 4) + 1, jnp.int32)
        cond_2048 = 0.0061147 + 1.02565 * jax.random.normal(jax.random.fold_in(_rk, 11), (16, 256), jnp.float32)
        _validS = jnp.arange(128)[None, :] < _lenS[:, None]
        _validS2 = jnp.arange(128)[None, :] < _lenS2[:, None]
        _causal = jnp.tril(jnp.ones((128, 128), dtype=bool))
        mask_1x1xSxS_ff0 = jnp.where(jnp.ones((1, 1, 128, 128), dtype=bool), 0.0, -1000000000.0).astype(jnp.float32)
        return (x, cond_2048, mask_1x1xSxS_ff0)
    x, cond_2048, mask_1x1xSxS_ff0 = _rec_inputs()

    def _L0_cond_setup():
        import jax, jax.numpy as jnp
        import numpy as np
        B, L, C, H = (2, 256, 256, 16)
        COND = 256
        HID = 4 * C
        LN_EPS = 1e-06

        def _ln(x):
            m = jnp.mean(x, axis=-1, keepdims=True)
            v = jnp.mean((x - m) ** 2, axis=-1, keepdims=True)
            return (x - m) / jnp.sqrt(v + LN_EPS)

        def _gelu_tanh(u):
            c = np.sqrt(2.0 / np.pi).astype(np.float32)
            return 0.5 * u * (1.0 + jnp.tanh(c * (u + 0.044715 * u ** 3)))
        key = jax.random.key(seed)
        ks = jax.random.split(key, 8)
        s = 0.02
        return {'x': jax.random.normal(ks[0], (B, L, C), jnp.float32), 'cond_BD': jax.random.normal(ks[1], (B, COND), jnp.float32), 'attn_bias': jnp.zeros((1, 1, L, L), jnp.float32), 'Wqkv': jax.random.normal(ks[2], (3 * C, C), jnp.float32) * s, 'q_bias': jnp.zeros((C,), jnp.float32), 'v_bias': jnp.zeros((C,), jnp.float32), 'scale_mul_log': jnp.full((1, H, 1, 1), np.log(4.0), jnp.float32), 'Wproj': jax.random.normal(ks[3], (C, C), jnp.float32) * s, 'bproj': jnp.zeros((C,), jnp.float32), 'Wada': jax.random.normal(ks[4], (6 * C, COND), jnp.float32) * s, 'bada': jnp.zeros((6 * C,), jnp.float32), 'Wfc1': jax.random.normal(ks[5], (HID, C), jnp.float32) * s, 'bfc1': jnp.zeros((HID,), jnp.float32), 'Wfc2': jax.random.normal(ks[6], (C, HID), jnp.float32) * s, 'bfc2': jnp.zeros((C,), jnp.float32)}
    _L0_cond_all = _L0_cond_setup()
    _L0_cond_in = {k: v for k, v in _L0_cond_all.items() if k in ('Wqkv', 'q_bias', 'v_bias', 'scale_mul_log', 'Wproj', 'bproj', 'Wada', 'bada', 'Wfc1', 'bfc1', 'Wfc2', 'bfc2')}
    del _L0_cond_all

    def _L1_cond_setup():
        import jax, jax.numpy as jnp
        import numpy as np
        D_MODEL = 256
        N_HEADS = 16
        N_KV_HEADS = 4
        HEAD_DIM = D_MODEL // N_HEADS
        N_GROUPS = N_HEADS // N_KV_HEADS
        BLOCK_SIZE = 128
        WINDOW = 32
        GLOBAL_EVERY = 64
        LATENT = 64
        ROPE_THETA = 10000.0
        LN_EPS = 1e-05

        def _rope_tables(T, dtype):
            freqs = 1.0 / ROPE_THETA ** (jnp.arange(0, HEAD_DIM, 2, dtype=jnp.float32) / HEAD_DIM)
            emb = jnp.arange(T, dtype=jnp.float32)[:, None] * freqs[None, :]
            cos = jnp.concatenate([jnp.cos(emb), jnp.cos(emb)], axis=-1).astype(dtype)
            sin = jnp.concatenate([jnp.sin(emb), jnp.sin(emb)], axis=-1).astype(dtype)
            return (cos, sin)

        def _rotate_half(x):
            h = x.shape[-1] // 2
            return jnp.concatenate([-x[..., h:], x[..., :h]], axis=-1)

        def _sparse_mask(T):
            idx = jnp.arange(T)
            blk = idx // BLOCK_SIZE
            future_block = blk[None, :] > blk[:, None]
            outside_window = jnp.abs(idx[None, :] - idx[:, None]) > WINDOW
            global_visible = jnp.broadcast_to((idx % GLOBAL_EVERY == 0)[None, :], (T, T))
            return outside_window & ~global_visible | future_block
        key = jax.random.key(seed)
        ks = jax.random.split(key, 9)
        B, T = (2, 256)
        s = 0.02
        return {'x': jax.random.normal(ks[0], (B, T, D_MODEL), jnp.float32), 't_emb': jax.random.normal(ks[1], (B, D_MODEL), jnp.float32), 'W_ada': jax.random.normal(ks[2], (2 * D_MODEL, D_MODEL), jnp.float32) * s, 'b_ada': jnp.zeros((2 * D_MODEL,), jnp.float32), 'Wq': jax.random.normal(ks[3], (N_HEADS * HEAD_DIM, D_MODEL), jnp.float32) * s, 'Wkd': jax.random.normal(ks[4], (LATENT, D_MODEL), jnp.float32) * s, 'Wku': jax.random.normal(ks[5], (N_KV_HEADS * HEAD_DIM, LATENT), jnp.float32) * s, 'Wvu': jax.random.normal(ks[6], (N_KV_HEADS * HEAD_DIM, LATENT), jnp.float32) * s, 'Wo': jax.random.normal(ks[7], (D_MODEL, N_HEADS * HEAD_DIM), jnp.float32) * s}
    _L1_cond_all = _L1_cond_setup()
    _L1_cond_in = {k: v for k, v in _L1_cond_all.items() if k in ('W_ada', 'b_ada', 'Wq', 'Wkd', 'Wku', 'Wvu', 'Wo')}
    del _L1_cond_all
    return {'x': x, 'cond_2048': cond_2048, 'mask_1x1xSxS_ff0': mask_1x1xSxS_ff0, 'L0_cond_Wqkv': _L0_cond_in['Wqkv'], 'L0_cond_q_bias': _L0_cond_in['q_bias'], 'L0_cond_v_bias': _L0_cond_in['v_bias'], 'L0_cond_scale_mul_log': _L0_cond_in['scale_mul_log'], 'L0_cond_Wproj': _L0_cond_in['Wproj'], 'L0_cond_bproj': _L0_cond_in['bproj'], 'L0_cond_Wada': _L0_cond_in['Wada'], 'L0_cond_bada': _L0_cond_in['bada'], 'L0_cond_Wfc1': _L0_cond_in['Wfc1'], 'L0_cond_bfc1': _L0_cond_in['bfc1'], 'L0_cond_Wfc2': _L0_cond_in['Wfc2'], 'L0_cond_bfc2': _L0_cond_in['bfc2'], 'L1_cond_W_ada': _L1_cond_in['W_ada'], 'L1_cond_b_ada': _L1_cond_in['b_ada'], 'L1_cond_Wq': _L1_cond_in['Wq'], 'L1_cond_Wkd': _L1_cond_in['Wkd'], 'L1_cond_Wku': _L1_cond_in['Wku'], 'L1_cond_Wvu': _L1_cond_in['Wvu'], 'L1_cond_Wo': _L1_cond_in['Wo']}

def reference(x, cond_2048, mask_1x1xSxS_ff0, L0_cond_Wqkv, L0_cond_q_bias, L0_cond_v_bias, L0_cond_scale_mul_log, L0_cond_Wproj, L0_cond_bproj, L0_cond_Wada, L0_cond_bada, L0_cond_Wfc1, L0_cond_bfc1, L0_cond_Wfc2, L0_cond_bfc2, L1_cond_W_ada, L1_cond_b_ada, L1_cond_Wq, L1_cond_Wkd, L1_cond_Wku, L1_cond_Wvu, L1_cond_Wo):
    import jax
    import jax.numpy as jnp

    def _L0_cond_ref(x, cond_BD, attn_bias, Wqkv, q_bias, v_bias, scale_mul_log, Wproj, bproj, Wada, bada, Wfc1, bfc1, Wfc2, bfc2):
        import jax, jax.numpy as jnp
        import numpy as np
        B, L, C, H = (2, 256, 256, 16)
        COND = 256
        HID = 4 * C
        LN_EPS = 1e-06

        def _ln(x):
            m = jnp.mean(x, axis=-1, keepdims=True)
            v = jnp.mean((x - m) ** 2, axis=-1, keepdims=True)
            return (x - m) / jnp.sqrt(v + LN_EPS)

        def _gelu_tanh(u):
            c = np.sqrt(2.0 / np.pi).astype(np.float32)
            return 0.5 * u * (1.0 + jnp.tanh(c * (u + 0.044715 * u ** 3)))
        Bs, Lx, Cx = x.shape
        D = Cx // H
        ada = (jax.nn.silu(cond_BD) @ Wada.T + bada).reshape(Bs, 1, 6, Cx)
        gamma1, gamma2, scale1, scale2, shift1, shift2 = [ada[:, :, i, :] for i in range(6)]

        def attn(xin):
            qkv_bias = jnp.concatenate([q_bias, jnp.zeros_like(q_bias), v_bias])
            qkv = (xin @ Wqkv.T + qkv_bias).reshape(Bs, Lx, 3, H, D)
            qkv = jnp.transpose(qkv, (2, 0, 3, 1, 4))
            q, k, v = (qkv[0], qkv[1], qkv[2])
            sm = jnp.exp(jnp.minimum(scale_mul_log, jnp.log(jnp.float32(100.0))))
            qn = q / jnp.maximum(jnp.linalg.norm(q, axis=-1, keepdims=True), 1e-12) * sm
            kn = k / jnp.maximum(jnp.linalg.norm(k, axis=-1, keepdims=True), 1e-12)
            scores = jnp.einsum('bhqd,bhkd->bhqk', qn, kn) + attn_bias
            p = jax.nn.softmax(scores, axis=-1)
            o = jnp.einsum('bhqk,bhkd->bhqd', p, v)
            o = jnp.transpose(o, (0, 2, 1, 3)).reshape(Bs, Lx, Cx)
            return o @ Wproj.T + bproj
        x = x + attn(_ln(x) * (scale1 + 1.0) + shift1) * gamma1
        h = _gelu_tanh((_ln(x) * (scale2 + 1.0) + shift2) @ Wfc1.T + bfc1)
        x = x + (h @ Wfc2.T + bfc2) * gamma2
        return x

    def _L1_cond_ref(x, t_emb, W_ada, b_ada, Wq, Wkd, Wku, Wvu, Wo):
        import jax, jax.numpy as jnp
        import numpy as np
        D_MODEL = 256
        N_HEADS = 16
        N_KV_HEADS = 4
        HEAD_DIM = D_MODEL // N_HEADS
        N_GROUPS = N_HEADS // N_KV_HEADS
        BLOCK_SIZE = 128
        WINDOW = 32
        GLOBAL_EVERY = 64
        LATENT = 64
        ROPE_THETA = 10000.0
        LN_EPS = 1e-05

        def _rope_tables(T, dtype):
            freqs = 1.0 / ROPE_THETA ** (jnp.arange(0, HEAD_DIM, 2, dtype=jnp.float32) / HEAD_DIM)
            emb = jnp.arange(T, dtype=jnp.float32)[:, None] * freqs[None, :]
            cos = jnp.concatenate([jnp.cos(emb), jnp.cos(emb)], axis=-1).astype(dtype)
            sin = jnp.concatenate([jnp.sin(emb), jnp.sin(emb)], axis=-1).astype(dtype)
            return (cos, sin)

        def _rotate_half(x):
            h = x.shape[-1] // 2
            return jnp.concatenate([-x[..., h:], x[..., :h]], axis=-1)

        def _sparse_mask(T):
            idx = jnp.arange(T)
            blk = idx // BLOCK_SIZE
            future_block = blk[None, :] > blk[:, None]
            outside_window = jnp.abs(idx[None, :] - idx[:, None]) > WINDOW
            global_visible = jnp.broadcast_to((idx % GLOBAL_EVERY == 0)[None, :], (T, T))
            return outside_window & ~global_visible | future_block
        B, T, C = x.shape
        proj = t_emb @ W_ada.T + b_ada
        scale, shift = (proj[:, :C], proj[:, C:])
        mu = jnp.mean(x, axis=-1, keepdims=True)
        var = jnp.mean(jnp.square(x - mu), axis=-1, keepdims=True)
        h = (x - mu) * jax.lax.rsqrt(var + LN_EPS)
        h = h * (1.0 + scale[:, None, :]) + shift[:, None, :]
        q = (h @ Wq.T).reshape(B, T, N_HEADS, HEAD_DIM).transpose(0, 2, 1, 3)
        c_kv = h @ Wkd.T
        k = (c_kv @ Wku.T).reshape(B, T, N_KV_HEADS, HEAD_DIM).transpose(0, 2, 1, 3)
        v = (c_kv @ Wvu.T).reshape(B, T, N_KV_HEADS, HEAD_DIM).transpose(0, 2, 1, 3)
        cos, sin = _rope_tables(T, x.dtype)
        cos, sin = (cos[None, None], sin[None, None])
        q = q * cos + _rotate_half(q) * sin
        k = k * cos + _rotate_half(k) * sin
        k_exp = jnp.repeat(k, N_GROUPS, axis=1)
        v_exp = jnp.repeat(v, N_GROUPS, axis=1)
        mask = _sparse_mask(T)
        scores = jnp.einsum('bhtd,bhsd->bhts', q, k_exp) / jnp.sqrt(jnp.asarray(HEAD_DIM, x.dtype))
        scores = jnp.where(mask[None, None], jnp.asarray(-jnp.inf, x.dtype), scores)
        attn = jax.nn.softmax(scores, axis=-1)
        y = jnp.einsum('bhts,bhsd->bhtd', attn, v_exp)
        out = y.transpose(0, 2, 1, 3).reshape(B, T, C) @ Wo.T
        return x + out
    x = _L0_cond_ref(x, cond_2048, mask_1x1xSxS_ff0, L0_cond_Wqkv, L0_cond_q_bias, L0_cond_v_bias, L0_cond_scale_mul_log, L0_cond_Wproj, L0_cond_bproj, L0_cond_Wada, L0_cond_bada, L0_cond_Wfc1, L0_cond_bfc1, L0_cond_Wfc2, L0_cond_bfc2)
    x = _L1_cond_ref(x, cond_2048, L1_cond_W_ada, L1_cond_b_ada, L1_cond_Wq, L1_cond_Wkd, L1_cond_Wku, L1_cond_Wvu, L1_cond_Wo)
    return x

_drawn_inputs = setup_inputs


def setup_inputs(seed=0):
    import zlib

    import numpy as np

    out = dict(_drawn_inputs(seed))
    spreads = {'L0_cond_q_bias': (0.0, 0.8),
     'L0_cond_v_bias': (0.0, 0.8),
     'L0_cond_scale_mul_log': (1.3862943649291992, 0.6),
     'L0_cond_bproj': (0.0, 0.356),
     'L0_cond_bada': (0.0, 0.412),
     'L0_cond_bfc1': (0.0, 0.8),
     'L0_cond_bfc2': (0.0, 0.369),
     'L1_cond_b_ada': (0.0, 0.8)}
    factors = {'L0_cond_Wqkv': 8.0,
     'L0_cond_Wproj': 5.695,
     'L1_cond_W_ada': 8.0,
     'L1_cond_Wq': 8.0,
     'L1_cond_Wkd': 8.0,
     'L1_cond_Wku': 8.0,
     'L1_cond_Wvu': 8.0,
     'L1_cond_Wo': 8.0}
    for name, (base, spread) in spreads.items():
        noise = np.random.default_rng([zlib.crc32(name.encode()), seed]).standard_normal(out[name].shape)
        drawn = base * np.exp(spread * noise) if base else spread * noise
        out[name] = jnp.asarray(drawn.astype(out[name].dtype))
    for name, factor in factors.items():
        out[name] = (out[name] * factor).astype(out[name].dtype)
    return out
```

```python
from contextlib import ExitStack

import numpy as np
import concourse.bass as bass
from concourse import mybir

F32 = mybir.dt.float32
F16 = mybir.dt.float16
BF16 = mybir.dt.bfloat16
U32 = mybir.dt.uint32
I32 = mybir.dt.int32
ALU = mybir.AluOpType
ACT = mybir.ActivationFunctionType
AX = mybir.AxisListType

NB, T, C = 16, 128, 256
H, D = 16, 16
KV = 4
HID = 4 * C
LAT = 64
J = C // 128
NH = HID // 128
EPS0, EPS1 = 1e-6, 1e-5
NEG = -1e30
CSCALE = 64.0
GELU_A = 0.044715
GELU_C = float(np.sqrt(np.float32(2.0 / np.pi)))
OFF = {"A1": 0, "A2": 1, "M": 2, "C1": 4, "C2": 5}
LAST = NB + OFF["C2"]
PEEL = OFF["C2"]
LN_STEPS = 17
RSQRT = 0x5F3759DF


def block_pair(nc, x, cond_t, mask, wqkv, qbias, vbias, sml, wproj, bproj, wada, bada_row, bada_col,
               wfc1, bfc1, wfc2, bfc2, wada1, bada1, wq1, wkd, wkvu, wo1, ident, cos_t, sin_t, window, out):
    ctx = ExitStack()
    with ctx:
        def sb(name, shape, dt=F32):
            return ctx.enter_context(nc.sbuf_tensor(name, shape, dt))

        def sem(name):
            return ctx.enter_context(nc.semaphore(name))

        S = [ctx.enter_context(nc.psum_tensor(f"scores{k}", [128, 2, 512], F32)) for k in range(2)]
        G = ctx.enter_context(nc.psum_tensor("general", [128, 4, 512], F32))

        w_qkv = sb("w_qkv", [128, J, 3 * C])
        w_proj = sb("w_proj", [128, J, C])
        w_fc1 = sb("w_fc1", [128, J, HID])
        w_fc2 = sb("w_fc2", [128, NH, C])
        p_all = sb("p_all", [128, 2, 2 * 2 * 512])
        p_flat = p_all[:].rearrange("p a b -> p (a b)")
        w_ada = p_flat[:, 0:J * 6 * C].rearrange("p (j c) -> p j c", j=J)
        w_ada1 = p_flat[:, J * 6 * C:J * 8 * C].rearrange("p (j c) -> p j c", j=J)
        w_l1 = sb("w_l1", [128, J, C + 2 * KV * D])
        w_kd = sb("w_kd", [LAT, C])
        w_kvu = sb("w_kvu", [LAT, 2 * KV * D])
        w_o1 = sb("w_o1", [128, J, C])
        b_fc1 = sb("b_fc1", [128, NH])
        b_ada_row = sb("b_ada_row", [NB, 2 * C])
        b_ada_col = sb("b_ada_col", [128, 12])
        b_ada1 = sb("b_ada1", [128, 4])
        b_proj = sb("b_proj", [NB, C])
        b_fc2 = sb("b_fc2", [NB, C])
        b_v = sb("b_v", [128, J])
        q_b = sb("q_b", [1, C])
        idf = sb("idf", [128, 128])
        idh = sb("idh", [128, 128], F16)
        idb = sb("idb", [128, 128], BF16)
        win = sb("win", [128, 128])
        winb = sb("winb", [128, 128], BF16)
        cos_s = sb("cos_s", [128, C + KV * D])
        sin_s = sb("sin_s", [128, C + KV * D])
        msk = sb("msk", [128, 128])
        msk_max = sb("msk_max", [128, 1])
        msk_rel = sb("msk_rel", [128, 128])
        msk_any = sb("msk_any", [128, 128])
        msk_row = sb("msk_row", [128, 1])
        msk_flag = sb("msk_flag", [1, 1])
        cond = sb("cond", [128, J, NB])
        cexp = sb("cexp", [128, J, NB])
        cden = sb("cden", [128, J, NB])
        crec = sb("crec", [128, J, NB])
        csil = sb("csil", [128, J, NB])
        ada = sb("ada", [128, 12, NB])
        bproj_v = sb("bproj_v", [NB, C])
        bv_wide = sb("bv_wide", [128, J, NB])
        GB = sb("gb", [128, NB, 4, C])
        sm_in = sb("sm_in", [128, H])
        sm_min = sb("sm_min", [128, H])
        sm = sb("sm", [128, H])
        qb_h = sb("qb_h", [1, 3, C], BF16)
        qb_r = sb("qb_r", [1, 2, C])
        qb3 = sb("qb3", [3, C], BF16)
        one3 = sb("one3", [3, 128], BF16)
        zones = sb("zones", [128, 2, 32])

        X = sb("x_res", [128, NB, C])
        st = sb("st", [128, 3, 6])
        msum = sb("msum", [128, 3])
        mdif = sb("mdif", [128, 3])
        msq = sb("msq", [128, 3])
        mean = sb("mean", [128, 3])
        eps = sb("eps", [128, 3])
        var = sb("var", [128, 3])
        rstd = sb("rstd", [128, 3])
        rtmp = sb("rtmp", [128, 3])
        ntmp = sb("ntmp", [128, 2 * H])
        xn = {s: sb(f"xn_{s}", [128, C]) for s in "AMC"}
        xh = {s: sb(f"xh_{s}", [128, J, 128]) for s in "AMC"}
        sq = sb("sq", [128, 2 * C])
        n2 = sb("n2", [128, 2 * H])
        rinv = sb("rinv", [128, 2 * H])
        tmpA = sb("tmpA", [128, 2 * C])
        stkA = sb("stkA", [128, 2, H, 64], F16)
        rot1 = sb("rot1", [128, C + KV * D])
        rot2 = sb("rot2", [128, C + KV * D])
        tmpC = sb("tmpC", [128, C + KV * D])
        stkC = sb("stkC", [128, H + KV, 64], F16)
        qk = {"A": sb("qk_A", [128, 2, 2 * H * 64], F16),
              "C": sb("qk_C", [128, 2, (H + KV) * 64], F16)}
        V = {"A": sb("v_A", [128, 2, H, 32]), "C": sb("v_C", [128, 2, KV, 32])}
        mx = {s: sb(f"mx_{s}", [128, H]) for s in "AC"}
        cmax = {s: sb(f"cmax_{s}", [128, 2, 2, 8], F16) for s in "AC"}
        cT = {s: sb(f"cT_{s}", [32, 128], F16) for s in "AC"}
        P = {s: p_all[:, n].rearrange("p (k r q) -> p k r q", k=2, r=2) for n, s in enumerate("AC")}
        rs = {s: sb(f"rs_{s}", [128, C]) for s in "AC"}
        oT = {s: sb(f"oT_{s}", [128, J, 128]) for s in "AC"}
        xg = {s: sb(f"xg_{s}", [128, C]) for s in "AM"}
        upd = {s: sb(f"upd_{s}", [128, C]) for s in "AM"}
        U = sb("u", [128, NH, 128])
        S2 = sb("s2", [128, NH, 128])
        Z = sb("z", [128, NH, 128])
        GL = Z
        gam = U[0:NB].rearrange("p n t -> p (n t)").rearrange("p (k c) -> p k c", k=4)

        scratch = nc.dram_tensor("gamma_rows", (NB, 4 * C), F32).ap()

        x_in = [sem("x_in0"), sem("x_in1")]
        w_in = {n: sem(f"in_{n}") for n in ("cond", "ada", "qkv", "consts", "mlp", "l1", "mask", "sm")}
        p_dve = sem("setup_dve")
        p_act = sem("setup_act")
        p_pool = sem("setup_pool")
        p_pe = sem("setup_pe")
        qb_in = sem("qbias_rows_in")
        gam_out = sem("gamma_rows_out")
        gb_in = [sem("gamma_in0"), sem("gamma_in1")]
        sems = {}
        for stage, steps in (("A", "stats xn xt xh qkv sq v n2 ri rsm tmp hi dup stk tr ev s0 s1 m0 m1 ch cl ct cev"
                                   " p0 p1 e0 e1 pv rs ot o xg upd res"),
                             ("M", "stats xn xt xh fc1 u sqr z tanh gl fc2 xg upd res"),
                             ("C", "stats xn xt xh qkv v r1 r2 tmp hi stk tr ev s0 s1 m0 m1 ch cl ct cev"
                                   " p0 p1 e0 e1 pv rs ot o res")):
            for n in steps.split():
                sems[stage, n] = sem(f"{stage}_{n}")
        ln_root = sem("ln_root")
        c_in = {s: sem(f"{s}_max_rows_in") for s in "AC"}
        y_out = sem("y_out")

        def wait(eng, s, n):
            if isinstance(n, int) and n <= 0:
                return
            eng.wait_ge(s, n)

        def freed(eng, turn, users):
            for ss, back in users:
                b = turn - back
                if isinstance(b, int) and not 0 <= b < NB:
                    continue
                for s in ss:
                    eng.wait_ge(sems[s], b + 1)
                return

        def stages(turn):
            return [s for s, k in OFF.items() if not isinstance(turn, int) or 0 <= turn - k < NB]

        def turns(eng, body, before_loop=None):
            for t in range(PEEL):
                body(t, t % 2)
            if before_loop:
                before_loop()
            with eng.Fori(PEEL, NB - 2, 2) as t:
                body(t, PEEL % 2)
                body(t + 1, (PEEL + 1) % 2)
            for t in range(NB - 1, LAST):
                body(t, t % 2)

        def at(b):
            return bass.ds(b, 1) if not isinstance(b, int) else slice(b, b + 1)

        def heads16(ap):
            return ap.rearrange("p (h d) -> p h d", d=D)

        def tiles(stage, par, first, count):
            return qk[stage][:, par, first * 128:(first + count) * 128]

        KT = {"A": 8, "C": 8}

        block = ctx.enter_context(nc.Block())

        @block.sync
        def _(sp):
            sp.dma_start(cond[:], cond_t).then_inc(w_in["cond"], 16)
            sp.dma_start(w_ada, wada).then_inc(w_in["ada"], 16)
            sp.dma_start(b_ada_row[:], bada_row.broadcast_to([NB, 2 * C])).then_inc(w_in["ada"], 16)
            sp.dma_start(b_ada_col[:], bada_col).then_inc(w_in["ada"], 16)
            sp.dma_start(w_ada1, wada1).then_inc(w_in["ada"], 16)
            sp.dma_start(b_ada1[:], bada1).then_inc(w_in["ada"], 16)
            sp.dma_start(X[:, 0:4, :], x[0:4].rearrange("b t c -> t b c")).then_inc(x_in[0], 16)
            sp.dma_start(w_qkv[:], wqkv).then_inc(w_in["qkv"], 16)
            sp.dma_start(w_fc1[:], wfc1).then_inc(w_in["mlp"], 16)
            sp.dma_start(w_fc2[:], wfc2).then_inc(w_in["mlp"], 16)
            sp.dma_start(b_fc1[:], bfc1).then_inc(w_in["mlp"], 16)
            sp.wait_ge(p_dve, QB_PARTS)
            sp.dma_start(qb3[:], qb_h[0:1, :, :]).then_inc(qb_in, 16)
            sp.wait_ge(p_dve, GAM_ROWS)
            sp.dma_start(scratch, gam.rearrange("b k c -> b (k c)")).then_inc(gam_out, 16)
            sp.dma_start(X[:, 4:NB, :], x[4:NB].rearrange("b t c -> t b c")).then_inc(x_in[1], 16)
            sp.wait_ge(gam_out, 16)
            for n, (a, z) in enumerate(((0, 4), (4, NB))):
                sp.dma_start(GB[:, a:z, :, :],
                             scratch[a:z].rearrange("b (k c) -> b k c", k=4).partition_broadcast(128)
                             ).then_inc(gb_in[n], 16)

            def max_rows(stage, b, par):
                sp.wait_ge(sems[stage, "cev"], b + 1)
                for r in range(2):
                    dst = tiles(stage, par, 0, 8).rearrange("p (t q) -> p t q", q=128)
                    sp.dma_start(dst[64 * r + 48:64 * r + 50], cT[stage][16 * r:16 * r + 16, :]
                                 ).then_inc(c_in[stage], 16)

            def turn_sp(turn, par):
                on = stages(turn)
                if "C2" in on:
                    b = turn - OFF["C2"]
                    sp.wait_ge(sems["C", "res"], b + 1)
                    sp.dma_start(out[at(b)].rearrange("o t c -> t (o c)"), X[:, at(b), :]
                                 ).then_inc(y_out, 16)
                if "A1" in on:
                    max_rows("A", turn, par)
                if "C1" in on:
                    max_rows("C", turn - OFF["C1"], par)

            turns(sp, turn_sp)
            sp.wait_ge(y_out, 16 * NB)

        @block.gpsimd
        def _(pool):
            pool.memset(stkA[:, :, :, 48:64], 0.0).then_inc(p_pool, 1)
            pool.memset(stkC[:, :, 48:64], 0.0).then_inc(p_pool, 1)
            pool.memset(V["A"][:], 0.0).then_inc(p_pool, 1)
            pool.memset(V["C"][:], 0.0).then_inc(p_pool, 1)
            pool.memset(zones[:], 0.0).then_inc(p_pool, 1)
            pool.memset(one3[:], 1.0).then_inc(p_pool, 1)
            pool.wait_ge(p_pool, 6)
            pool.memset(stkA[:, 1, :, 48:50], CSCALE).then_inc(p_pool, 1)
            pool.memset(stkC[:, H:H + KV, 48:50], CSCALE).then_inc(p_pool, 1)
            pool.memset(zones[:, 0, 0:16], 1.0).then_inc(p_pool, 1)
            pool.memset(zones[:, 1, 16:32], 1.0).then_inc(p_pool, 1)

            def turn_pool(turn, par):
                on = stages(turn)
                if "A2" in on:
                    b = turn - 1
                    if isinstance(turn, int):
                        pool.wait_ge(gb_in[0], 16)
                    wait(pool, sems["A", "upd"], b)
                    wait(pool, sems["A", "res"], b)
                    pool.tensor_tensor(xg["A"][:], X[:, at(b), :], GB[:, at(b), 2, :], ALU.add
                                       ).then_inc(sems["A", "xg"], 1)
                if "M" in on:
                    b = turn - 2
                    pool.wait_ge(sems["A", "res"], b + 1)
                    wait(pool, sems["M", "res"], b)
                    pool.tensor_tensor(xg["M"][:], X[:, at(b), :], GB[:, at(b), 3, :], ALU.add
                                       ).then_inc(sems["M", "xg"], 1)

            turns(pool, turn_pool, lambda: pool.wait_ge(gb_in[1], 16))

        @block.scalar
        def _(act):
            act.dma_start(idf[:], ident).then_inc(w_in["consts"], 16)
            act.dma_start(q_b[:], qbias).then_inc(w_in["consts"], 16)
            act.dma_start(b_v[:], vbias).then_inc(w_in["consts"], 16)
            act.dma_start(b_proj[:], bproj.broadcast_to([NB, C])).then_inc(w_in["consts"], 16)
            act.dma_start(b_fc2[:], bfc2.broadcast_to([NB, C])).then_inc(w_in["consts"], 16)
            act.dma_start(w_proj[:], wproj).then_inc(w_in["consts"], 16)
            act.dma_start(sm_in[:], sml.broadcast_to([128, H])).then_inc(w_in["sm"], 16)
            act.dma_start(msk[:], mask).then_inc(w_in["mask"], 16)
            act.dma_start(w_kd[:], wkd).then_inc(w_in["l1"], 16)
            act.dma_start(w_kvu[:], wkvu).then_inc(w_in["l1"], 16)
            act.dma_start(w_l1[:, :, 0:C], wq1).then_inc(w_in["l1"], 16)
            act.dma_start(w_o1[:], wo1).then_inc(w_in["l1"], 16)
            act.dma_start(cos_s[:], cos_t).then_inc(w_in["l1"], 16)
            act.dma_start(sin_s[:], sin_t).then_inc(w_in["l1"], 16)
            act.dma_start(win[:], window).then_inc(w_in["l1"], 16)
            act.wait_ge(w_in["cond"], 16)
            act.activation(cexp[:], cond[:], ACT.Exp, scale=-1.0).then_inc(p_act, 1)
            act.wait_ge(p_dve, SM_MIN)
            act.activation(sm[:], sm_min[:], ACT.Exp).then_inc(p_act, 1)

            def modulate(stage, b, bank, scale0, shift0):
                act.wait_ge(sems[stage, "xt"], b + 1)
                wait(act, sems[stage, "fc1" if stage == "M" else "qkv"], b)
                for j in range(J):
                    ins = act.activation(xh[stage][:, j, :], G[:, bank, j * 128:(j + 1) * 128], ACT.Identity,
                                         bias=ada[:, shift0 + j, at(b)], scale=ada[:, scale0 + j, at(b)])
                ins.then_inc(sems[stage, "xh"], 1)

            def exps(stage, b, k):
                act.wait_ge(sems[stage, f"p{k}"], b + 1)
                wait(act, sems[stage, "pv"], b)
                act.activation(P[stage][:, k], S[k][:], ACT.Exp).then_inc(sems[stage, f"e{k}"], 1)

            def max_out(stage, b, par):
                act.wait_ge(sems[stage, "ct"], b + 1)
                wait(act, c_in[stage], 32 * b)
                act.copy(cT[stage][:], G[0:32, 1, 0:64].bitcast(F16)).then_inc(sems[stage, "cev"], 1)

            def turn_act(turn, par):
                on = stages(turn)
                if "A1" in on:
                    b = turn
                    if isinstance(turn, int) and turn == 0:
                        act.wait_ge(p_dve, ADA)
                    modulate("A", b, 0, 0, 4)
                if "A2" in on:
                    exps("A", turn - 1, 0)
                    exps("A", turn - 1, 1)
                if "M" in on:
                    modulate("M", turn - 2, 3, 2, 6)
                if "A1" in on:
                    b = turn
                    act.wait_ge(sems["A", "qkv"], b + 1)
                    wait(act, sems["A", "n2"], b)
                    act.activation(sq[:], G[:, 0, :], ACT.Square).then_inc(sems["A", "sq"], 1)
                    if isinstance(turn, int) and turn == 0:
                        act.wait_ge(p_pool, 10)
                    wait(act, sems["A", "pv"], b - 1)
                    act.copy(V["A"][:, par].rearrange("p (t r) w -> p t (r w)", r=2)
                             .rearrange("p t (a w) -> p t a w", a=4)[:, :, 0::3, :],
                             G[:, 1, 0:C].rearrange("p (t r d) -> p t r d", r=2, d=D)
                             ).then_inc(sems["A", "v"], 1)
                if "C1" in on:
                    modulate("C", turn - OFF["C1"], 2, 8, 10)
                if "C2" in on:
                    exps("C", turn - OFF["C2"], 0)
                    exps("C", turn - OFF["C2"], 1)
                if "A1" in on:
                    b = turn
                    act.wait_ge(sems["A", "tr"], b + 1)
                    wait(act, sems["A", "p1"], b - 1)
                    act.copy(qk["A"][:, par, :].bitcast(U32),
                             G[:, 0:2, :].rearrange("p a b -> p (a b)").bitcast(U32)
                             ).then_inc(sems["A", "ev"], 1)
                if "M" in on:
                    b = turn - 2
                    act.wait_ge(sems["M", "u"], b + 1)
                    wait(act, sems["M", "gl"], b)
                    act.activation(S2[:], U[:], ACT.Square, scale=float(np.sqrt(GELU_A))
                                   ).then_inc(sems["M", "sqr"], 1)
                if "C1" in on:
                    b = turn - OFF["C1"]
                    act.wait_ge(sems["C", "tr"], b + 1)
                    wait(act, sems["C", "p1"], b - 1)
                    act.copy(qk["C"][:, par, :].bitcast(U32),
                             G[:, 2:4, :].rearrange("p a b -> p (a b)")[:, 0:(H + KV) * 32].bitcast(U32)
                             ).then_inc(sems["C", "ev"], 1)
                if "M" in on:
                    b = turn - 2
                    act.wait_ge(sems["M", "z"], b + 1)
                    act.activation(S2[:], Z[:], ACT.Tanh, scale=GELU_C).then_inc(sems["M", "tanh"], 1)
                if "A1" in on:
                    max_out("A", turn, par)
                if "C1" in on:
                    max_out("C", turn - OFF["C1"], par)

            turns(act, turn_act)

        @block.vector
        def _(dve):
            done = [0]

            def setup(ins, now=True):
                done[0] += 1
                ins.then_inc(p_dve, 1)
                if now:
                    dve.wait_ge(p_dve, done[0])

            setup(dve.memset(eps[:, 0:2], EPS0), now=False)
            setup(dve.memset(eps[:, 2:3], EPS1), now=False)
            setup(dve.memset(st[:], 1.0))
            dve.wait_ge(p_act, 1)
            setup(dve.tensor_scalar(cden[:], cexp[:], 1.0, None, ALU.add))
            setup(dve.reciprocal(crec[:], cden[:]))
            setup(dve.tensor_tensor(csil[:], cond[:], crec[:], ALU.mult))
            assert done[0] == SILU
            dve.wait_ge(w_in["sm"], 16)
            setup(dve.tensor_scalar(sm_min[:], sm_in[:], float(np.log(np.float32(100.0))), None, ALU.min))
            assert done[0] == SM_MIN
            dve.wait_ge(w_in["consts"], 96)
            setup(dve.tensor_copy(idh[:], idf[:]), now=False)
            setup(dve.tensor_copy(idb[:], idf[:]), now=False)
            setup(dve.tensor_copy(bv_wide[:], b_v[:].unsqueeze(2).broadcast_to([128, J, NB])))
            assert done[0] == CONSTS
            setup(dve.tensor_copy(qb_h[:, 0, :], q_b[:]))
            setup(dve.tensor_tensor(qb_r[:, 0, :], q_b[:], qb_h[:, 0, :], ALU.subtract))
            setup(dve.tensor_copy(qb_h[:, 1, :], qb_r[:, 0, :]))
            setup(dve.tensor_tensor(qb_r[:, 1, :], qb_r[:, 0, :], qb_h[:, 1, :], ALU.subtract))
            setup(dve.tensor_copy(qb_h[:, 2, :], qb_r[:, 1, :]))
            assert done[0] == QB_PARTS
            dve.wait_ge(p_pe, 1)
            setup(dve.tensor_tensor(ada[:, 0:8, :], G[:, 0, 0:8 * NB].rearrange("p (k b) -> p k b", b=NB),
                                    b_ada_col[:, 4:12].unsqueeze(2).broadcast_to([128, 8, NB]), ALU.add), now=False)
            setup(dve.tensor_tensor(ada[:, 8:12, :], G[:, 0, 8 * NB:12 * NB].rearrange("p (k b) -> p k b", b=NB),
                                    b_ada1[:].unsqueeze(2).broadcast_to([128, 4, NB]), ALU.add))
            setup(dve.tensor_scalar(ada[:, 0:4, :], ada[:, 0:4, :], 1.0, None, ALU.add), now=False)
            setup(dve.tensor_scalar(ada[:, 8:10, :], ada[:, 8:10, :], 1.0, None, ALU.add))
            assert done[0] == ADA
            dve.wait_ge(p_pe, 2)
            setup(dve.tensor_tensor(gam[:, 0:2, :].rearrange("b k c -> b (k c)"), G[0:NB, 1, :], b_ada_row[:],
                                    ALU.add), now=False)
            dve.wait_ge(p_pe, 3)
            setup(dve.tensor_tensor(bproj_v[:], G[0:NB, 2, 0:C], b_proj[:], ALU.add))
            setup(dve.tensor_tensor(gam[:, 2, :], gam[:, 0, :], bproj_v[:], ALU.mult), now=False)
            setup(dve.tensor_tensor(gam[:, 3, :], gam[:, 1, :], b_fc2[:], ALU.mult))
            assert done[0] == GAM_ROWS
            dve.wait_ge(w_in["mask"], 16)
            setup(dve.tensor_scalar(msk[:], msk[:], NEG, None, ALU.max))
            setup(dve.tensor_reduce(msk_max[:], msk[:], AX.X, ALU.max))
            setup(dve.tensor_scalar(msk_rel[:], msk[:], msk_max[:], None, ALU.subtract))
            setup(dve.tensor_scalar(msk_any[:], msk_rel[:], 0.0, None, ALU.is_lt))
            setup(dve.tensor_reduce(msk_row[:], msk_any[:], AX.X, ALU.max))
            assert done[0] == MASK_ROW
            dve.wait_ge(p_pe, 4)
            setup(dve.tensor_reduce(msk_flag[:], G[0:1, 3, 0:128], AX.X, ALU.max))
            assert done[0] == MASK_FLAG
            dve.wait_ge(w_in["l1"], 112)
            setup(dve.tensor_copy(winb[:], win[:]), now=False)
            dve.wait_ge(p_pe, 5)
            setup(dve.tensor_copy(w_l1[:, :, C:], G[:, 0, 0:J * 128].rearrange("p (j k) -> p j k", j=J)), now=False)
            dve.wait_ge(w_in["mlp"], 48)
            setup(dve.tensor_scalar(w_fc2[:], w_fc2[:], 0.5, None, ALU.mult))
            assert done[0] == SETUP_END

            dve.wait_ge(x_in[0], 16)
            dve.wait_ge(p_pool, 10)

            def roots(y, v, t, count, first, base):
                n = [first]

                def step(ins):
                    ins.then_inc(count, 1)
                    dve.wait_ge(count, base + n[0])
                    n[0] += 1

                step(dve.tensor_scalar(y.bitcast(I32), v.bitcast(I32), -0.5, float(RSQRT), ALU.mult, ALU.add))
                for _ in range(3):
                    step(dve.tensor_tensor(t, y, y, ALU.mult))
                    step(dve.scalar_tensor_tensor(t, v, -0.5, t, ALU.mult, ALU.mult))
                    step(dve.scalar_tensor_tensor(y, t, 1.5, y, ALU.add, ALU.mult))

            def norms(turn):
                todo = [(k, s[0], turn - OFF[s]) for k, s in enumerate(("A1", "M", "C1")) if s in stages(turn)]
                if not todo:
                    return
                for k, s, b in todo:
                    dve.wait_ge(x_in[0], 16)
                    if s != "A":
                        dve.wait_ge(sems["A" if s == "M" else "M", "res"], b + 1)
                    dve.bn_stats(st[:, k, :], X[:, at(b), :].rearrange("p o c -> p (o c)")).then_inc(sems[s, "stats"], 1)
                for k, s, b in todo:
                    dve.wait_ge(sems[s, "stats"], b + 1)
                even, odd, even2, odd2 = (st[:, :, n] for n in (1, 4, 2, 5))
                base = LN_STEPS * turn
                dve.tensor_tensor(msum[:], even, odd, ALU.add).then_inc(ln_root, 1)
                dve.tensor_tensor(mdif[:], even, odd, ALU.subtract).then_inc(ln_root, 1)
                dve.tensor_tensor(msq[:], even2, odd2, ALU.add).then_inc(ln_root, 1)
                dve.wait_ge(ln_root, base + 1)
                dve.tensor_scalar(mean[:], msum[:], 0.5, None, ALU.mult).then_inc(ln_root, 1)
                dve.wait_ge(ln_root, base + 3)
                dve.scalar_tensor_tensor(msq[:], msq[:], 1.0 / C, eps[:], ALU.mult, ALU.add).then_inc(ln_root, 1)
                dve.tensor_tensor(mdif[:], mdif[:], mdif[:], ALU.mult).then_inc(ln_root, 1)
                dve.wait_ge(ln_root, base + 6)
                dve.scalar_tensor_tensor(var[:], mdif[:], 0.25, msq[:], ALU.mult, ALU.add).then_inc(ln_root, 1)
                dve.wait_ge(ln_root, base + 7)
                roots(rstd[:], var[:], rtmp[:], ln_root, 8, base)
                for k, s, b in todo:
                    wait(dve, sems[s, "xt"], b)
                    dve.tensor_scalar(xn[s][:], X[:, at(b), :].rearrange("p o c -> p (o c)"), mean[:, k:k + 1],
                                      rstd[:, k:k + 1], ALU.subtract, ALU.mult).then_inc(sems[s, "xn"], 1)

            def qk_parts_A(b):
                dve.wait_ge(sems["A", "sq"], b + 1)
                dve.tensor_reduce(n2[:], heads16(sq[:]), AX.X, ALU.add).then_inc(sems["A", "n2"], 1)
                dve.wait_ge(sems["A", "n2"], b + 1)
                dve.tensor_scalar(n2[:], n2[:], 1e-24, None, ALU.max).then_inc(sems["A", "ri"], 1)
                dve.wait_ge(sems["A", "ri"], 11 * b + 1)
                roots(rinv[:], n2[:], ntmp[:], sems["A", "ri"], 2, 11 * b)
                dve.tensor_tensor(rinv[:, 0:H], rinv[:, 0:H], sm[:], ALU.mult).then_inc(sems["A", "rsm"], 1)
                dve.wait_ge(sems["A", "rsm"], b + 1)
                dve.tensor_tensor(heads16(tmpA[:]), heads16(G[:, 0, :]),
                                  rinv[:].unsqueeze(2).broadcast_to([128, 2 * H, D]), ALU.mult
                                  ).then_inc(sems["A", "tmp"], 1)
                dve.wait_ge(sems["A", "tmp"], b + 1)
                wait(dve, sems["A", "tr"], b)
                t4 = tmpA[:].rearrange("p (k h d) -> p k h d", k=2, d=D)
                flat = stkA[:].rearrange("p k h w -> p k (h w)")
                dve.tensor_copy(stkA[:, :, :, 0:16], t4).then_inc(sems["A", "hi"], 1)
                dve.wait_ge(sems["A", "hi"], b + 1)
                dve.tensor_copy(stkA[:, 0, :, 32:48], stkA[:, 0, :, 0:16]).then_inc(sems["A", "dup"], 1)
                dve.tensor_copy(stkA[:, 1, :, 16:32], stkA[:, 1, :, 0:16]).then_inc(sems["A", "dup"], 1)
                dve.tensor_tensor(stkA[:, 0, :, 16:32], t4[:, 0], stkA[:, 0, :, 0:16], ALU.subtract
                                  ).then_inc(sems["A", "stk"], 1)
                dve.tensor_tensor(stkA[:, 1, :, 32:48], t4[:, 1], stkA[:, 1, :, 0:16], ALU.subtract
                                  ).then_inc(sems["A", "stk"], 1)

            def qk_parts_C(b, par):
                dve.wait_ge(sems["C", "qkv"], b + 1)
                n = C + KV * D
                ps = G[:, 2, 0:n].rearrange("p (h two e) -> p h two e", two=2, e=D // 2)
                sn = sin_s[:].rearrange("p (h two e) -> p h two e", two=2, e=D // 2)
                r2 = rot2[:].rearrange("p (h two e) -> p h two e", two=2, e=D // 2)
                wait(dve, sems["C", "pv"], b - 1)
                dve.tensor_copy(V["C"][:, par].rearrange("p (t r) w -> p t (r w)", r=2)
                                .rearrange("p t (a w) -> p t a w", a=4)[:, :, 0::3, :],
                                G[:, 2, n:n + KV * D].rearrange("p (t r d) -> p t r d", r=2, d=D)
                                ).then_inc(sems["C", "v"], 1)
                dve.tensor_tensor(rot1[:], G[:, 2, 0:n], cos_s[:], ALU.mult).then_inc(sems["C", "r1"], 1)
                for half in range(2):
                    dve.tensor_tensor(r2[:, :, half, :], ps[:, :, 1 - half, :], sn[:, :, half, :], ALU.mult
                                      ).then_inc(sems["C", "r2"], 1)
                dve.wait_ge(sems["C", "r1"], b + 1)
                dve.wait_ge(sems["C", "r2"], 2 * (b + 1))
                dve.tensor_tensor(tmpC[:], rot1[:], rot2[:], ALU.add).then_inc(sems["C", "tmp"], 1)
                dve.wait_ge(sems["C", "tmp"], b + 1)
                wait(dve, sems["C", "tr"], b)
                t3 = heads16(tmpC[:])
                dve.tensor_copy(stkC[:, :, 0:16], t3).then_inc(sems["C", "hi"], 1)
                dve.wait_ge(sems["C", "hi"], b + 1)
                dve.tensor_copy(stkC[:, 0:H, 32:48], stkC[:, 0:H, 0:16]).then_inc(sems["C", "stk"], 1)
                dve.tensor_copy(stkC[:, H:, 16:32], stkC[:, H:, 0:16]).then_inc(sems["C", "stk"], 1)
                dve.tensor_tensor(stkC[:, 0:H, 16:32], t3[:, 0:H], stkC[:, 0:H, 0:16], ALU.subtract
                                  ).then_inc(sems["C", "stk"], 1)
                dve.tensor_tensor(stkC[:, H:, 32:48], t3[:, H:], stkC[:, H:, 0:16], ALU.subtract
                                  ).then_inc(sems["C", "stk"], 1)

            def maxima(stage, b):
                m3 = mx[stage][:].rearrange("p (r t) -> p r t", r=2)
                for k in range(2):
                    dve.wait_ge(sems[stage, f"s{k}"], b + 1)
                    dve.tensor_reduce(m3[:, :, 4 * k:4 * k + 4],
                                      S[k][:].rearrange("p r (t q) -> p r t q", q=128), AX.X, ALU.max
                                      ).then_inc(sems[stage, f"m{k}"], 1)
                for k in range(2):
                    dve.wait_ge(sems[stage, f"m{k}"], b + 1)
                wait(dve, sems[stage, "ct"], b)
                high, low = cmax[stage][:, :, 0, :], cmax[stage][:, :, 1, :]
                dve.tensor_scalar(high, m3, -1.0 / CSCALE, None, ALU.mult).then_inc(sems[stage, "ch"], 1)
                dve.wait_ge(sems[stage, "ch"], b + 1)
                dve.scalar_tensor_tensor(low, m3, -1.0 / CSCALE, high, ALU.mult, ALU.subtract
                                         ).then_inc(sems[stage, "cl"], 1)

            def normalize(stage, b, bank):
                dve.wait_ge(sems[stage, "pv"], b + 1)
                dve.reciprocal(rs[stage][:], G[:, bank, C:2 * C]).then_inc(sems[stage, "rs"], 1)
                dve.wait_ge(sems[stage, "rs"], b + 1)
                wait(dve, sems[stage, "o"], b)
                dve.tensor_tensor(oT[stage][:].rearrange("p j q -> p (j q)"), G[:, bank, 0:C], rs[stage][:], ALU.mult
                                  ).then_inc(sems[stage, "ot"], 1)

            def gated_residual(stage, b, bank, done_step, gamma):
                dve.wait_ge(sems[stage, done_step], b + 1)
                dve.tensor_tensor(upd[stage][:], G[:, bank, 0:C], GB[:, at(b), gamma, :].rearrange("p o c -> p (o c)"),
                                  ALU.mult).then_inc(sems[stage, "upd"], 1)
                dve.wait_ge(sems[stage, "upd"], b + 1)
                dve.wait_ge(sems[stage, "xg"], b + 1)
                dve.tensor_tensor(X[:, at(b), :].rearrange("p o c -> p (o c)"), upd[stage][:], xg[stage][:], ALU.add
                                  ).then_inc(sems[stage, "res"], 1)

            def turn_dve(turn, par):
                on = stages(turn)
                a, a2, m, c, c2 = (turn - OFF[s] for s in ("A1", "A2", "M", "C1", "C2"))
                if isinstance(turn, int) and turn == 1:
                    dve.wait_ge(gb_in[0], 16)
                if isinstance(turn, int) and turn == 3:
                    dve.wait_ge(x_in[1], 16)
                if "A1" in on:
                    qk_parts_A(a)
                if "C1" in on:
                    qk_parts_C(c, par)
                if "A2" in on:
                    normalize("A", a2, 3)
                if "M" in on:
                    dve.wait_ge(sems["M", "fc1"], m + 1)
                    wait(dve, sems["M", "sqr"], m)
                    dve.tensor_tensor(U[:], G[:, 2:4, :].rearrange("p a (n t) -> p (a n) t", t=128),
                                      b_fc1[:].unsqueeze(2).broadcast_to([128, NH, 128]), ALU.add
                                      ).then_inc(sems["M", "u"], 1)
                if "A2" in on:
                    gated_residual("A", a2, 0, "o", 0)
                if "M" in on:
                    dve.wait_ge(sems["M", "sqr"], m + 1)
                    wait(dve, sems["M", "fc2"], m)
                    dve.scalar_tensor_tensor(Z[:], S2[:], 1.0, U[:], ALU.add, ALU.mult
                                             ).then_inc(sems["M", "z"], 1)
                if "A1" in on:
                    maxima("A", a)
                if "C2" in on:
                    normalize("C", c2, 1)
                if "M" in on:
                    dve.wait_ge(sems["M", "tanh"], m + 1)
                    dve.scalar_tensor_tensor(GL[:], S2[:], 1.0, U[:], ALU.add, ALU.mult
                                             ).then_inc(sems["M", "gl"], 1)
                if "C2" in on:
                    dve.wait_ge(sems["C", "o"], c2 + 1)
                    row = X[:, at(c2), :].rearrange("p o c -> p (o c)")
                    dve.tensor_tensor(row, G[:, 0, 0:C], row, ALU.add).then_inc(sems["C", "res"], 1)
                norms(turn + 1)
                if "C1" in on:
                    maxima("C", c)
                if "M" in on:
                    gated_residual("M", m, 2, "fc2", 1)

            norms(0)
            turns(dve, turn_dve, lambda: dve.wait_ge(gb_in[1], 16))

        @block.tensor
        def _(pe):
            pe.wait_ge(p_dve, SILU)
            pe.wait_ge(w_in["ada"], 80)
            for k in range(12):
                src, w, col = (csil, w_ada, 2 * C + k * 128) if k < 8 else (cond, w_ada1, (k - 8) * 128)
                for j in range(J):
                    ins = pe.matmul(G[:, 0, k * NB:(k + 1) * NB], w[:, j, col:col + 128], src[:, j, :],
                                    start=(j == 0), stop=(j == J - 1))
            ins.then_inc(p_pe, 1)
            for j in range(J):
                ins = pe.matmul(G[0:NB, 1, :], csil[:, j, :], w_ada[:, j, 0:2 * C], start=(j == 0), stop=(j == J - 1))
            ins.then_inc(p_pe, 1)
            pe.wait_ge(p_dve, CONSTS)
            for j in range(J):
                ins = pe.matmul(G[0:NB, 2, 0:C], bv_wide[:, j, :], w_proj[:, j, :], start=(j == 0), stop=(j == J - 1))
            ins.then_inc(p_pe, 1)
            pe.wait_ge(p_dve, MASK_ROW)
            pe.transpose(G[0:1, 3, 0:128], msk_row[:], idf[:]).then_inc(p_pe, 1)
            pe.wait_ge(w_in["l1"], 112)
            pe.wait_ge(p_dve, ADA)
            for j in range(J):
                ins = pe.matmul(G[:, 0, j * 128:(j + 1) * 128], w_kd[:, j * 128:(j + 1) * 128], w_kvu[:],
                                start=True, stop=True)
            ins.then_inc(p_pe, 1)
            pe.wait_ge(w_in["qkv"], 16)
            pe.wait_ge(qb_in, 16)
            pe.wait_ge(p_pool, 10)
            pe.wait_ge(p_dve, SETUP_END)

            def tokens_to_channels(stage, b, bank):
                pe.wait_ge(sems[stage, "xn"], b + 1)
                for j in range(J):
                    ins = pe.transpose(G[:, bank, j * 128:(j + 1) * 128], xn[stage][:, j * 128:(j + 1) * 128], idf[:])
                ins.then_inc(sems[stage, "xt"], 1)

            def bank(stage_step, b, turn, users):
                freed(pe, turn, users)

            def scores(stage, b, par, k, masked, turn, users):
                if k == 0:
                    pe.wait_ge(sems[stage, "ev"], b + 1)
                freed(pe, turn, users)
                if stage == "C":
                    for r in range(2):
                        pe.matmul(S[k][:, r, :], idb[:], winb[:].unsqueeze(1).broadcast_to([128, 4, 128]),
                                  start=True, stop=False, skip_group_check=True)
                elif masked:
                    for r in range(2):
                        pe.matmul(S[k][:, r, :], idf[:], msk_rel[:].unsqueeze(1).broadcast_to([128, 4, 128]),
                                  start=True, stop=False, skip_group_check=True)
                added = masked or stage == "C"
                for t in range(4):
                    for r in range(2):
                        rows = slice(64 * r, 64 * r + 48)
                        tk = KT[stage] + (4 * k + t if stage == "A" else k)
                        ins = pe.matmul(S[k][:, r, t * 128:(t + 1) * 128], tiles(stage, par, 4 * k + t, 1)[rows],
                                        tiles(stage, par, tk, 1)[rows], start=not added, stop=True,
                                        skip_group_check=True)
                ins.then_inc(sems[stage, f"s{k}"], 1)

            def shifted(stage, b, par, k, masked, turn, users):
                if k == 0:
                    pe.wait_ge(c_in[stage], 32 * (b + 1))
                freed(pe, turn, users)
                if stage == "C":
                    for r in range(2):
                        pe.matmul(S[k][:, r, :], winb[:], idb[:].unsqueeze(1).broadcast_to([128, 4, 128]),
                                  start=True, stop=False, skip_group_check=True)
                    for r in range(2):
                        rows = slice(64 * r, 64 * r + 64)
                        ins = pe.matmul(S[k][:, r, :], tiles(stage, par, KT[stage] + k, 1)[rows],
                                        tiles(stage, par, 4 * k, 4)[rows], start=False, stop=True,
                                        skip_group_check=True)
                else:
                    if masked:
                        for r in range(2):
                            pe.matmul(S[k][:, r, :], msk_rel[:], idf[:].unsqueeze(1).broadcast_to([128, 4, 128]),
                                      start=True, stop=False, skip_group_check=True)
                    for t in range(4):
                        for r in range(2):
                            rows = slice(64 * r, 64 * r + 64)
                            ins = pe.matmul(S[k][:, r, t * 128:(t + 1) * 128],
                                            tiles(stage, par, KT[stage] + 4 * k + t, 1)[rows],
                                            tiles(stage, par, 4 * k + t, 1)[rows], start=not masked, stop=True,
                                            skip_group_check=True)
                ins.then_inc(sems[stage, f"p{k}"], 1)

            def max_transposed(stage, b, turn, users):
                pe.wait_ge(sems[stage, "cl"], b + 1)
                freed(pe, turn, users)
                pe.transpose(G[0:32, 1, 0:64].bitcast(F16), cmax[stage][:].rearrange("p r s t -> p (r s t)"), idh[:]
                             ).then_inc(sems[stage, "ct"], 1)

            def values_A(b, par, g_bank, turn, users):
                for k in range(2):
                    pe.wait_ge(sems["A", f"e{k}"], b + 1)
                pe.wait_ge(sems["A", "v"], b + 1)
                freed(pe, turn, users)
                for g in range(J):
                    for what in range(2):
                        for r in range(2):
                            for j in range(4):
                                h = 8 * g + 2 * j + r
                                t = h // 2
                                ins = pe.matmul(G[32 * j:32 * j + 32, g_bank, what * C + g * 128:what * C + (g + 1) * 128],
                                                zones[:, r, :] if what else V["A"][:, par, h, :],
                                                P["A"][:, t // 4, r, (t % 4) * 128:(t % 4 + 1) * 128],
                                                start=(r == 0), stop=(r == 1), skip_group_check=True)
                ins.then_inc(sems["A", "pv"], 1)

            def values_C(b, par, g_bank, turn, users):
                for k in range(2):
                    pe.wait_ge(sems["C", f"e{k}"], b + 1)
                pe.wait_ge(sems["C", "v"], b + 1)
                freed(pe, turn, users)
                for what in range(2):
                    for r in range(2):
                        for s in range(2):
                            for ih in range(2):
                                j = 2 * s + ih
                                ins = pe.matmul(G[32 * j:32 * j + 32, g_bank, what * C:(what + 1) * C],
                                                zones[:, r, :] if what else V["C"][:, par, 2 * s + r, :],
                                                P["C"][:, s, r, ih * 256:(ih + 1) * 256],
                                                start=(r == 0), stop=(r == 1), skip_group_check=True)
                ins.then_inc(sems["C", "pv"], 1)

            def project(stage, b, w, turn, users):
                pe.wait_ge(sems[stage, "ot"], b + 1)
                freed(pe, turn, users)
                for j in range(J):
                    ins = pe.matmul(G[:, 0, 0:C], oT[stage][:, j, :], w[:, j, :], start=(j == 0), stop=(j == J - 1))
                ins.then_inc(sems[stage, "o"], 1)

            def turn_pe(turn, par, masked):
                on = stages(turn)
                odd = (par + 1) % 2
                a, a2, m, c, c2 = (turn - OFF[s] for s in ("A1", "A2", "M", "C1", "C2"))
                A1, A2, M_, C1, C2 = OFF.values()

                def rd(stage, *steps):
                    return tuple((stage, s) for s in steps)

                ev_a, ev_c = rd("A", "ev"), rd("C", "ev")
                if "A1" in on:
                    freed(pe, turn, [(rd("C", "res"), C2 + 1), (rd("A", "res"), A2 + 1), (ev_a, A1 + 1)])
                    tokens_to_channels("A", a, 0)
                if "A2" in on:
                    for k in range(2):
                        shifted("A", a2, odd, k, masked, turn, [(rd("C", f"m{k}"), C1 + 1), (rd("A", f"m{k}"), A1 + 1)])
                if "M" in on:
                    freed(pe, turn, [(ev_c, C1 + 1), (rd("M", "u"), M_ + 1), (rd("A", "ot"), A2 + 1)])
                    tokens_to_channels("M", m, 3)
                if "A1" in on:
                    pe.wait_ge(sems["A", "xh"], a + 1)
                    freed(pe, turn, [(rd("C", "cev"), C1 + 1), (rd("A", "cev"), A1 + 1)])
                    for j in range(J):
                        pe.matmul(G[:, 1, 0:C], xh["A"][:, j, :], w_qkv[:, j, 2 * C:3 * C], start=(j == 0),
                                  stop=(j == J - 1))
                        ins = pe.matmul(G[:, 0, :], xh["A"][:, j, :], w_qkv[:, j, 0:2 * C], start=(j == 0),
                                        stop=(j == J - 1), skip_group_check=True)
                        if j == 0:
                            pe.matmul(G[:, 0, 0:C], one3[:], qb3[:], start=False, stop=False, skip_group_check=True)
                    ins.then_inc(sems["A", "qkv"], 1)
                if "C1" in on:
                    freed(pe, turn, [(rd("M", "upd"), M_ + 1)])
                    tokens_to_channels("C", c, 2)
                if "A2" in on:
                    values_A(a2, odd, 3, turn, [(rd("M", "xh"), M_), (ev_c, C1 + 1), (rd("M", "u"), M_ + 1),
                                                (rd("A", "ot"), A2 + 1)])
                if "C1" in on:
                    pe.wait_ge(sems["C", "xh"], c + 1)
                    n = C + 2 * KV * D
                    for j in range(J):
                        ins = pe.matmul(G[:, 2, 0:n], xh["C"][:, j, :], w_l1[:, j, :], start=(j == 0), stop=(j == J - 1))
                    ins.then_inc(sems["C", "qkv"], 1)
                if "C2" in on:
                    for k in range(2):
                        shifted("C", c2, odd, k, masked, turn,
                                [(rd("A", f"e{k}"), A2), (rd("C", f"m{k}"), C1 + 1)])
                if "A1" in on:
                    pe.wait_ge(sems["A", "stk"], 2 * (a + 1))
                    pe.wait_ge(sems["A", "dup"], 2 * (a + 1))
                    pe.wait_ge(sems["A", "v"], a + 1)
                    for kq in range(2):
                        for t in range(8):
                            ins = pe.transpose(G[:, kq, t * 64:(t + 1) * 64].bitcast(F16),
                                               stkA[:, kq, 2 * t:2 * t + 2, :].rearrange("p h w -> p (h w)"), idh[:])
                    ins.then_inc(sems["A", "tr"], 1)
                if "M" in on:
                    pe.wait_ge(sems["M", "xh"], m + 1)
                    freed(pe, turn, [(rd("C", "tmp", "v"), C1)])
                    freed(pe, turn, [(rd("A", "ot"), A2)])
                    for n in range(NH):
                        for j in range(J):
                            ins = pe.matmul(G[:, 2 + n // 4, (n % 4) * 128:(n % 4 + 1) * 128],
                                            w_fc1[:, j, n * 128:(n + 1) * 128], xh["M"][:, j, :],
                                            start=(j == 0), stop=(j == J - 1))
                    ins.then_inc(sems["M", "fc1"], 1)
                if "A2" in on:
                    project("A", a2, w_proj, turn, [(ev_a, A1)])
                if "C2" in on:
                    values_C(c2, odd, 1, turn, [(ev_a, A1), (rd("C", "cev"), C1 + 1)])
                if "A1" in on:
                    for k in range(2):
                        scores("A", a, par, k, masked, turn,
                               [(rd("C", f"e{k}"), C2), (rd("A", f"e{k}"), A2)])
                if "C1" in on:
                    pe.wait_ge(sems["C", "stk"], 4 * (c + 1))
                    pe.wait_ge(sems["C", "v"], c + 1)
                    freed(pe, turn, [(rd("M", "u"), M_)])
                    for t in range((H + KV) // 2):
                        ins = pe.transpose(G[:, 2 + t // 8, (t % 8) * 64:(t % 8 + 1) * 64].bitcast(F16),
                                           stkC[:, 2 * t:2 * t + 2, :].rearrange("p h w -> p (h w)"), idh[:])
                    ins.then_inc(sems["C", "tr"], 1)
                if "C2" in on:
                    project("C", c2, w_o1, turn, [(rd("A", "res"), A2), (ev_a, A1)])
                if "C1" in on:
                    for k in range(2):
                        scores("C", c, par, k, masked, turn,
                               [(rd("A", f"m{k}"), A1), (rd("C", f"e{k}"), C2), (rd("A", f"e{k}"), A2)])
                if "A1" in on:
                    max_transposed("A", a, turn, [(rd("C", "ot"), C2), (ev_a, A1)])
                if "M" in on:
                    pe.wait_ge(sems["M", "gl"], m + 1)
                    freed(pe, turn, [(ev_c, C1), (rd("M", "u"), M_)])
                    for n in range(NH):
                        ins = pe.matmul(G[:, 2, 0:C], GL[:, n, :], w_fc2[:, n, :], start=(n == 0), stop=(n == NH - 1))
                    ins.then_inc(sems["M", "fc2"], 1)
                if "C1" in on:
                    max_transposed("C", c, turn, [(rd("A", "cev"), A1), (rd("C", "ot"), C2), (rd("C", "cev"), C1 + 1)])

            flag = pe.value_load(msk_flag[0:1, 0:1].bitcast(I32))
            with pe.If(flag):
                turns(pe, lambda turn, par: turn_pe(turn, par, True))
            with pe.Else():
                turns(pe, lambda turn, par: turn_pe(turn, par, False))


SILU = 6
SM_MIN = 7
CONSTS = 10
QB_PARTS = 15
ADA = 19
GAM_ROWS = 23
MASK_ROW = 28
MASK_FLAG = 29
SETUP_END = 32


def _tables():
    freqs = (np.float32(1.0) / np.power(np.float32(10000.0), np.arange(0, D, 2, dtype=np.float32) / np.float32(D))
             ).astype(np.float32)
    emb = np.arange(T, dtype=np.float32)[:, None] * freqs[None, :]
    cos = np.concatenate([np.cos(emb), np.cos(emb)], -1).astype(np.float32)
    sin = np.concatenate([-np.sin(emb), np.sin(emb)], -1).astype(np.float32)
    inv = np.float32(1.0 / np.sqrt(D))

    def full(t):
        return np.concatenate([np.tile(t * inv, (1, H)), np.tile(t, (1, KV))], 1).astype(np.float32)

    i = np.arange(T)
    hidden = (np.abs(i[None, :] - i[:, None]) > 32) & ~(i % 64 == 0)[None, :]
    return full(cos), full(sin), np.where(hidden, np.float32(NEG), np.float32(0.0)), np.eye(128, dtype=np.float32)


def kernel(**inputs):
    import concourse.bacc as bacc
    from concourse.bass_utils import run_bass_kernel_spmd

    a = {k: np.asarray(v) for k, v in inputs.items()}

    def chunks(w):
        return np.ascontiguousarray(w.T.reshape(-1, 128, w.shape[0]).transpose(1, 0, 2))

    def col(v):
        return np.ascontiguousarray(v.reshape(-1, 128).T)

    d = np.arange(D)
    q_order = np.concatenate([(4 * (2 * s + r) + i) * D + d for s in range(2) for i in range(4) for r in range(2)])
    o_order = np.concatenate([(4 * (2 * s + r) + 2 * ih + c) * D + d
                              for c in range(2) for s in range(2) for ih in range(2) for r in range(2)])
    cos_t, sin_t, window, ident = _tables()
    data = {
        "x": a["x"],
        "cond_t": np.ascontiguousarray(a["cond_2048"].T.reshape(J, 128, NB).transpose(1, 0, 2)),
        "mask": a["mask_1x1xSxS_ff0"].reshape(T, T),
        "wqkv": chunks(a["L0_cond_Wqkv"]),
        "qbias": a["L0_cond_q_bias"].reshape(1, C),
        "vbias": col(a["L0_cond_v_bias"]),
        "sml": a["L0_cond_scale_mul_log"].reshape(1, H),
        "wproj": chunks(a["L0_cond_Wproj"]),
        "bproj": a["L0_cond_bproj"].reshape(1, C),
        "wada": chunks(a["L0_cond_Wada"]),
        "bada_row": np.ascontiguousarray(a["L0_cond_bada"][:2 * C]).reshape(1, 2 * C),
        "bada_col": col(a["L0_cond_bada"]),
        "wfc1": chunks(a["L0_cond_Wfc1"]),
        "bfc1": col(a["L0_cond_bfc1"]),
        "wfc2": chunks(a["L0_cond_Wfc2"]),
        "bfc2": a["L0_cond_bfc2"].reshape(1, C),
        "wada1": chunks(a["L1_cond_W_ada"]),
        "bada1": col(a["L1_cond_b_ada"]),
        "wq1": chunks(a["L1_cond_Wq"][q_order]),
        "wkd": a["L1_cond_Wkd"],
        "wkvu": np.ascontiguousarray(np.concatenate([a["L1_cond_Wku"], a["L1_cond_Wvu"]], 0).T),
        "wo1": chunks(a["L1_cond_Wo"][:, o_order]),
        "ident": ident, "cos_t": cos_t, "sin_t": sin_t, "window": window,
    }
    nc = bacc.Bacc("TRN2", target_bir_lowering=False, num_devices=1)
    arrays, args = {}, {}
    for name, v in data.items():
        v = np.ascontiguousarray(v)
        arrays[f"in_{name}"] = v
        args[name] = nc.dram_tensor(f"in_{name}", v.shape, mybir.dt.from_np(v.dtype), kind="ExternalInput").ap()
    args["out"] = nc.dram_tensor("out_0", (NB, T, C), F32, kind="ExternalOutput").ap()
    block_pair(nc, **args)
    r = run_bass_kernel_spmd(nc, [arrays], core_ids=[0])
    return r.results[0]["out_0"]
```

```python
from contextlib import ExitStack

import numpy as np
import concourse.bass as bass
from concourse import mybir

F32 = mybir.dt.float32
F16 = mybir.dt.float16
BF16 = mybir.dt.bfloat16
U32 = mybir.dt.uint32
I32 = mybir.dt.int32
ALU = mybir.AluOpType
ACT = mybir.ActivationFunctionType
AX = mybir.AxisListType

NB, T, C = 16, 128, 256
H, D = 16, 16
KV = 4
HID = 4 * C
LAT = 64
J = C // 128
NH = HID // 128
EPS0, EPS1 = 1e-6, 1e-5
NEG = -1e30
CSCALE = 64.0
GELU_A = 0.044715
GELU_C = float(np.sqrt(np.float32(2.0 / np.pi)))
WS = 64.0
OFF = {"A1": 0, "A2": 1, "A3": 2, "M1": 3, "M2": 4, "C1": 5, "C2": 6, "C3": 7}
LAST = NB + OFF["C3"]
PEEL = OFF["C3"]
RSQRT = 0x5F3759DF


def block_pair(nc, x, cond_t, mask, wqkv, qbias, vbias, sml, wproj, bproj, wada, bada_row, bada_col,
               wfc1, bfc1, wfc2, bfc2, wada1, bada1, wq1, wkd, wkvu, wo1, ident, cos_t, sin_t, window, out):
    ctx = ExitStack()
    with ctx:
        def sb(name, shape, dt=F32):
            return ctx.enter_context(nc.sbuf_tensor(name, shape, dt))

        def sem(name):
            return ctx.enter_context(nc.semaphore(name))

        S = [ctx.enter_context(nc.psum_tensor(f"scores{k}", [128, 2, 512], F32)) for k in range(2)]
        G = ctx.enter_context(nc.psum_tensor("general", [128, 4, 512], F32))

        raw_qkv = sb("raw_qkv", [128, J, 3 * C])
        raw_fc1 = sb("raw_fc1", [128, J, HID])
        raw_fc2 = sb("raw_fc2", [128, NH, C])
        raw_l1 = sb("raw_l1", [128, J, C + 2 * KV * D])
        w_qkv = [sb(f"w_qkv{n}", [128, J, 3 * C], F16) for n in "hl"]
        w_fc1 = [sb(f"w_fc1{n}", [128, J, HID], F16) for n in "hl"]
        w_fc2 = [sb(f"w_fc2{n}", [128, NH, C], F16) for n in "hl"]
        w_l1 = [sb(f"w_l1{n}", [128, J, C + 2 * KV * D], F16) for n in "hl"]
        w_proj = sb("w_proj", [128, J, C])
        w_o1 = sb("w_o1", [128, J, C])
        p_all = sb("p_all", [128, 2, 2 * 2 * 512])
        p_flat = p_all[:].rearrange("p a b -> p (a b)")
        w_ada = p_flat[:, 0:J * 6 * C].rearrange("p (j c) -> p j c", j=J)
        w_ada1 = p_flat[:, J * 6 * C:J * 8 * C].rearrange("p (j c) -> p j c", j=J)
        w_kd = sb("w_kd", [LAT, C])
        w_kvu = sb("w_kvu", [LAT, 2 * KV * D])
        b_fc1 = sb("b_fc1", [128, NH])
        b_ada_row = sb("b_ada_row", [NB, 2 * C])
        b_ada_col = sb("b_ada_col", [128, 12])
        b_ada1 = sb("b_ada1", [128, 4])
        b_proj = sb("b_proj", [NB, C])
        b_fc2 = sb("b_fc2", [NB, C])
        b_v = sb("b_v", [128, J])
        q_b = sb("q_b", [1, C])
        idf = sb("idf", [128, 128])
        idh = sb("idh", [128, 128], F16)
        idb = sb("idb", [128, 128], BF16)
        win = sb("win", [128, 128])
        winb = sb("winb", [128, 128], BF16)
        cos_s = sb("cos_s", [128, C + KV * D])
        sin_s = sb("sin_s", [128, C + KV * D])
        msk = sb("msk", [128, 128])
        msk_max = sb("msk_max", [128, 1])
        msk_rel = sb("msk_rel", [128, 128])
        msk_any = sb("msk_any", [128, 128])
        msk_row = sb("msk_row", [128, 1])
        msk_flag = sb("msk_flag", [1, 1])
        cond = sb("cond", [128, J, NB])
        cexp = sb("cexp", [128, J, NB])
        cden = sb("cden", [128, J, NB])
        crec = sb("crec", [128, J, NB])
        csil = sb("csil", [128, J, NB])
        ada = sb("ada", [128, 12, NB])
        gam = sb("gam", [NB, 4, C])
        bproj_v = sb("bproj_v", [NB, C])
        bv_wide = sb("bv_wide", [128, J, NB])
        sm_in = sb("sm_in", [128, H])
        sm_min = sb("sm_min", [128, H])
        sm = sb("sm", [128, H])
        qb_h = sb("qb_h", [1, 3, C], BF16)
        qb_r = sb("qb_r", [1, 3, C])
        qb3 = sb("qb3", [3, C], BF16)
        one3 = sb("one3", [3, 128], BF16)

        X = sb("x_res", [128, NB, C])
        gb = {s: sb(f"gb_{s}", [128, 2, 2, C]) for s in "AM"}
        st = sb("st", [128, 3, 6])
        msum = sb("msum", [128, 3])
        mdif = sb("mdif", [128, 3])
        msq = sb("msq", [128, 3])
        mean = sb("mean", [128, 3])
        eps = sb("eps", [128, 3])
        rin = sb("rin", [128, 3 + 2 * H])
        root = sb("root", [128, 3 + 2 * H])
        rtmp = sb("rtmp", [128, 3 + 2 * H])
        nmr = sb("nmr", [128, 3])
        xn = {s: sb(f"xn_{s}", [128, C]) for s in "AMC"}
        x32 = {s: sb(f"x32_{s}", [128, J, 128]) for s in "AMC"}
        xh = {s: sb(f"xh_{s}", [128, J, 128], F16) for s in "AMC"}
        xl = {s: sb(f"xl_{s}", [128, J, 128], F16) for s in "AMC"}
        sq = sb("sq", [128, 2 * C])
        qsc = sb("qsc", [128, 2 * H])
        tmpA = sb("tmpA", [128, 2 * C])
        stkA = sb("stkA", [128, 2, H, 64], F16)
        rot1 = sb("rot1", [128, C + KV * D])
        rot2 = sb("rot2", [128, C + KV * D])
        tmpC = sb("tmpC", [128, C + KV * D])
        stkC = sb("stkC", [128, H + KV, 64], F16)
        qk = {"A": sb("qk_A", [128, 2, 2 * H * 64], F16),
              "C": sb("qk_C", [128, 2, (H + KV) * 64], F16)}
        V = {"A": sb("v_A", [128, 2, H, 32]), "C": sb("v_C", [128, 2, KV, 32])}
        mx = {s: sb(f"mx_{s}", [128, H]) for s in "AC"}
        cmax = {s: sb(f"cmax_{s}", [128, 2, 2, 8], F16) for s in "AC"}
        cT = {s: sb(f"cT_{s}", [32, 128], F16) for s in "AC"}
        P = {s: p_all[:, n].rearrange("p (k r q) -> p k r q", k=2, r=2) for n, s in enumerate("AC")}
        ou = {s: sb(f"ou_{s}", [128, 4, 128]) for s in "AC"}
        rcp = {s: sb(f"rcp_{s}", [128, H]) for s in "AC"}
        on = {s: sb(f"on_{s}", [128, C]) for s in "AC"}
        oT = {s: sb(f"oT_{s}", [128, J, 128]) for s in "AC"}
        xg = {s: sb(f"xg_{s}", [128, C]) for s in "AM"}
        upd = {s: sb(f"upd_{s}", [128, C]) for s in "AM"}
        U = sb("u", [128, NH, 128])
        S2 = sb("s2", [128, NH, 128])
        Z = sb("z", [128, NH, 128])
        GH = sb("gh", [128, NH, 128], F16)
        GLo = sb("gl", [128, NH, 128], F16)

        scratch = nc.dram_tensor("gamma_rows", (NB, 4 * C), F32).ap()

        x_in = [sem("x_in0"), sem("x_in1")]
        w_in = {n: sem(f"in_{n}") for n in ("cond", "ada", "qkv", "consts", "mlp", "l1", "mask", "sm")}
        p_dve = sem("setup_dve")
        p_act = sem("setup_act")
        p_pool = sem("setup_pool")
        p_pe = sem("setup_pe")
        w_split = sem("weights_split")
        qb_in = sem("qbias_rows_in")
        gam_out = sem("gamma_rows_out")
        gb_in = {s: sem(f"gamma_in_{s}") for s in "AM"}
        attention = ("tr evq evk hi dup lo s0 s1 m0 m1 ch cl ct cev p0 p1 e0 e1 pv ou ut rcp on ot oe o res"
                     " xn xt x32 xh xl stats qkv v tmp ")
        sems = {}
        for stage, steps in (("A", attention + "sq n2 qsc xg upd"),
                             ("M", "stats xn xt x32 xh xl fc1 u sqr z tanh gl gh glo fc2 xg upd res"),
                             ("C", attention + "r1 r2")):
            for n in steps.split():
                sems[stage, n] = sem(f"{stage}_{n}")
        roots_done = sem("roots")
        c_in = {s: sem(f"{s}_max_rows_in") for s in "AC"}
        y_out = sem("y_out")

        def wait(eng, s, n):
            if isinstance(n, int) and n <= 0:
                return
            eng.wait_ge(s, n)

        def rd(stage, *steps):
            return tuple((stage[0], s) for s in steps), stage

        READERS = {
            0: [(rd("M1", "x32"), rd("C1", "x32")), (rd("A3", "upd"),), (rd("M1", "u"),), (rd("C1", "evq"),)],
            1: [(rd("A1", "x32"),), (rd("M2", "upd"),), (rd("C1", "tmp"),), (rd("A2", "ou"),), (rd("C1", "evk"),)],
            2: [(rd("A3", "oe"), rd("C3", "oe")), (rd("A1", "tmp"),), (rd("C3", "res"),), (rd("A2", "on"),)],
            3: [(rd("A2", "cev"), rd("C2", "cev")), (rd("A1", "v"),), (rd("M1", "u"),), (rd("C2", "ou"),),
                (rd("C2", "on"),)],
            "S0": [(rd("A2", "e0"),), (rd("C2", "e0"),), (rd("A1", "m0"),), (rd("C1", "m0"),)],
            "S1": [(rd("A2", "e1"),), (rd("C2", "e1"),), (rd("A1", "evq"),), (rd("A1", "m1"),), (rd("C1", "m1"),)],
        }

        def bank_free(eng, bank, nth, turn):
            uses = READERS[bank]
            for back in range(1, len(uses) + 1):
                k = nth - back
                t = turn if k >= 0 else turn - 1
                active = [(ss, t - OFF[stage]) for ss, stage in uses[k] if stage in stages(t)]
                for ss, b in active:
                    for s in ss:
                        eng.wait_ge(sems[s], b + 1)
                if active:
                    return

        def stages(turn):
            return [s for s, k in OFF.items() if not isinstance(turn, int) or 0 <= turn - k < NB]

        def turns(eng, body, before_loop=None):
            for t in range(PEEL):
                body(t, t % 2)
            if before_loop:
                before_loop()
            with eng.Fori(PEEL, NB - 2, 2) as t:
                body(t, PEEL % 2)
                body(t + 1, (PEEL + 1) % 2)
            for t in range(NB - 1, LAST):
                body(t, t % 2)

        def at(b):
            return bass.ds(b, 1) if not isinstance(b, int) else slice(b, b + 1)

        def xrow(b):
            return X[:, at(b), :].rearrange("p o c -> p (o c)")

        def heads16(ap):
            return ap.rearrange("p (h d) -> p h d", d=D)

        def tiles(stage, par, first, count):
            return qk[stage][:, par, first * 128:(first + count) * 128]

        def parity(stage, par):
            return (par + OFF[stage]) % 2

        block = ctx.enter_context(nc.Block())

        @block.sync
        def _(sp):
            sp.dma_start(cond[:], cond_t).then_inc(w_in["cond"], 16)
            sp.dma_start(X[:, 0:2, :], x[0:2].rearrange("b t c -> t b c")).then_inc(x_in[0], 16)
            sp.dma_start(w_ada, wada).then_inc(w_in["ada"], 16)
            sp.dma_start(b_ada_row[:], bada_row.broadcast_to([NB, 2 * C])).then_inc(w_in["ada"], 16)
            sp.dma_start(b_ada_col[:], bada_col).then_inc(w_in["ada"], 16)
            sp.dma_start(w_ada1, wada1).then_inc(w_in["ada"], 16)
            sp.dma_start(b_ada1[:], bada1).then_inc(w_in["ada"], 16)
            sp.dma_start(raw_fc1[:], wfc1).then_inc(w_in["mlp"], 16)
            sp.dma_start(raw_fc2[:], wfc2).then_inc(w_in["mlp"], 16)
            sp.dma_start(b_fc1[:], bfc1).then_inc(w_in["mlp"], 16)
            sp.wait_ge(p_dve, QB_PARTS)
            sp.dma_start(qb3[:], qb_h[0:1, :, :]).then_inc(qb_in, 16)
            sp.dma_start(X[:, 2:NB, :], x[2:NB].rearrange("b t c -> t b c")).then_inc(x_in[1], 16)
            sp.wait_ge(p_dve, GAM_ROWS)
            sp.dma_start(scratch, gam[:].rearrange("b k c -> b (k c)")).then_inc(gam_out, 16)
            sp.wait_ge(gam_out, 16)

            def max_rows(stage, b, par):
                sp.wait_ge(sems[stage, "cev"], b + 1)
                for r in range(2):
                    dst = tiles(stage, par, 0, 8).rearrange("p (t q) -> p t q", q=128)
                    sp.dma_start(dst[64 * r + 48:64 * r + 50], cT[stage][16 * r:16 * r + 16, :]
                                 ).then_inc(c_in[stage], 16)

            def gammas(stage, b, par):
                if not isinstance(b, int):
                    sp.wait_ge(gam_out, 16)
                wait(sp, sems[stage, "upd"], b - 1)
                wait(sp, sems[stage, "xg"], b - 1)
                wait(sp, gb_in[stage], 16 * b)
                k = 0 if stage == "A" else 2 * C
                sp.dma_start(gb[stage][:, par].rearrange("p k c -> p (k c)"),
                             scratch[at(b), k:k + 2 * C].rearrange("o c -> (o c)").partition_broadcast(128)
                             ).then_inc(gb_in[stage], 16)

            def turn_sp(turn, par):
                on_ = stages(turn)
                if "A2" in on_:
                    gammas("A", turn - 1, (par + 1) % 2)
                if "M1" in on_:
                    gammas("M", turn - 3, (par + 1) % 2)
                if "A2" in on_:
                    max_rows("A", turn - OFF["A2"], parity("A2", par))
                if "C2" in on_:
                    max_rows("C", turn - OFF["C2"], parity("C2", par))
                if "C3" in on_:
                    b = turn - OFF["C3"]
                    sp.wait_ge(sems["C", "res"], b + 1)
                    sp.dma_start(out[at(b)].rearrange("o t c -> t (o c)"), X[:, at(b), :]
                                 ).then_inc(y_out, 16)

            turns(sp, turn_sp)
            sp.wait_ge(y_out, 16 * NB)

        @block.gpsimd
        def _(pool):
            pool.memset(stkA[:, :, :, 48:64], 0.0).then_inc(p_pool, 1)
            pool.memset(stkC[:, :, 48:64], 0.0).then_inc(p_pool, 1)
            pool.memset(V["A"][:], 1.0).then_inc(p_pool, 1)
            pool.memset(V["C"][:], 1.0).then_inc(p_pool, 1)
            pool.memset(one3[:], 1.0).then_inc(p_pool, 1)
            pool.wait_ge(p_pool, 5)
            pool.memset(stkA[:, 1, :, 48:50], CSCALE).then_inc(p_pool, 1)
            pool.memset(stkC[:, H:H + KV, 48:50], CSCALE).then_inc(p_pool, 1)

            def low(stage, b):
                pool.wait_ge(sems[stage, "xh"], b + 1)
                wait(pool, sems[stage, "fc1" if stage == "M" else "qkv"], b)
                pool.tensor_tensor(xl[stage][:], x32[stage][:], xh[stage][:], ALU.subtract
                                   ).then_inc(sems[stage, "xl"], 1)

            def with_bias(stage, b, par):
                pool.wait_ge(p_pool, 7)
                pool.wait_ge(gb_in[stage], 16 * (b + 1))
                if stage == "M":
                    pool.wait_ge(sems["A", "res"], b + 1)
                wait(pool, sems[stage, "res"], b)
                pool.tensor_tensor(xg[stage][:], xrow(b), gb[stage][:, par, 1, :], ALU.add
                                   ).then_inc(sems[stage, "xg"], 1)

            def residual(stage, b):
                pool.wait_ge(p_pool, 7)
                pool.wait_ge(sems[stage, "upd"], b + 1)
                pool.wait_ge(sems[stage, "xg"], b + 1)
                pool.tensor_tensor(xrow(b), upd[stage][:], xg[stage][:], ALU.add).then_inc(sems[stage, "res"], 1)

            def turn_pool(turn, par):
                on_ = stages(turn)
                b = {s: turn - OFF[s] for s in OFF}
                if "A1" in on_:
                    low("A", b["A1"])
                if "M2" in on_:
                    with_bias("M", b["M2"], parity("M2", par))
                if "A3" in on_:
                    with_bias("A", b["A3"], parity("A3", par))
                if "M2" in on_:
                    residual("M", b["M2"])
                if "C1" in on_:
                    low("C", b["C1"])
                if "A3" in on_:
                    residual("A", b["A3"])
                if "M1" in on_:
                    low("M", b["M1"])
                if "A1" in on_:
                    n = b["A1"] + 1
                    pool.wait_ge(sems["A", "hi"], n)
                    t4 = tmpA[:].rearrange("p (k h d) -> p k h d", k=2, d=D)
                    for k in range(2):
                        pool.tensor_tensor(stkA[:, k, :, 16 + 16 * k:32 + 16 * k], t4[:, k], stkA[:, k, :, 0:16],
                                           ALU.subtract).then_inc(sems["A", "lo"], 1)
                if "C1" in on_:
                    n = b["C1"] + 1
                    pool.wait_ge(sems["C", "hi"], n)
                    t3 = heads16(tmpC[:])
                    for k, hs in enumerate((slice(0, H), slice(H, H + KV))):
                        pool.tensor_tensor(stkC[:, hs, 16 + 16 * k:32 + 16 * k], t3[:, hs], stkC[:, hs, 0:16],
                                           ALU.subtract).then_inc(sems["C", "lo"], 1)
                if "M1" in on_:
                    n = b["M1"] + 1
                    pool.wait_ge(sems["M", "gh"], n)
                    wait(pool, sems["M", "fc2"], n - 1)
                    pool.tensor_tensor(GLo[:], Z[:], GH[:], ALU.subtract).then_inc(sems["M", "glo"], 1)

            turns(pool, turn_pool)

        @block.scalar
        def _(act):
            act.dma_start(idf[:], ident).then_inc(w_in["consts"], 16)
            act.dma_start(q_b[:], qbias).then_inc(w_in["consts"], 16)
            act.dma_start(b_v[:], vbias).then_inc(w_in["consts"], 16)
            act.dma_start(sm_in[:], sml.broadcast_to([128, H])).then_inc(w_in["sm"], 16)
            act.dma_start(raw_qkv[:], wqkv).then_inc(w_in["qkv"], 16)
            act.wait_ge(w_in["cond"], 16)
            act.activation(cexp[:], cond[:], ACT.Exp, scale=-1.0).then_inc(p_act, 1)
            act.dma_start(b_proj[:], bproj.broadcast_to([NB, C])).then_inc(w_in["consts"], 16)
            act.dma_start(b_fc2[:], bfc2.broadcast_to([NB, C])).then_inc(w_in["consts"], 16)
            act.dma_start(w_proj[:], wproj).then_inc(w_in["consts"], 16)
            act.dma_start(msk[:], mask).then_inc(w_in["mask"], 16)
            act.dma_start(w_kd[:], wkd).then_inc(w_in["l1"], 16)
            act.dma_start(w_kvu[:], wkvu).then_inc(w_in["l1"], 16)
            act.dma_start(raw_l1[:, :, 0:C], wq1).then_inc(w_in["l1"], 16)
            act.dma_start(w_o1[:], wo1).then_inc(w_in["l1"], 16)
            act.dma_start(cos_s[:], cos_t).then_inc(w_in["l1"], 16)
            act.dma_start(sin_s[:], sin_t).then_inc(w_in["l1"], 16)
            act.dma_start(win[:], window).then_inc(w_in["l1"], 16)
            act.wait_ge(p_dve, SM_MIN)
            act.activation(sm[:], sm_min[:], ACT.Exp).then_inc(p_act, 1)

            def normalize(stage, b):
                k = "AMC".index(stage)
                wait(act, sems[stage, "xt"], b)
                act.activation(xn[stage][:], xrow(b), ACT.Identity, bias=nmr[:, k:k + 1], scale=root[:, k:k + 1]
                               ).then_inc(sems[stage, "xn"], 1)

            def modulate(stage, b, bank, col, scale0, shift0):
                act.wait_ge(sems[stage, "xt"], b + 1)
                wait(act, sems[stage, "xl"], b)
                for j in range(J):
                    ins = act.activation(x32[stage][:, j, :], G[:, bank, col + j * 128:col + (j + 1) * 128],
                                         ACT.Identity, bias=ada[:, shift0 + j, at(b)], scale=ada[:, scale0 + j, at(b)])
                ins.then_inc(sems[stage, "x32"], 1)

            def high(stage, b):
                act.wait_ge(sems[stage, "x32"], b + 1)
                wait(act, sems[stage, "fc1" if stage == "M" else "qkv"], b)
                act.copy(xh[stage][:], x32[stage][:]).then_inc(sems[stage, "xh"], 1)

            def exps(stage, b):
                for k in range(2):
                    act.wait_ge(sems[stage, f"p{k}"], b + 1)
                    wait(act, sems[stage, "pv"], b)
                    act.activation(P[stage][:, k], S[k][:], ACT.Exp).then_inc(sems[stage, f"e{k}"], 1)

            def turn_act(turn, par):
                on_ = stages(turn)
                b = {s: turn - OFF[s] for s in OFF}
                if "A1" in on_:
                    modulate("A", b["A1"], 1, 0, 0, 4)
                    high("A", b["A1"])
                if "C1" in on_:
                    act.wait_ge(sems["C", "xt"], b["C1"] + 1)
                if "M1" in on_:
                    modulate("M", b["M1"], 0, 0, 2, 6)
                if "C1" in on_:
                    modulate("C", b["C1"], 0, C, 8, 10)
                if "C3" in on_:
                    act.wait_ge(sems["C", "ot"], b["C3"] + 1)
                for s, stage in (("A", "A3"), ("C", "C3")):
                    if stage in on_:
                        act.wait_ge(sems[s, "ot"], b[stage] + 1)
                        wait(act, sems[s, "o"], b[stage])
                        col = 0 if s == "A" else C
                        act.copy(oT[s][:].rearrange("p j q -> p (j q)"), G[:, 2, col:col + C]
                                 ).then_inc(sems[s, "oe"], 1)
                if "C1" in on_:
                    high("C", b["C1"])
                if "M1" in on_:
                    high("M", b["M1"])
                if "C2" in on_:
                    act.wait_ge(sems["C", "ct"], b["C2"] + 1)
                for s, stage in (("A", "A2"), ("C", "C2")):
                    if stage in on_:
                        n = b[stage]
                        act.wait_ge(sems[s, "ct"], n + 1)
                        wait(act, c_in[s], 32 * n)
                        col = 0 if s == "A" else 64
                        act.copy(cT[s][:], G[0:32, 3, col:col + 64].bitcast(F16)).then_inc(sems[s, "cev"], 1)
                if "A1" in on_:
                    n = b["A1"]
                    act.wait_ge(sems["A", "qkv"], n + 1)
                    wait(act, sems["A", "n2"], n)
                    act.activation(sq[:], G[:, 2, :], ACT.Square).then_inc(sems["A", "sq"], 1)
                    if isinstance(n, int) and n == 0:
                        act.wait_ge(p_pool, 7)
                    wait(act, sems["A", "pv"], n - 1)
                    act.activation(V["A"][:, parity("A1", par), :, 0:D], heads16(G[:, 3, 0:C]), ACT.Identity,
                                   scale=1.0 / WS).then_inc(sems["A", "v"], 1)
                if "A2" in on_:
                    exps("A", b["A2"])
                if "A1" in on_:
                    n = b["A1"]
                    act.wait_ge(sems["A", "tmp"], n + 1)
                    wait(act, sems["A", "tr"], n)
                    act.copy(stkA[:, :, :, 0:16].rearrange("p k h w -> p (k h) w"), heads16(tmpA[:])
                             ).then_inc(sems["A", "hi"], 1)
                if "C2" in on_:
                    exps("C", b["C2"])
                if "C1" in on_:
                    n = b["C1"]
                    act.wait_ge(sems["C", "tmp"], n + 1)
                    wait(act, sems["C", "tr"], n)
                    act.copy(stkC[:, :, 0:16], heads16(tmpC[:])).then_inc(sems["C", "hi"], 1)
                nxt = stages(turn + 1)
                if any(s in nxt for s in ("A1", "M1", "C1")):
                    act.wait_ge(roots_done, ROOT_STEPS * (turn + 2))
                for s, stage in (("A", "A1"), ("M", "M1"), ("C", "C1")):
                    if stage in nxt:
                        normalize(s, turn + 1 - OFF[stage])
                if "M1" in on_:
                    n = b["M1"]
                    act.wait_ge(sems["M", "fc1"], n + 1)
                    wait(act, sems["M", "gl"], n)
                    for k in range(NH):
                        ins = act.activation(U[:, k, :], G[:, 0 if k < 4 else 3, (k % 4) * 128:(k % 4 + 1) * 128],
                                             ACT.Identity, bias=b_fc1[:, k:k + 1], scale=1.0 / WS)
                    ins.then_inc(sems["M", "u"], 1)
                    act.wait_ge(sems["M", "u"], n + 1)
                    act.activation(S2[:], U[:], ACT.Square, scale=float(np.sqrt(GELU_A))
                                   ).then_inc(sems["M", "sqr"], 1)
                for s, stage in (("A", "A2"), ("C", "C2")):
                    if stage in on_:
                        act.wait_ge(sems[s, "pv"], b[stage] + 1)
                        wait(act, sems[s, "ut"], b[stage])
                        act.copy(ou[s][:].rearrange("p a q -> p (a q)"), G[:, 1 if s == "A" else 3, :]
                                 ).then_inc(sems[s, "ou"], 1)
                if "M1" in on_:
                    n = b["M1"]
                    act.wait_ge(sems["M", "z"], n + 1)
                    act.activation(S2[:], Z[:], ACT.Tanh, scale=GELU_C).then_inc(sems["M", "tanh"], 1)
                if "A1" in on_:
                    n = b["A1"]
                    act.wait_ge(sems["A", "tr"], n + 1)
                    wait(act, sems["A", "p1"], n - 1)
                    act.copy(qk["A"][:, parity("A1", par), :].bitcast(U32),
                             S[1][:].rearrange("p a b -> p (a b)").bitcast(U32)).then_inc(sems["A", "evq"], 1)
                if "C1" in on_:
                    n = b["C1"]
                    act.wait_ge(sems["C", "tr"], n + 1)
                    wait(act, sems["C", "p1"], n - 1)
                    dst = qk["C"][:, parity("C1", par), :].bitcast(U32)
                    act.copy(dst[:, 0:H * 32], G[:, 0, :].bitcast(U32)).then_inc(sems["C", "evq"], 1)
                    act.copy(dst[:, H * 32:], G[:, 1, 0:KV * 32].bitcast(U32)).then_inc(sems["C", "evk"], 1)
                if "M1" in on_:
                    n = b["M1"]
                    act.wait_ge(sems["M", "gl"], n + 1)
                    wait(act, sems["M", "fc2"], n)
                    act.copy(GH[:], Z[:]).then_inc(sems["M", "gh"], 1)

            act.wait_ge(p_dve, ADA)
            act.wait_ge(roots_done, ROOT_STEPS)
            normalize("A", 0)
            turns(act, turn_act)

        @block.vector
        def _(dve):
            done = [0]

            def setup(ins, now=True):
                done[0] += 1
                ins.then_inc(p_dve, 1)
                if now:
                    dve.wait_ge(p_dve, done[0])

            def split(parts, raw, scale, nth):
                dve.tensor_scalar(parts[0][:], raw, scale, None, ALU.mult).then_inc(w_split, 1)
                dve.wait_ge(w_split, 2 * nth + 1)
                dve.scalar_tensor_tensor(parts[1][:], raw, scale, parts[0][:], ALU.mult, ALU.subtract
                                         ).then_inc(w_split, 1)

            setup(dve.memset(eps[:, 0:2], EPS0), now=False)
            setup(dve.memset(eps[:, 2:3], EPS1), now=False)
            setup(dve.memset(rin[:], 1.0), now=False)
            setup(dve.memset(st[:], 1.0))
            dve.wait_ge(w_in["sm"], 16)
            setup(dve.tensor_scalar(sm_min[:], sm_in[:], float(np.log(np.float32(100.0))), None, ALU.min))
            assert done[0] == SM_MIN
            dve.wait_ge(p_act, 1)
            setup(dve.tensor_scalar(cden[:], cexp[:], 1.0, None, ALU.add))
            setup(dve.reciprocal(crec[:], cden[:]))
            setup(dve.tensor_tensor(csil[:], cond[:], crec[:], ALU.mult))
            assert done[0] == SILU
            dve.wait_ge(w_in["consts"], 96)
            setup(dve.tensor_scalar(qb_r[:, 0, :], q_b[:], WS, None, ALU.mult))
            setup(dve.tensor_copy(qb_h[:, 0, :], qb_r[:, 0, :]))
            setup(dve.tensor_tensor(qb_r[:, 1, :], qb_r[:, 0, :], qb_h[:, 0, :], ALU.subtract))
            setup(dve.tensor_copy(qb_h[:, 1, :], qb_r[:, 1, :]))
            setup(dve.tensor_tensor(qb_r[:, 2, :], qb_r[:, 1, :], qb_h[:, 1, :], ALU.subtract))
            setup(dve.tensor_copy(qb_h[:, 2, :], qb_r[:, 2, :]))
            assert done[0] == QB_PARTS
            setup(dve.tensor_copy(idh[:], idf[:]), now=False)
            setup(dve.tensor_copy(idb[:], idf[:]), now=False)
            setup(dve.tensor_copy(bv_wide[:], b_v[:].unsqueeze(2).broadcast_to([128, J, NB])))
            assert done[0] == CONSTS

            def norms_and_roots(turn, first=False):
                todo = [(k, s[0], turn - OFF[s]) for k, s in enumerate(("A1", "M1", "C1")) if s in stages(turn)]
                heads = not first and "A1" in stages(turn - 1)
                if not todo and not heads:
                    return
                for k, s, b in todo:
                    dve.wait_ge(x_in[0], 16)
                    if s != "A":
                        dve.wait_ge(sems["A" if s == "M" else "M", "res"], b + 1)
                    dve.bn_stats(st[:, k, :], xrow(b)).then_inc(sems[s, "stats"], 1)
                if heads:
                    dve.wait_ge(sems["A", "sq"], turn)
                    dve.tensor_reduce(rin[:, 3:], heads16(sq[:]), AX.X, ALU.add).then_inc(sems["A", "n2"], 1)
                for k, s, b in todo:
                    dve.wait_ge(sems[s, "stats"], b + 1)
                base = ROOT_STEPS * turn
                n = [0]

                def step(ins, now=True):
                    ins.then_inc(roots_done, 1)
                    n[0] += 1
                    if now:
                        dve.wait_ge(roots_done, base + n[0])

                even, odd, even2, odd2 = (st[:, :, n_] for n_ in (1, 4, 2, 5))
                step(dve.tensor_tensor(msum[:], even, odd, ALU.add), now=False)
                step(dve.tensor_tensor(mdif[:], even, odd, ALU.subtract), now=False)
                step(dve.tensor_tensor(msq[:], even2, odd2, ALU.add))
                step(dve.tensor_scalar(mean[:], msum[:], 0.5, None, ALU.mult), now=False)
                step(dve.scalar_tensor_tensor(msq[:], msq[:], 1.0 / C, eps[:], ALU.mult, ALU.add), now=False)
                if heads:
                    dve.wait_ge(sems["A", "n2"], turn)
                step(dve.tensor_scalar(rin[:, 3:], rin[:, 3:], 1e-24 * WS * WS, None, ALU.max), now=False)
                step(dve.tensor_tensor(mdif[:], mdif[:], mdif[:], ALU.mult))
                step(dve.scalar_tensor_tensor(rin[:, 0:3], mdif[:], 0.25, msq[:], ALU.mult, ALU.add))
                step(dve.tensor_scalar(root[:].bitcast(I32), rin[:].bitcast(I32), -0.5, float(RSQRT), ALU.mult, ALU.add))
                for _ in range(3):
                    step(dve.tensor_tensor(rtmp[:], root[:], root[:], ALU.mult))
                    step(dve.scalar_tensor_tensor(rtmp[:], rin[:], -0.5, rtmp[:], ALU.mult, ALU.mult))
                    step(dve.scalar_tensor_tensor(root[:], rtmp[:], 1.5, root[:], ALU.add, ALU.mult))
                step(dve.scalar_tensor_tensor(nmr[:], mean[:], -1.0, root[:, 0:3], ALU.mult, ALU.mult), now=False)
                assert n[0] == ROOT_STEPS

            dve.wait_ge(x_in[0], 16)
            norms_and_roots(0, first=True)
            dve.wait_ge(w_in["qkv"], 16)
            split(w_qkv, raw_qkv[:], WS, 0)
            dve.wait_ge(p_pe, 1)
            setup(dve.tensor_tensor(ada[:, 0:8, :], G[:, 0, 0:8 * NB].rearrange("p (k b) -> p k b", b=NB),
                                    b_ada_col[:, 4:12].unsqueeze(2).broadcast_to([128, 8, NB]), ALU.add), now=False)
            setup(dve.tensor_tensor(ada[:, 8:12, :], G[:, 0, 8 * NB:12 * NB].rearrange("p (k b) -> p k b", b=NB),
                                    b_ada1[:].unsqueeze(2).broadcast_to([128, 4, NB]), ALU.add))
            setup(dve.tensor_scalar(ada[:, 0:4, :], ada[:, 0:4, :], 1.0, None, ALU.add), now=False)
            setup(dve.tensor_scalar(ada[:, 8:10, :], ada[:, 8:10, :], 1.0, None, ALU.add))
            assert done[0] == ADA
            dve.wait_ge(p_pe, 2)
            for k in range(2):
                setup(dve.tensor_tensor(gam[:, 2 * k, :], G[0:NB, 1, k * C:(k + 1) * C], b_ada_row[:, k * C:(k + 1) * C],
                                        ALU.add), now=False)
            dve.wait_ge(p_pe, 3)
            setup(dve.tensor_tensor(bproj_v[:], G[0:NB, 2, 0:C], b_proj[:], ALU.add))
            setup(dve.tensor_tensor(gam[:, 1, :], gam[:, 0, :], bproj_v[:], ALU.mult), now=False)
            setup(dve.tensor_tensor(gam[:, 3, :], gam[:, 2, :], b_fc2[:], ALU.mult))
            assert done[0] == GAM_ROWS
            dve.wait_ge(w_in["mask"], 16)
            setup(dve.tensor_scalar(msk[:], msk[:], NEG, None, ALU.max))
            setup(dve.tensor_reduce(msk_max[:], msk[:], AX.X, ALU.max))
            setup(dve.tensor_scalar(msk_rel[:], msk[:], msk_max[:], None, ALU.subtract))
            setup(dve.tensor_scalar(msk_any[:], msk_rel[:], 0.0, None, ALU.is_lt))
            setup(dve.tensor_reduce(msk_row[:], msk_any[:], AX.X, ALU.max))
            assert done[0] == MASK_ROW
            dve.wait_ge(p_pe, 4)
            setup(dve.tensor_reduce(msk_flag[:], G[0:1, 3, 0:128], AX.X, ALU.max))
            assert done[0] == MASK_FLAG

            def later_setup(turn):
                if turn == 0:
                    dve.wait_ge(w_in["l1"], 112)
                    setup(dve.tensor_copy(winb[:], win[:]), now=False)
                    dve.wait_ge(p_pe, 5)
                    setup(dve.tensor_copy(raw_l1[:, :, C:], G[:, 0, 0:J * 128].rearrange("p (j k) -> p j k", j=J)))
                    assert done[0] == L1_WEIGHTS
                    dve.wait_ge(w_in["mlp"], 48)
                    split(w_fc1, raw_fc1[:], WS, 1)
                if turn == 1:
                    split(w_fc2, raw_fc2[:], 0.5 * WS, 2)
                if turn == 2:
                    split(w_l1, raw_l1[:], WS, 3)

            def qk_parts_A(b):
                dve.wait_ge(roots_done, ROOT_STEPS * (b + 2))
                if isinstance(b, int) and b == 0:
                    dve.wait_ge(p_act, 2)
                dve.tensor_tensor(qsc[:, 0:H], root[:, 3:3 + H], sm[:], ALU.mult).then_inc(sems["A", "qsc"], 1)
                dve.tensor_copy(qsc[:, H:], root[:, 3 + H:]).then_inc(sems["A", "qsc"], 1)
                dve.wait_ge(sems["A", "qsc"], 2 * (b + 1))
                wait(dve, sems["A", "lo"], 2 * b)
                dve.tensor_tensor(heads16(tmpA[:]), heads16(G[:, 2, :]),
                                  qsc[:].unsqueeze(2).broadcast_to([128, 2 * H, D]), ALU.mult
                                  ).then_inc(sems["A", "tmp"], 1)

            def dup_A(b):
                dve.wait_ge(sems["A", "hi"], b + 1)
                dve.tensor_copy(stkA[:, 0, :, 32:48], stkA[:, 0, :, 0:16]).then_inc(sems["A", "dup"], 1)
                dve.tensor_copy(stkA[:, 1, :, 16:32], stkA[:, 1, :, 0:16]).then_inc(sems["A", "dup"], 1)

            def qk_parts_C(b, par):
                dve.wait_ge(sems["C", "qkv"], b + 1)
                n = C + KV * D
                ps = G[:, 1, 0:n].rearrange("p (h two e) -> p h two e", two=2, e=D // 2)
                sn = sin_s[:].rearrange("p (h two e) -> p h two e", two=2, e=D // 2)
                r2 = rot2[:].rearrange("p (h two e) -> p h two e", two=2, e=D // 2)
                wait(dve, sems["C", "pv"], b - 1)
                dve.tensor_scalar(V["C"][:, par, :, 0:D], heads16(G[:, 1, n:n + KV * D]), 1.0 / WS, None, ALU.mult
                                  ).then_inc(sems["C", "v"], 1)
                dve.tensor_tensor(rot1[:], G[:, 1, 0:n], cos_s[:], ALU.mult).then_inc(sems["C", "r1"], 1)
                for half in range(2):
                    dve.tensor_tensor(r2[:, :, half, :], ps[:, :, 1 - half, :], sn[:, :, half, :], ALU.mult
                                      ).then_inc(sems["C", "r2"], 1)
                dve.wait_ge(sems["C", "r1"], b + 1)
                dve.wait_ge(sems["C", "r2"], 2 * (b + 1))
                wait(dve, sems["C", "lo"], 2 * b)
                dve.tensor_tensor(tmpC[:], rot1[:], rot2[:], ALU.add).then_inc(sems["C", "tmp"], 1)

            def dup_C(b):
                dve.wait_ge(sems["C", "hi"], b + 1)
                dve.tensor_copy(stkC[:, 0:H, 32:48], stkC[:, 0:H, 0:16]).then_inc(sems["C", "dup"], 1)
                dve.tensor_copy(stkC[:, H:, 16:32], stkC[:, H:, 0:16]).then_inc(sems["C", "dup"], 1)

            def maxima(stage, b):
                m3 = mx[stage][:].rearrange("p (r t) -> p r t", r=2)
                for k in range(2):
                    dve.wait_ge(sems[stage, f"s{k}"], b + 1)
                    dve.tensor_reduce(m3[:, :, 4 * k:4 * k + 4],
                                      S[k][:].rearrange("p r (t q) -> p r t q", q=128), AX.X, ALU.max
                                      ).then_inc(sems[stage, f"m{k}"], 1)

            def shift_rows(stage, b):
                m3 = mx[stage][:].rearrange("p (r t) -> p r t", r=2)
                for k in range(2):
                    dve.wait_ge(sems[stage, f"m{k}"], b + 1)
                wait(dve, sems[stage, "ct"], b)
                high, low = cmax[stage][:, :, 0, :], cmax[stage][:, :, 1, :]
                dve.tensor_scalar(high, m3, -1.0 / CSCALE, None, ALU.mult).then_inc(sems[stage, "ch"], 1)
                dve.wait_ge(sems[stage, "ch"], b + 1)
                dve.scalar_tensor_tensor(low, m3, -1.0 / CSCALE, high, ALU.mult, ALU.subtract
                                         ).then_inc(sems[stage, "cl"], 1)

            def over_sums(stage, b, bank):
                dve.wait_ge(sems[stage, "ut"], b + 1)
                v = G[:, bank, :].rearrange("p (h w) -> p h w", w=32)
                dve.reciprocal(rcp[stage][:], v[:, :, D]).then_inc(sems[stage, "rcp"], 1)
                dve.wait_ge(sems[stage, "rcp"], b + 1)
                wait(dve, sems[stage, "ot"], b)
                dve.tensor_tensor(heads16(on[stage][:]), v[:, :, 0:D], rcp[stage][:].unsqueeze(2).broadcast_to([128, H, D]),
                                  ALU.mult).then_inc(sems[stage, "on"], 1)

            def gated(stage, b, bank, done_step, scale, par):
                dve.wait_ge(sems[stage, done_step], b + 1)
                dve.wait_ge(gb_in[stage], 16 * (b + 1))
                wait(dve, sems[stage, "res"], b)
                dve.scalar_tensor_tensor(upd[stage][:], G[:, bank, 0:C], scale, gb[stage][:, par, 0, :],
                                         ALU.mult, ALU.mult).then_inc(sems[stage, "upd"], 1)

            def turn_dve(turn, par):
                on_ = stages(turn)
                b = {s: turn - OFF[s] for s in OFF}
                if "M2" in on_:
                    gated("M", b["M2"], 1, "fc2", 1.0 / WS, parity("M2", par))
                if "A3" in on_:
                    gated("A", b["A3"], 0, "o", 1.0, parity("A3", par))
                if isinstance(turn, int) and turn == 1:
                    dve.wait_ge(x_in[1], 16)
                norms_and_roots(turn + 1)
                if "A1" in on_:
                    qk_parts_A(b["A1"])
                if "C1" in on_:
                    qk_parts_C(b["C1"], parity("C1", par))
                if "A1" in on_:
                    dup_A(b["A1"])
                if "C1" in on_:
                    dup_C(b["C1"])
                if isinstance(turn, int):
                    later_setup(turn)
                if "C3" in on_:
                    n = b["C3"]
                    dve.wait_ge(sems["C", "o"], n + 1)
                    dve.tensor_tensor(xrow(n), G[:, 2, 0:C], xrow(n), ALU.add).then_inc(sems["C", "res"], 1)
                if "M1" in on_:
                    n = b["M1"]
                    dve.wait_ge(sems["M", "sqr"], n + 1)
                    wait(dve, sems["M", "glo"], n)
                    dve.scalar_tensor_tensor(Z[:], S2[:], 1.0, U[:], ALU.add, ALU.mult).then_inc(sems["M", "z"], 1)
                if "A2" in on_:
                    over_sums("A", b["A2"], 2)
                if "M1" in on_:
                    n = b["M1"]
                    dve.wait_ge(sems["M", "tanh"], n + 1)
                    dve.scalar_tensor_tensor(Z[:], S2[:], 1.0, U[:], ALU.add, ALU.mult).then_inc(sems["M", "gl"], 1)
                if "A1" in on_:
                    maxima("A", b["A1"])
                if "C2" in on_:
                    over_sums("C", b["C2"], 3)
                if "A1" in on_:
                    shift_rows("A", b["A1"])
                if "C1" in on_:
                    maxima("C", b["C1"])
                    shift_rows("C", b["C1"])

            turns(dve, turn_dve)

        @block.tensor
        def _(pe):
            pe.wait_ge(p_dve, SILU)
            pe.wait_ge(w_in["ada"], 80)
            for k in range(12):
                src, w, col = (csil, w_ada, 2 * C + k * 128) if k < 8 else (cond, w_ada1, (k - 8) * 128)
                for j in range(J):
                    ins = pe.matmul(G[:, 0, k * NB:(k + 1) * NB], w[:, j, col:col + 128], src[:, j, :],
                                    start=(j == 0), stop=(j == J - 1))
            ins.then_inc(p_pe, 1)
            for j in range(J):
                ins = pe.matmul(G[0:NB, 1, :], csil[:, j, :], w_ada[:, j, 0:2 * C], start=(j == 0), stop=(j == J - 1))
            ins.then_inc(p_pe, 1)
            pe.wait_ge(p_dve, CONSTS)
            for j in range(J):
                ins = pe.matmul(G[0:NB, 2, 0:C], bv_wide[:, j, :], w_proj[:, j, :], start=(j == 0), stop=(j == J - 1))
            ins.then_inc(p_pe, 1)
            pe.wait_ge(p_dve, MASK_ROW)
            pe.transpose(G[0:1, 3, 0:128], msk_row[:], idf[:]).then_inc(p_pe, 1)
            pe.wait_ge(w_in["l1"], 112)
            pe.wait_ge(p_dve, ADA)
            for j in range(J):
                ins = pe.matmul(G[:, 0, j * 128:(j + 1) * 128], w_kd[:, j * 128:(j + 1) * 128], w_kvu[:],
                                start=True, stop=True)
            ins.then_inc(p_pe, 1)
            pe.wait_ge(qb_in, 16)
            pe.wait_ge(p_pool, 7)
            pe.wait_ge(p_dve, MASK_FLAG)

            def tokens_to_channels(stage, b, bank, col):
                pe.wait_ge(sems[stage, "xn"], b + 1)
                for j in range(J):
                    ins = pe.transpose(G[:, bank, col + j * 128:col + (j + 1) * 128],
                                       xn[stage][:, j * 128:(j + 1) * 128], idf[:])
                ins.then_inc(sems[stage, "xt"], 1)

            def passes(x_parts, w_parts):
                return [(x_parts[0], w_parts[0]), (x_parts[1], w_parts[0]), (x_parts[0], w_parts[1])]

            def scores(stage, b, par, k, masked, turn, nth):
                if k == 0:
                    pe.wait_ge(sems[stage, "evq"], b + 1)
                    if stage == "C":
                        pe.wait_ge(sems[stage, "evk"], b + 1)
                bank_free(pe, f"S{k}", nth, turn)
                if stage == "C":
                    for r in range(2):
                        pe.matmul(S[k][:, r, :], idb[:], winb[:].unsqueeze(1).broadcast_to([128, 4, 128]),
                                  start=True, stop=False, skip_group_check=True)
                elif masked:
                    for r in range(2):
                        pe.matmul(S[k][:, r, :], idf[:], msk_rel[:].unsqueeze(1).broadcast_to([128, 4, 128]),
                                  start=True, stop=False, skip_group_check=True)
                added = masked or stage == "C"
                for t in range(4):
                    for r in range(2):
                        rows = slice(64 * r, 64 * r + 48)
                        tk = KT + (4 * k + t if stage == "A" else k)
                        ins = pe.matmul(S[k][:, r, t * 128:(t + 1) * 128], tiles(stage, par, 4 * k + t, 1)[rows],
                                        tiles(stage, par, tk, 1)[rows], start=not added, stop=True,
                                        skip_group_check=True)
                ins.then_inc(sems[stage, f"s{k}"], 1)

            def shifted(stage, b, par, k, masked, turn, nth):
                if k == 0:
                    pe.wait_ge(c_in[stage], 32 * (b + 1))
                bank_free(pe, f"S{k}", nth, turn)
                if stage == "C":
                    for r in range(2):
                        pe.matmul(S[k][:, r, :], winb[:], idb[:].unsqueeze(1).broadcast_to([128, 4, 128]),
                                  start=True, stop=False, skip_group_check=True)
                    for r in range(2):
                        rows = slice(64 * r, 64 * r + 64)
                        ins = pe.matmul(S[k][:, r, :], tiles(stage, par, KT + k, 1)[rows],
                                        tiles(stage, par, 4 * k, 4)[rows], start=False, stop=True,
                                        skip_group_check=True)
                else:
                    if masked:
                        for r in range(2):
                            pe.matmul(S[k][:, r, :], msk_rel[:], idf[:].unsqueeze(1).broadcast_to([128, 4, 128]),
                                      start=True, stop=False, skip_group_check=True)
                    for t in range(4):
                        for r in range(2):
                            rows = slice(64 * r, 64 * r + 64)
                            ins = pe.matmul(S[k][:, r, t * 128:(t + 1) * 128], tiles(stage, par, KT + 4 * k + t, 1)[rows],
                                            tiles(stage, par, 4 * k + t, 1)[rows], start=not masked, stop=True,
                                            skip_group_check=True)
                ins.then_inc(sems[stage, f"p{k}"], 1)

            def output(stage, b, bank, nth, w, turn):
                pe.wait_ge(sems[stage, "oe"], b + 1)
                bank_free(pe, bank, nth, turn)
                for j in range(J):
                    ins = pe.matmul(G[:, bank, 0:C], oT[stage][:, j, :], w[:, j, :], start=(j == 0), stop=(j == J - 1))
                ins.then_inc(sems[stage, "o"], 1)

            def turn_pe(turn, par, masked):
                on_ = stages(turn)
                b = {s: turn - OFF[s] for s in OFF}
                if "A1" in on_:
                    bank_free(pe, 1, 0, turn)
                    tokens_to_channels("A", b["A1"], 1, 0)
                if "M1" in on_ or "C1" in on_:
                    bank_free(pe, 0, 0, turn)
                if "M1" in on_:
                    tokens_to_channels("M", b["M1"], 0, 0)
                if "C1" in on_:
                    tokens_to_channels("C", b["C1"], 0, C)
                if "A3" in on_ or "C3" in on_:
                    bank_free(pe, 2, 0, turn)
                for s, stage in (("A", "A3"), ("C", "C3")):
                    if stage in on_:
                        pe.wait_ge(sems[s, "on"], b[stage] + 1)
                        col = 0 if s == "A" else C
                        for j in range(J):
                            ins = pe.transpose(G[:, 2, col + j * 128:col + (j + 1) * 128],
                                               on[s][:, j * 128:(j + 1) * 128], idf[:])
                        ins.then_inc(sems[s, "ot"], 1)
                if "M2" in on_:
                    n = b["M2"]
                    pe.wait_ge(sems["M", "glo"], n + 1)
                    if isinstance(n, int) and n == 0:
                        pe.wait_ge(w_split, 6)
                    bank_free(pe, 1, 1, turn)
                    for k in range(NH):
                        for i, (g, w) in enumerate(passes((GH, GLo), w_fc2)):
                            ins = pe.matmul(G[:, 1, 0:C], g[:, k, :], w[:, k, :], start=(k == 0 and i == 0),
                                            stop=(k == NH - 1 and i == 2))
                    ins.then_inc(sems["M", "fc2"], 1)
                if "A2" in on_ or "C2" in on_:
                    bank_free(pe, 3, 0, turn)
                for s, stage in (("A", "A2"), ("C", "C2")):
                    if stage in on_:
                        pe.wait_ge(sems[s, "cl"], b[stage] + 1)
                        col = 0 if s == "A" else 64
                        pe.transpose(G[0:32, 3, col:col + 64].bitcast(F16), cmax[s][:].rearrange("p r s t -> p (r s t)"),
                                     idh[:]).then_inc(sems[s, "ct"], 1)
                if "A3" in on_:
                    output("A", b["A3"], 0, 1, w_proj, turn)
                if "A1" in on_:
                    n = b["A1"]
                    pe.wait_ge(sems["A", "xl"], n + 1)
                    if isinstance(n, int) and n == 0:
                        pe.wait_ge(w_split, 2)
                    bank_free(pe, 2, 1, turn)
                    bank_free(pe, 3, 1, turn)
                    for i, (x_, w) in enumerate(passes((xh["A"], xl["A"]), w_qkv)):
                        for j in range(J):
                            pe.matmul(G[:, 3, 0:C], x_[:, j, :], w[:, j, 2 * C:3 * C], start=(i == 0 and j == 0),
                                      stop=(i == 2 and j == J - 1))
                            ins = pe.matmul(G[:, 2, :], x_[:, j, :], w[:, j, 0:2 * C], start=(i == 0 and j == 0),
                                            stop=(i == 2 and j == J - 1), skip_group_check=True)
                            if i == 0 and j == 0:
                                pe.matmul(G[:, 2, 0:C], one3[:], qb3[:], start=False, stop=False, skip_group_check=True)
                    ins.then_inc(sems["A", "qkv"], 1)
                if "A2" in on_:
                    for k in range(2):
                        shifted("A", b["A2"], parity("A2", par), k, masked, turn, 0)
                if "C1" in on_:
                    n = b["C1"]
                    pe.wait_ge(sems["C", "xl"], n + 1)
                    if isinstance(n, int) and n == 0:
                        pe.wait_ge(w_split, 8)
                    bank_free(pe, 1, 2, turn)
                    width = C + 2 * KV * D
                    for i, (x_, w) in enumerate(passes((xh["C"], xl["C"]), w_l1)):
                        for j in range(J):
                            ins = pe.matmul(G[:, 1, 0:width], x_[:, j, :], w[:, j, :], start=(i == 0 and j == 0),
                                            stop=(i == 2 and j == J - 1))
                    ins.then_inc(sems["C", "qkv"], 1)
                if "C2" in on_:
                    for k in range(2):
                        shifted("C", b["C2"], parity("C2", par), k, masked, turn, 1)
                if "M1" in on_:
                    n = b["M1"]
                    pe.wait_ge(sems["M", "xl"], n + 1)
                    if isinstance(n, int) and n == 0:
                        pe.wait_ge(w_split, 4)
                    bank_free(pe, 0, 2, turn)
                    bank_free(pe, 3, 2, turn)
                    for k in range(NH):
                        for i, (x_, w) in enumerate(passes((xh["M"], xl["M"]), w_fc1)):
                            for j in range(J):
                                ins = pe.matmul(G[:, 0 if k < 4 else 3, (k % 4) * 128:(k % 4 + 1) * 128],
                                                w[:, j, k * 128:(k + 1) * 128], x_[:, j, :],
                                                start=(i == 0 and j == 0), stop=(i == 2 and j == J - 1))
                    ins.then_inc(sems["M", "fc1"], 1)
                if "C3" in on_:
                    output("C", b["C3"], 2, 2, w_o1, turn)
                if "A2" in on_:
                    n = b["A2"]
                    for k in range(2):
                        pe.wait_ge(sems["A", f"e{k}"], n + 1)
                    pe.wait_ge(sems["A", "v"], n + 1)
                    bank_free(pe, 1, 3, turn)
                    for h in range(H):
                        t, j = h // 2, h % 4
                        ins = pe.matmul(G[32 * j:32 * j + 32, 1, (h // 4) * 128:(h // 4 + 1) * 128],
                                        V["A"][:, parity("A2", par), h, :],
                                        P["A"][:, t // 4, h % 2, (t % 4) * 128:(t % 4 + 1) * 128], start=True, stop=True)
                    ins.then_inc(sems["A", "pv"], 1)
                if "C2" in on_:
                    n = b["C2"]
                    for k in range(2):
                        pe.wait_ge(sems["C", f"e{k}"], n + 1)
                    pe.wait_ge(sems["C", "v"], n + 1)
                    bank_free(pe, 3, 3, turn)
                    for g in range(KV):
                        ins = pe.matmul(G[32 * g:32 * g + 32, 3, :], V["C"][:, parity("C2", par), g, :],
                                        P["C"][:, g // 2, g % 2, :], start=True, stop=True)
                    ins.then_inc(sems["C", "pv"], 1)
                if "A1" in on_:
                    n = b["A1"]
                    pe.wait_ge(sems["A", "lo"], 2 * (n + 1))
                    pe.wait_ge(sems["A", "dup"], 2 * (n + 1))
                    bank_free(pe, "S1", 2, turn)
                    for kq in range(2):
                        for t in range(8):
                            ins = pe.transpose(S[1][:, kq, t * 64:(t + 1) * 64].bitcast(F16),
                                               stkA[:, kq, 2 * t:2 * t + 2, :].rearrange("p h w -> p (h w)"), idh[:])
                    ins.then_inc(sems["A", "tr"], 1)
                if "C1" in on_:
                    n = b["C1"]
                    pe.wait_ge(sems["C", "lo"], 2 * (n + 1))
                    pe.wait_ge(sems["C", "dup"], 2 * (n + 1))
                    bank_free(pe, 0, 3, turn)
                    bank_free(pe, 1, 4, turn)
                    for t in range((H + KV) // 2):
                        ins = pe.transpose(G[:, t // 8, (t % 8) * 64:(t % 8 + 1) * 64].bitcast(F16),
                                           stkC[:, 2 * t:2 * t + 2, :].rearrange("p h w -> p (h w)"), idh[:])
                    ins.then_inc(sems["C", "tr"], 1)
                if "A2" in on_:
                    transpose_sums("A", b["A2"], 2, 3, turn)
                if "A1" in on_:
                    for k in range(2):
                        scores("A", b["A1"], parity("A1", par), k, masked, turn, 2 + k)
                if "C2" in on_:
                    transpose_sums("C", b["C2"], 3, 4, turn)
                if "C1" in on_:
                    for k in range(2):
                        scores("C", b["C1"], parity("C1", par), k, masked, turn, 3 + k)

            def transpose_sums(s, b, bank, nth, turn):
                pe.wait_ge(sems[s, "ou"], b + 1)
                bank_free(pe, bank, nth, turn)
                for t in range(4):
                    ins = pe.transpose(G[:, bank, t * 128:(t + 1) * 128], ou[s][:, t, :], idf[:])
                ins.then_inc(sems[s, "ut"], 1)

            flag = pe.value_load(msk_flag[0:1, 0:1].bitcast(I32))
            with pe.If(flag):
                turns(pe, lambda turn, par: turn_pe(turn, par, True))
            with pe.Else():
                turns(pe, lambda turn, par: turn_pe(turn, par, False))


KT = 8
ROOT_STEPS = 19
SM_MIN = 5
SILU = 8
QB_PARTS = 14
CONSTS = 17
ADA = 21
GAM_ROWS = 26
MASK_ROW = 31
MASK_FLAG = 32
L1_WEIGHTS = 34


def _tables():
    freqs = (np.float32(1.0) / np.power(np.float32(10000.0), np.arange(0, D, 2, dtype=np.float32) / np.float32(D))
             ).astype(np.float32)
    emb = np.arange(T, dtype=np.float32)[:, None] * freqs[None, :]
    cos = np.concatenate([np.cos(emb), np.cos(emb)], -1).astype(np.float32)
    sin = np.concatenate([-np.sin(emb), np.sin(emb)], -1).astype(np.float32)
    inv = np.float32(1.0 / np.sqrt(D))

    def full(t):
        return np.concatenate([np.tile(t * inv, (1, H)), np.tile(t, (1, KV))], 1).astype(np.float32)

    i = np.arange(T)
    hidden = (np.abs(i[None, :] - i[:, None]) > 32) & ~(i % 64 == 0)[None, :]
    return full(cos) / np.float32(WS), full(sin) / np.float32(WS), np.where(hidden, np.float32(NEG), np.float32(0.0)), np.eye(128, dtype=np.float32)


def kernel(**inputs):
    import concourse.bacc as bacc
    from concourse.bass_utils import run_bass_kernel_spmd

    a = {k: np.asarray(v) for k, v in inputs.items()}

    def chunks(w):
        return np.ascontiguousarray(w.T.reshape(-1, 128, w.shape[0]).transpose(1, 0, 2))

    def col(v):
        return np.ascontiguousarray(v.reshape(-1, 128).T)

    d = np.arange(D)
    q_order = np.concatenate([(4 * (2 * s + r) + i) * D + d for s in range(2) for i in range(4) for r in range(2)])
    o_order = np.concatenate([(4 * g + i) * D + d for i in range(4) for g in range(KV)])
    cos_t, sin_t, window, ident = _tables()
    data = {
        "x": a["x"],
        "cond_t": np.ascontiguousarray(a["cond_2048"].T.reshape(J, 128, NB).transpose(1, 0, 2)),
        "mask": a["mask_1x1xSxS_ff0"].reshape(T, T),
        "wqkv": chunks(a["L0_cond_Wqkv"]),
        "qbias": a["L0_cond_q_bias"].reshape(1, C),
        "vbias": col(a["L0_cond_v_bias"]),
        "sml": a["L0_cond_scale_mul_log"].reshape(1, H),
        "wproj": chunks(a["L0_cond_Wproj"]),
        "bproj": a["L0_cond_bproj"].reshape(1, C),
        "wada": chunks(a["L0_cond_Wada"]),
        "bada_row": np.ascontiguousarray(a["L0_cond_bada"][:2 * C]).reshape(1, 2 * C),
        "bada_col": col(a["L0_cond_bada"]),
        "wfc1": chunks(a["L0_cond_Wfc1"]),
        "bfc1": col(a["L0_cond_bfc1"]),
        "wfc2": chunks(a["L0_cond_Wfc2"]),
        "bfc2": a["L0_cond_bfc2"].reshape(1, C),
        "wada1": chunks(a["L1_cond_W_ada"]),
        "bada1": col(a["L1_cond_b_ada"]),
        "wq1": chunks(a["L1_cond_Wq"][q_order]),
        "wkd": a["L1_cond_Wkd"],
        "wkvu": np.ascontiguousarray(np.concatenate([a["L1_cond_Wku"], a["L1_cond_Wvu"]], 0).T),
        "wo1": chunks(a["L1_cond_Wo"][:, o_order]),
        "ident": ident, "cos_t": cos_t, "sin_t": sin_t, "window": window,
    }
    nc = bacc.Bacc("TRN2", target_bir_lowering=False, num_devices=1)
    arrays, args = {}, {}
    for name, v in data.items():
        v = np.ascontiguousarray(v)
        arrays[f"in_{name}"] = v
        args[name] = nc.dram_tensor(f"in_{name}", v.shape, mybir.dt.from_np(v.dtype), kind="ExternalInput").ap()
    args["out"] = nc.dram_tensor("out_0", (NB, T, C), F32, kind="ExternalOutput").ap()
    block_pair(nc, **args)
    r = run_bass_kernel_spmd(nc, [arrays], core_ids=[0])
    return r.results[0]["out_0"]
```

```python
from contextlib import ExitStack

import numpy as np
import concourse.bass as bass
from concourse import mybir

F32 = mybir.dt.float32
F16 = mybir.dt.float16
BF16 = mybir.dt.bfloat16
U32 = mybir.dt.uint32
I32 = mybir.dt.int32
ALU = mybir.AluOpType
ACT = mybir.ActivationFunctionType
AX = mybir.AxisListType

NB, T, C = 16, 128, 256
H, D = 16, 16
KV = 4
HID = 4 * C
LAT = 64
J = C // 128
NH = HID // 128
EPS0, EPS1 = 1e-6, 1e-5
NEG = -1e30
CSCALE = 64.0
GELU_A = 0.044715
GELU_C = float(np.sqrt(np.float32(2.0 / np.pi)))
WS = 64.0
OFF = {"A1": 0, "A2": 1, "A3": 2, "M1": 3, "M2": 4, "C1": 5, "C2": 6, "C3": 7}
LAST = NB + OFF["C3"]
PEEL = OFF["C3"] + 1
LOOP_END = PEEL + (NB - 1 - PEEL) // 2 * 2
RSQRT = 0x5F3759DF


def block_pair(nc, x, cond_t, mask, wqkv, qbias, vbias, sml, wproj, bproj, wada, bada_row, bada_col,
               wfc1, bfc1, wfc2, bfc2, wada1, bada1, wq1, wkd, wkvu, wo1, ident, cos_t, sin_t, window, out):
    ctx = ExitStack()
    with ctx:
        def sb(name, shape, dt=F32):
            return ctx.enter_context(nc.sbuf_tensor(name, shape, dt))

        def sem(name):
            return ctx.enter_context(nc.semaphore(name))

        S = [ctx.enter_context(nc.psum_tensor(f"scores{k}", [128, 2, 512], F32)) for k in range(2)]
        G = ctx.enter_context(nc.psum_tensor("general", [128, 4, 512], F32))

        raw_qkv = sb("raw_qkv", [128, J, 3 * C])
        raw_fc1 = sb("raw_fc1", [128, J, HID])
        raw_fc2 = sb("raw_fc2", [128, NH, C])
        raw_l1 = sb("raw_l1", [128, J, C + 2 * KV * D])
        w_qkv = [sb(f"w_qkv{n}", [128, J, 3 * C], F16) for n in "hl"]
        w_fc1 = [sb(f"w_fc1{n}", [128, J, HID], F16) for n in "hl"]
        w_fc2 = [sb(f"w_fc2{n}", [128, NH, C], F16) for n in "hl"]
        w_l1 = [sb(f"w_l1{n}", [128, J, C + 2 * KV * D], F16) for n in "hl"]
        w_proj = sb("w_proj", [128, J, C])
        w_o1 = sb("w_o1", [128, J, C])
        p_all = sb("p_all", [128, 2, 2 * 2 * 512])
        p_flat = p_all[:].rearrange("p a b -> p (a b)")
        w_ada = p_flat[:, 0:J * 6 * C].rearrange("p (j c) -> p j c", j=J)
        w_ada1 = p_flat[:, J * 6 * C:J * 8 * C].rearrange("p (j c) -> p j c", j=J)
        w_kd = sb("w_kd", [LAT, C])
        w_kvu = sb("w_kvu", [LAT, 2 * KV * D])
        b_fc1 = sb("b_fc1", [128, NH])
        b_ada_row = sb("b_ada_row", [NB, 2 * C])
        b_ada_col = sb("b_ada_col", [128, 12])
        b_ada1 = sb("b_ada1", [128, 4])
        b_proj = sb("b_proj", [NB, C])
        b_fc2 = sb("b_fc2", [NB, C])
        b_v = sb("b_v", [128, J])
        q_b = sb("q_b", [1, C])
        idf = sb("idf", [128, 128])
        idh = sb("idh", [128, 128], F16)
        idb = sb("idb", [128, 128], BF16)
        win = sb("win", [128, 128])
        winb = sb("winb", [128, 128], BF16)
        cos_s = sb("cos_s", [128, C + KV * D])
        sin_s = sb("sin_s", [128, C + KV * D])
        msk = sb("msk", [128, 128])
        msk_max = sb("msk_max", [128, 1])
        msk_rel = sb("msk_rel", [128, 128])
        msk_any = sb("msk_any", [128, 128])
        msk_row = sb("msk_row", [128, 1])
        msk_flag = sb("msk_flag", [1, 1])
        cond = sb("cond", [128, J, NB])
        cexp = sb("cexp", [128, J, NB])
        cden = sb("cden", [128, J, NB])
        crec = sb("crec", [128, J, NB])
        csil = sb("csil", [128, J, NB])
        ada = sb("ada", [128, 12, NB])
        gam = sb("gam", [NB, 4, C])
        bproj_v = sb("bproj_v", [NB, C])
        bv_wide = sb("bv_wide", [128, J, NB])
        sm_in = sb("sm_in", [128, H])
        sm_min = sb("sm_min", [128, H])
        sm = sb("sm", [128, H])
        qb_h = sb("qb_h", [1, 3, C], BF16)
        qb_r = sb("qb_r", [1, 3, C])
        qb3 = sb("qb3", [3, C], BF16)
        one3 = sb("one3", [3, 128], BF16)

        X = sb("x_res", [128, NB, C])
        gb = {s: sb(f"gb_{s}", [128, 2, 2, C]) for s in "AM"}
        st = sb("st", [128, 3, 6])
        msum = sb("msum", [128, 3])
        mdif = sb("mdif", [128, 3])
        msq = sb("msq", [128, 3])
        mean = sb("mean", [128, 3])
        eps = sb("eps", [128, 3])
        rin = sb("rin", [128, 3 + 2 * H])
        root = sb("root", [128, 3 + 2 * H])
        rtmp = sb("rtmp", [128, 3 + 2 * H])
        nmr = sb("nmr", [128, 3])
        xn = {s: sb(f"xn_{s}", [128, C]) for s in "AMC"}
        x32 = {s: sb(f"x32_{s}", [128, J, 128]) for s in "AMC"}
        xh = {s: sb(f"xh_{s}", [128, J, 128], F16) for s in "AMC"}
        xl = {s: sb(f"xl_{s}", [128, J, 128], F16) for s in "AMC"}
        sq = sb("sq", [128, 2 * C])
        qsc = sb("qsc", [128, 2 * H])
        tmpA = sb("tmpA", [128, 2 * C])
        stkA = sb("stkA", [128, 2, H, 64], F16)
        rot1 = sb("rot1", [128, C + KV * D])
        rot2 = sb("rot2", [128, C + KV * D])
        tmpC = sb("tmpC", [128, C + KV * D])
        stkC = sb("stkC", [128, H + KV, 64], F16)
        qk = {"A": sb("qk_A", [128, 2, 2 * H * 64], F16),
              "C": sb("qk_C", [128, 2, (H + KV) * 64], F16)}
        V = {"A": sb("v_A", [128, 2, H, 32]), "C": sb("v_C", [128, 2, KV, 32])}
        mx = {s: sb(f"mx_{s}", [128, H]) for s in "AC"}
        cmax = {s: sb(f"cmax_{s}", [128, 2, 2, 8], F16) for s in "AC"}
        cT = {s: sb(f"cT_{s}", [32, 128], F16) for s in "AC"}
        P = {s: p_all[:, n].rearrange("p (k r q) -> p k r q", k=2, r=2) for n, s in enumerate("AC")}
        ou = {s: sb(f"ou_{s}", [128, 4, 128]) for s in "AC"}
        rcp = {s: sb(f"rcp_{s}", [128, H]) for s in "AC"}
        on = {s: sb(f"on_{s}", [128, C]) for s in "AC"}
        oT = {s: sb(f"oT_{s}", [128, J, 128]) for s in "AC"}
        xg = {s: sb(f"xg_{s}", [128, C]) for s in "AM"}
        upd = {s: sb(f"upd_{s}", [128, C]) for s in "AM"}
        U = sb("u", [128, NH, 128])
        S2 = sb("s2", [128, NH, 128])
        Z = sb("z", [128, NH, 128])
        GH = sb("gh", [128, NH, 128], F16)
        GLo = sb("gl", [128, NH, 128], F16)

        scratch = nc.dram_tensor("gamma_rows", (NB, 4 * C), F32).ap()

        x_in = [sem("x_in0"), sem("x_in1")]
        w_in = {n: sem(f"in_{n}") for n in ("cond", "first", "ada1", "ada", "qkv", "consts", "mlp", "l1", "kv", "sm")}
        p_dve = sem("setup_dve")
        p_act = sem("setup_act")
        p_pool = sem("setup_pool")
        p_pe = sem("setup_pe")
        w_split = sem("weights_split")
        qb_in = sem("qbias_rows_in")
        gam_out = sem("gamma_rows_out")
        gb_in = {s: sem(f"gamma_in_{s}") for s in "AM"}
        attention = ("tr evq evk hi dup lo s0 s1 m0 m1 ch cl ct cev p0 p1 e0 e1 pv ou ut rcp on ot oe o res"
                     " xn xt x32 xh xl stats qkv v tmp ")
        sems = {}
        for stage, steps in (("A", attention + "sq n2 qsc xg upd"),
                             ("M", "stats xn xt x32 xh xl fc1a fc1b ua ub sqr z tanh gl gh glo fc2 xg upd res"),
                             ("C", attention + "r1 r2")):
            for n in steps.split():
                sems[stage, n] = sem(f"{stage}_{n}")
        roots_done = sem("roots")
        c_in = {s: sem(f"{s}_max_rows_in") for s in "AC"}
        y_out = sem("y_out")

        def wait(eng, s, n):
            if isinstance(n, int) and n <= 0:
                return
            eng.wait_ge(s, n)

        USES = {
            0: [("xt_A", {"A1": "x32"}), ("v", {"A1": "v"}), ("fc1b", {"M1": "ub"}),
                ("pv_C", {"C2": "ou"})],
            1: [("ot", {"A3": "oe", "C3": "oe"}), ("o_A", {"A3": "upd"}), ("fc1a", {"M1": "ua"}),
                ("qkv", {"C1": "tmp v"}), ("tr_k", {"C1": "evk"}), ("ut_C", {"C2": "on"})],
            2: [("fc2", {"M2": "upd"}), ("qk", {"A1": "tmp"}), ("pv_A", {"A2": "ou"}),
                ("ut_A", {"A2": "on"})],
            3: [("xt_MC", {"M1": "x32", "C1": "x32"}), ("ct", {"A2": "cev", "C2": "cev"}), ("o_C", {"C3": "res"}),
                ("tr_q", {"C1": "evq"})],
            "S0": [("p0_A", {"A2": "e0"}), ("p0_C", {"C2": "e0"}), ("s0_A", {"A1": "m0"}),
                   ("s0_C", {"C1": "m0"})],
            "S1": [("p1_A", {"A2": "e1"}), ("p1_C", {"C2": "e1"}), ("tr", {"A1": "evq"}),
                   ("s1_A", {"A1": "m1"}), ("s1_C", {"C1": "m1"})],
        }
        BANK = {use: bank for bank, uses in USES.items() for use, _ in uses}

        def bank_free(eng, use, turn):
            uses = USES[BANK[use]]
            nth = [name for name, _ in uses].index(use)
            for back in range(1, len(uses) + 1):
                k = nth - back
                t = turn if k >= 0 else turn - 1
                active = [(stage[0], steps, t - OFF[stage]) for stage, steps in uses[k][1].items() if stage in stages(t)]
                for s, steps, b in active:
                    for step in steps.split():
                        eng.wait_ge(sems[s, step], b + 1)
                if active:
                    return

        def stages(turn):
            return [s for s, k in OFF.items() if not isinstance(turn, int) or 0 <= turn - k < NB]

        def turns(eng, body, before_loop=None):
            for t in range(PEEL):
                body(t, t % 2)
            if before_loop:
                before_loop()
            with eng.Fori(PEEL, LOOP_END - 1, 2) as t:
                body(t, PEEL % 2)
                body(t + 1, (PEEL + 1) % 2)
            for t in range(LOOP_END, LAST):
                body(t, t % 2)

        def at(b):
            return bass.ds(b, 1) if not isinstance(b, int) else slice(b, b + 1)

        def xrow(b):
            return X[:, at(b), :].rearrange("p o c -> p (o c)")

        def heads16(ap):
            return ap.rearrange("p (h d) -> p h d", d=D)

        def tiles(stage, par, first, count):
            return qk[stage][:, par, first * 128:(first + count) * 128]

        def parity(stage, par):
            return (par + OFF[stage]) % 2

        block = ctx.enter_context(nc.Block())

        @block.sync
        def _(sp):
            sp.dma_start(cond[:], cond_t).then_inc(w_in["cond"], 16)
            sp.dma_start(X[:, 0:2, :], x[0:2].rearrange("b t c -> t b c")).then_inc(x_in[0], 16)
            for k in (2, 4):
                sp.dma_start(w_ada[:, :, k * C:(k + 1) * C], wada[:, :, k * C:(k + 1) * C]).then_inc(w_in["ada1"], 16)
            sp.dma_start(b_ada_col[:], bada_col).then_inc(w_in["ada1"], 16)
            sp.dma_start(w_ada[:, :, 0:2 * C], wada[:, :, 0:2 * C]).then_inc(w_in["ada"], 16)
            for k in (3, 5):
                sp.dma_start(w_ada[:, :, k * C:(k + 1) * C], wada[:, :, k * C:(k + 1) * C]).then_inc(w_in["ada"], 16)
            sp.dma_start(b_ada_row[:], bada_row.broadcast_to([NB, 2 * C])).then_inc(w_in["ada"], 16)
            sp.dma_start(w_ada1, wada1).then_inc(w_in["ada"], 16)
            sp.dma_start(b_ada1[:], bada1).then_inc(w_in["ada"], 16)
            sp.wait_ge(p_dve, QB_PARTS)
            sp.dma_start(qb3[:], qb_h[0:1, :, :]).then_inc(qb_in, 16)
            sp.dma_start(raw_fc1[:], wfc1).then_inc(w_in["mlp"], 16)
            sp.dma_start(raw_fc2[:], wfc2).then_inc(w_in["mlp"], 16)
            sp.dma_start(b_fc1[:], bfc1).then_inc(w_in["mlp"], 16)
            sp.dma_start(X[:, 2:NB, :], x[2:NB].rearrange("b t c -> t b c")).then_inc(x_in[1], 16)
            sp.wait_ge(p_dve, GAM_ROWS)
            sp.dma_start(scratch, gam[:].rearrange("b k c -> b (k c)")).then_inc(gam_out, 16)
            sp.wait_ge(gam_out, 16)

            def max_rows(stage, b, par):
                sp.wait_ge(sems[stage, "cev"], b + 1)
                for r in range(2):
                    dst = tiles(stage, par, 0, 8).rearrange("p (t q) -> p t q", q=128)
                    sp.dma_start(dst[64 * r + 48:64 * r + 50], cT[stage][16 * r:16 * r + 16, :]
                                 ).then_inc(c_in[stage], 16)

            def gammas(stage, b, par):
                if not isinstance(b, int):
                    sp.wait_ge(gam_out, 16)
                wait(sp, sems[stage, "upd"], b - 1)
                wait(sp, sems[stage, "xg"], b - 1)
                wait(sp, gb_in[stage], 16 * b)
                k = 0 if stage == "A" else 2 * C
                sp.dma_start(gb[stage][:, par].rearrange("p k c -> p (k c)"),
                             scratch[at(b), k:k + 2 * C].rearrange("o c -> (o c)").partition_broadcast(128)
                             ).then_inc(gb_in[stage], 16)

            def turn_sp(turn, par):
                on_ = stages(turn)
                if "A2" in on_:
                    gammas("A", turn - 1, (par + 1) % 2)
                if "M1" in on_:
                    gammas("M", turn - 3, (par + 1) % 2)
                if "A2" in on_:
                    max_rows("A", turn - OFF["A2"], parity("A2", par))
                if "C2" in on_:
                    max_rows("C", turn - OFF["C2"], parity("C2", par))
                if "C3" in on_:
                    b = turn - OFF["C3"]
                    sp.wait_ge(sems["C", "res"], b + 1)
                    sp.dma_start(out[at(b)].rearrange("o t c -> t (o c)"), X[:, at(b), :]
                                 ).then_inc(y_out, 16)

            turns(sp, turn_sp)
            sp.wait_ge(y_out, 16 * NB)

        @block.gpsimd
        def _(pool):
            pool.memset(stkA[:, :, :, 48:64], 0.0).then_inc(p_pool, 1)
            pool.memset(stkC[:, :, 48:64], 0.0).then_inc(p_pool, 1)
            pool.memset(V["A"][:], 1.0).then_inc(p_pool, 1)
            pool.memset(V["C"][:], 1.0).then_inc(p_pool, 1)
            pool.memset(one3[:], 1.0).then_inc(p_pool, 1)
            pool.wait_ge(p_pool, 5)
            pool.memset(stkA[:, 1, :, 48:50], CSCALE).then_inc(p_pool, 1)
            pool.memset(stkC[:, H:H + KV, 48:50], CSCALE).then_inc(p_pool, 1)

            def low(stage, b):
                pool.wait_ge(sems[stage, "xh"], b + 1)
                wait(pool, sems[stage, "fc1b" if stage == "M" else "qkv"], b)
                pool.tensor_tensor(xl[stage][:], x32[stage][:], xh[stage][:], ALU.subtract
                                   ).then_inc(sems[stage, "xl"], 1)

            def with_bias(stage, b, par):
                pool.wait_ge(p_pool, 7)
                pool.wait_ge(gb_in[stage], 16 * (b + 1))
                if stage == "M":
                    pool.wait_ge(sems["A", "res"], b + 1)
                wait(pool, sems[stage, "res"], b)
                pool.tensor_tensor(xg[stage][:], xrow(b), gb[stage][:, par, 1, :], ALU.add
                                   ).then_inc(sems[stage, "xg"], 1)

            def residual(stage, b):
                pool.wait_ge(p_pool, 7)
                pool.wait_ge(sems[stage, "upd"], b + 1)
                pool.wait_ge(sems[stage, "xg"], b + 1)
                pool.tensor_tensor(xrow(b), upd[stage][:], xg[stage][:], ALU.add).then_inc(sems[stage, "res"], 1)

            def low_parts_A(b, k):
                pool.wait_ge(sems["A", "hi"], b + 1)
                pool.tensor_tensor(stkA[:, k, :, 16 + 16 * k:32 + 16 * k],
                                   tmpA[:].rearrange("p (k h d) -> p k h d", k=2, d=D)[:, k], stkA[:, k, :, 0:16],
                                   ALU.subtract).then_inc(sems["A", "lo"], 1)

            def low_parts_C(b, k):
                hs = slice(0, H) if k == 0 else slice(H, H + KV)
                pool.wait_ge(sems["C", "hi"], b + 1)
                pool.tensor_tensor(stkC[:, hs, 16 + 16 * k:32 + 16 * k], heads16(tmpC[:])[:, hs], stkC[:, hs, 0:16],
                                   ALU.subtract).then_inc(sems["C", "lo"], 1)

            def low_gelu(b):
                pool.wait_ge(sems["M", "gh"], b + 1)
                wait(pool, sems["M", "fc2"], b)
                pool.tensor_tensor(GLo[:], Z[:], GH[:], ALU.subtract).then_inc(sems["M", "glo"], 1)

            def turn_pool(turn, par):
                on_ = stages(turn)
                b = {s: turn - OFF[s] for s in OFF}
                if "A1" in on_:
                    low("A", b["A1"])
                if "A3" in on_:
                    with_bias("A", b["A3"], parity("A3", par))
                if "M2" in on_:
                    with_bias("M", b["M2"], parity("M2", par))
                if "M1" in on_:
                    low("M", b["M1"])
                if "M2" in on_:
                    residual("M", b["M2"])
                if "A3" in on_:
                    residual("A", b["A3"])
                if "C1" in on_:
                    low("C", b["C1"])
                if "A1" in on_:
                    low_parts_A(b["A1"], 0)
                    low_parts_A(b["A1"], 1)
                if "C1" in on_:
                    low_parts_C(b["C1"], 0)
                    low_parts_C(b["C1"], 1)
                if "M1" in on_:
                    low_gelu(b["M1"])
            turns(pool, turn_pool)

        @block.scalar
        def _(act):
            act.dma_start(idf[:], ident).then_inc(w_in["first"], 16)
            act.dma_start(q_b[:], qbias).then_inc(w_in["first"], 16)
            act.dma_start(msk[:], mask).then_inc(w_in["first"], 16)
            act.dma_start(sm_in[:], sml.broadcast_to([128, H])).then_inc(w_in["sm"], 16)
            act.dma_start(raw_qkv[:], wqkv).then_inc(w_in["qkv"], 16)
            act.wait_ge(w_in["cond"], 16)
            act.activation(cexp[:], cond[:], ACT.Exp, scale=-1.0).then_inc(p_act, 1)
            act.dma_start(b_v[:], vbias).then_inc(w_in["consts"], 16)
            act.dma_start(b_proj[:], bproj.broadcast_to([NB, C])).then_inc(w_in["consts"], 16)
            act.dma_start(b_fc2[:], bfc2.broadcast_to([NB, C])).then_inc(w_in["consts"], 16)
            act.dma_start(w_proj[:], wproj).then_inc(w_in["consts"], 16)
            act.dma_start(w_kd[:], wkd).then_inc(w_in["kv"], 16)
            act.dma_start(w_kvu[:], wkvu).then_inc(w_in["kv"], 16)
            act.dma_start(raw_l1[:, :, 0:C], wq1).then_inc(w_in["l1"], 16)
            act.dma_start(w_o1[:], wo1).then_inc(w_in["l1"], 16)
            act.dma_start(cos_s[:], cos_t).then_inc(w_in["l1"], 16)
            act.dma_start(sin_s[:], sin_t).then_inc(w_in["l1"], 16)
            act.dma_start(win[:], window).then_inc(w_in["l1"], 16)
            act.wait_ge(p_dve, SM_MIN)
            act.activation(sm[:], sm_min[:], ACT.Exp).then_inc(p_act, 1)

            def normalize(stage, b):
                k = "AMC".index(stage)
                wait(act, sems[stage, "xt"], b)
                act.activation(xn[stage][:], xrow(b), ACT.Identity, bias=nmr[:, k:k + 1], scale=root[:, k:k + 1]
                               ).then_inc(sems[stage, "xn"], 1)

            def modulate(stage, b, bank, col, scale0, shift0, other=None):
                act.wait_ge(sems[stage, "xt"], b + 1)
                if other is not None:
                    act.wait_ge(sems["C" if stage == "M" else "M", "xt"], other + 1)
                wait(act, sems[stage, "xl"], b)
                for j in range(J):
                    ins = act.activation(x32[stage][:, j, :], G[:, bank, col + j * 128:col + (j + 1) * 128],
                                         ACT.Identity, bias=ada[:, shift0 + j, at(b)], scale=ada[:, scale0 + j, at(b)])
                ins.then_inc(sems[stage, "x32"], 1)

            def high(stage, b):
                act.wait_ge(sems[stage, "x32"], b + 1)
                wait(act, sems[stage, "fc1b" if stage == "M" else "qkv"], b)
                act.copy(xh[stage][:], x32[stage][:]).then_inc(sems[stage, "xh"], 1)

            def outputs(stage, b, both):
                if both:
                    act.wait_ge(sems["C", "ot"], both["C3"] + 1)
                    act.wait_ge(sems["A", "ot"], both["A3"] + 1)
                else:
                    act.wait_ge(sems[stage, "ot"], b + 1)
                wait(act, sems[stage, "o"], b)
                col = 0 if stage == "A" else C
                act.copy(oT[stage][:].rearrange("p j q -> p (j q)"), G[:, BANK["ot"], col:col + C]
                         ).then_inc(sems[stage, "oe"], 1)

            def max_rows(stage, b, both):
                if both:
                    act.wait_ge(sems["C", "ct"], both["C2"] + 1)
                    act.wait_ge(sems["A", "ct"], both["A2"] + 1)
                else:
                    act.wait_ge(sems[stage, "ct"], b + 1)
                wait(act, c_in[stage], 32 * b)
                col = 0 if stage == "A" else 64
                act.copy(cT[stage][:], G[0:32, BANK["ct"], col:col + 64].bitcast(F16)).then_inc(sems[stage, "cev"], 1)

            def squares(b):
                act.wait_ge(sems["A", "qkv"], b + 1)
                wait(act, sems["A", "n2"], b)
                act.activation(sq[:], G[:, BANK["qk"], :], ACT.Square).then_inc(sems["A", "sq"], 1)

            def values_A(b, par):
                act.wait_ge(sems["A", "qkv"], b + 1)
                if isinstance(b, int) and b == 0:
                    act.wait_ge(p_pool, 7)
                wait(act, sems["A", "pv"], b - 1)
                act.activation(V["A"][:, par, :, 0:D], heads16(G[:, BANK["v"], 0:C]), ACT.Identity,
                               scale=1.0 / WS).then_inc(sems["A", "v"], 1)

            def exp_slot(stage, b, k):
                act.wait_ge(sems[stage, f"p{k}"], b + 1)
                wait(act, sems[stage, "pv"], b)
                act.activation(P[stage][:, k], S[k][:], ACT.Exp).then_inc(sems[stage, f"e{k}"], 1)

            def high_parts_A(b):
                act.wait_ge(sems["A", "tmp"], b + 1)
                wait(act, sems["A", "tr"], b)
                act.copy(stkA[:, :, :, 0:16].rearrange("p k h w -> p (k h) w"), heads16(tmpA[:])
                         ).then_inc(sems["A", "hi"], 1)

            def high_parts_C(b):
                act.wait_ge(sems["C", "tmp"], b + 1)
                wait(act, sems["C", "tr"], b)
                act.copy(stkC[:, :, 0:16], heads16(tmpC[:])).then_inc(sems["C", "hi"], 1)

            def fc1_bias(b, half):
                ab = "ab"[half]
                act.wait_ge(sems["M", "fc1" + ab], b + 1)
                wait(act, sems["M", "gl"], b)
                for k in range(4 * half, 4 * half + 4):
                    ins = act.activation(U[:, k, :], G[:, BANK["fc1" + ab], (k % 4) * 128:(k % 4 + 1) * 128],
                                         ACT.Identity, bias=b_fc1[:, k:k + 1], scale=1.0 / WS)
                ins.then_inc(sems["M", "u" + ab], 1)

            def gelu_square(b):
                act.wait_ge(sems["M", "ua"], b + 1)
                act.wait_ge(sems["M", "ub"], b + 1)
                act.activation(S2[:], U[:], ACT.Square, scale=float(np.sqrt(GELU_A))).then_inc(sems["M", "sqr"], 1)

            def gelu_tanh(b):
                act.wait_ge(sems["M", "z"], b + 1)
                act.activation(S2[:], Z[:], ACT.Tanh, scale=GELU_C).then_inc(sems["M", "tanh"], 1)

            def gelu_high(b):
                act.wait_ge(sems["M", "gl"], b + 1)
                wait(act, sems["M", "fc2"], b)
                act.copy(GH[:], Z[:]).then_inc(sems["M", "gh"], 1)

            def sums(stage, b):
                act.wait_ge(sems[stage, "pv"], b + 1)
                wait(act, sems[stage, "ut"], b)
                act.copy(ou[stage][:].rearrange("p a q -> p (a q)"), G[:, BANK["pv_" + stage], :]
                         ).then_inc(sems[stage, "ou"], 1)

            def evacuate_A(b, par):
                act.wait_ge(sems["A", "tr"], b + 1)
                wait(act, sems["A", "p0"], b - 1)
                wait(act, sems["A", "p1"], b - 1)
                act.copy(qk["A"][:, par, :].bitcast(U32), S[1][:].rearrange("p a b -> p (a b)").bitcast(U32)
                         ).then_inc(sems["A", "evq"], 1)

            def evacuate_C(b, par, what):
                act.wait_ge(sems["C", "tr"], b + 1)
                wait(act, sems["C", "p0"], b - 1)
                wait(act, sems["C", "p1"], b - 1)
                dst = qk["C"][:, par, :].bitcast(U32)
                if what == "q":
                    act.copy(dst[:, 0:H * 32], G[:, BANK["tr_q"], :].bitcast(U32)).then_inc(sems["C", "evq"], 1)
                else:
                    act.copy(dst[:, H * 32:], G[:, BANK["tr_k"], 0:KV * 32].bitcast(U32)).then_inc(sems["C", "evk"], 1)

            def turn_act(turn, par):
                on_ = stages(turn)
                nxt = stages(turn + 1)
                b = {s: turn - OFF[s] for s in OFF}
                both_ot = b if "A3" in on_ and "C3" in on_ else None
                both_ct = b if "A2" in on_ and "C2" in on_ else None

                def layer_norm(s, stage):
                    if stage in nxt:
                        act.wait_ge(roots_done, ROOT_STEPS * (turn + 2))
                        normalize(s, turn + 1 - OFF[stage])

                if "A1" in on_:
                    modulate("A", b["A1"], BANK["xt_A"], 0, 0, 4)
                    high("A", b["A1"])
                if "C3" in on_:
                    outputs("C", b["C3"], both_ot)
                if "M1" in on_:
                    modulate("M", b["M1"], BANK["xt_MC"], 0, 2, 6, b["C1"] if "C1" in on_ else None)
                if "C1" in on_:
                    modulate("C", b["C1"], BANK["xt_MC"], C, 8, 10, b["M1"] if "M1" in on_ else None)
                if "A3" in on_:
                    outputs("A", b["A3"], both_ot)
                if "A2" in on_:
                    max_rows("A", b["A2"], both_ct)
                if "C1" in on_:
                    high("C", b["C1"])
                if "M1" in on_:
                    high("M", b["M1"])
                if "A1" in on_:
                    squares(b["A1"])
                if "C2" in on_:
                    max_rows("C", b["C2"], both_ct)
                if "A1" in on_:
                    values_A(b["A1"], parity("A1", par))
                if "M1" in on_:
                    fc1_bias(b["M1"], 0)
                if "A2" in on_:
                    exp_slot("A", b["A2"], 1)
                if "M1" in on_:
                    fc1_bias(b["M1"], 1)
                if "A2" in on_:
                    exp_slot("A", b["A2"], 0)
                if "M1" in on_:
                    gelu_square(b["M1"])
                if "A1" in on_:
                    high_parts_A(b["A1"])
                if "C2" in on_:
                    exp_slot("C", b["C2"], 1)
                    exp_slot("C", b["C2"], 0)
                if "C1" in on_:
                    high_parts_C(b["C1"])
                if "M1" in on_:
                    gelu_tanh(b["M1"])
                if "A1" in on_:
                    evacuate_A(b["A1"], parity("A1", par))
                if "A2" in on_:
                    sums("A", b["A2"])
                if "C2" in on_:
                    sums("C", b["C2"])
                if "C1" in on_:
                    evacuate_C(b["C1"], parity("C1", par), "k")
                    evacuate_C(b["C1"], parity("C1", par), "q")
                if "M1" in on_:
                    gelu_high(b["M1"])
                layer_norm("M", "M1")
                layer_norm("A", "A1")
                layer_norm("C", "C1")

            act.wait_ge(roots_done, ROOT_STEPS)
            normalize("A", 0)
            act.wait_ge(p_dve, ADA1)
            turns(act, turn_act)

        @block.vector
        def _(dve):
            done = [0]

            def setup(ins, now=True):
                done[0] += 1
                ins.then_inc(p_dve, 1)
                if now:
                    dve.wait_ge(p_dve, done[0])

            def split(parts, raw, scale, nth):
                dve.tensor_scalar(parts[0][:], raw, scale, None, ALU.mult).then_inc(w_split, 1)
                dve.wait_ge(w_split, 2 * nth + 1)
                dve.scalar_tensor_tensor(parts[1][:], raw, scale, parts[0][:], ALU.mult, ALU.subtract
                                         ).then_inc(w_split, 1)

            setup(dve.memset(eps[:, 0:2], EPS0), now=False)
            setup(dve.memset(eps[:, 2:3], EPS1), now=False)
            setup(dve.memset(rin[:], 1.0), now=False)
            setup(dve.memset(st[:], 1.0))
            dve.wait_ge(w_in["sm"], 16)
            setup(dve.tensor_scalar(sm_min[:], sm_in[:], float(np.log(np.float32(100.0))), None, ALU.min))
            assert done[0] == SM_MIN
            dve.wait_ge(p_act, 1)
            setup(dve.tensor_scalar(cden[:], cexp[:], 1.0, None, ALU.add))
            setup(dve.reciprocal(crec[:], cden[:]))
            setup(dve.tensor_tensor(csil[:], cond[:], crec[:], ALU.mult))
            assert done[0] == SILU
            dve.wait_ge(w_in["first"], 48)
            setup(dve.tensor_scalar(msk[:], msk[:], NEG, None, ALU.max))
            setup(dve.tensor_reduce(msk_max[:], msk[:], AX.X, ALU.max))
            setup(dve.tensor_scalar(msk_rel[:], msk[:], msk_max[:], None, ALU.subtract))
            setup(dve.tensor_scalar(msk_any[:], msk_rel[:], 0.0, None, ALU.is_lt))
            setup(dve.tensor_reduce(msk_row[:], msk_any[:], AX.X, ALU.max))
            assert done[0] == MASK_ROW
            setup(dve.tensor_scalar(qb_r[:, 0, :], q_b[:], WS, None, ALU.mult))
            setup(dve.tensor_copy(qb_h[:, 0, :], qb_r[:, 0, :]))
            setup(dve.tensor_tensor(qb_r[:, 1, :], qb_r[:, 0, :], qb_h[:, 0, :], ALU.subtract))
            setup(dve.tensor_copy(qb_h[:, 1, :], qb_r[:, 1, :]))
            setup(dve.tensor_tensor(qb_r[:, 2, :], qb_r[:, 1, :], qb_h[:, 1, :], ALU.subtract))
            setup(dve.tensor_copy(qb_h[:, 2, :], qb_r[:, 2, :]))
            assert done[0] == QB_PARTS
            dve.wait_ge(p_pe, 1)
            setup(dve.tensor_reduce(msk_flag[:], G[0:1, 3, 0:128], AX.X, ALU.max))
            setup(dve.tensor_copy(idh[:], idf[:]), now=False)
            setup(dve.tensor_copy(idb[:], idf[:]))
            assert done[0] == CONSTS

            def statistics(stage, turn):
                if stage not in stages(turn):
                    return
                s, b = stage[0], turn - OFF[stage]
                dve.wait_ge(x_in[0], 16)
                if stage != "A1":
                    dve.wait_ge(sems["A" if s == "M" else "M", "res"], b + 1)
                dve.bn_stats(st[:, "AMC".index(s), :], xrow(b)).then_inc(sems[s, "stats"], 1)

            def norm_sums(b):
                dve.wait_ge(sems["A", "sq"], b + 1)
                wait(dve, roots_done, ROOT_STEPS * (b + 1))
                dve.tensor_reduce(rin[:, 3:], heads16(sq[:]), AX.X, ALU.add).then_inc(sems["A", "n2"], 1)

            def rooting(turn):
                return any(s in stages(turn + 1) for s in ("A1", "M1", "C1")) or "A1" in stages(turn)

            def root_step(turn, n, ins):
                ins.then_inc(roots_done, 1)
                return ROOT_STEPS * (turn + 1) + n

            def variances(turn):
                if not rooting(turn):
                    return
                for k, stage in enumerate(("A1", "M1", "C1")):
                    if stage in stages(turn + 1):
                        dve.wait_ge(sems[stage[0], "stats"], turn + 2 - OFF[stage])
                wait(dve, roots_done, ROOT_STEPS * (turn + 1))
                even, odd, even2, odd2 = (st[:, :, n_] for n_ in (1, 4, 2, 5))
                root_step(turn, 1, dve.tensor_tensor(msum[:], even, odd, ALU.add))
                root_step(turn, 2, dve.tensor_tensor(mdif[:], even, odd, ALU.subtract))
                ready = root_step(turn, 3, dve.tensor_tensor(msq[:], even2, odd2, ALU.add))
                dve.wait_ge(roots_done, ready)
                root_step(turn, 4, dve.tensor_scalar(mean[:], msum[:], 0.5, None, ALU.mult))
                root_step(turn, 5, dve.scalar_tensor_tensor(msq[:], msq[:], 1.0 / C, eps[:], ALU.mult, ALU.add))
                if "A1" in stages(turn):
                    dve.wait_ge(sems["A", "n2"], turn + 1)
                root_step(turn, 6, dve.tensor_scalar(rin[:, 3:], rin[:, 3:], 1e-24 * WS * WS, None, ALU.max))
                ready = root_step(turn, 7, dve.tensor_tensor(mdif[:], mdif[:], mdif[:], ALU.mult))
                dve.wait_ge(roots_done, ready)
                ready = root_step(turn, 8, dve.scalar_tensor_tensor(rin[:, 0:3], mdif[:], 0.25, msq[:], ALU.mult, ALU.add))
                dve.wait_ge(roots_done, ready)
                for stage in ("A1", "M1", "C1"):
                    if stage in stages(turn):
                        dve.wait_ge(sems[stage[0], "xn"], turn + 1 - OFF[stage])
                root_step(turn, 9, dve.tensor_scalar(root[:].bitcast(I32), rin[:].bitcast(I32), -0.5, float(RSQRT),
                                                     ALU.mult, ALU.add))

            def newton(turn, first, last):
                if not rooting(turn):
                    return
                for k in range(first, last + 1):
                    dve.wait_ge(roots_done, ROOT_STEPS * (turn + 1) + 9 + k)
                    if k % 3 == 0:
                        ins = dve.tensor_tensor(rtmp[:], root[:], root[:], ALU.mult)
                    elif k % 3 == 1:
                        ins = dve.scalar_tensor_tensor(rtmp[:], rin[:], -0.5, rtmp[:], ALU.mult, ALU.mult)
                    else:
                        ins = dve.scalar_tensor_tensor(root[:], rtmp[:], 1.5, root[:], ALU.add, ALU.mult)
                    root_step(turn, 10 + k, ins)
                if last == 8:
                    dve.wait_ge(roots_done, ROOT_STEPS * (turn + 1) + 18)
                    root_step(turn, 19, dve.scalar_tensor_tensor(nmr[:], mean[:], -1.0, root[:, 0:3], ALU.mult, ALU.mult))

            dve.wait_ge(x_in[0], 16)
            statistics("A1", 0)
            variances(-1)
            newton(-1, 0, 8)
            ada_ps = G[:, 1, 0:12 * NB].rearrange("p (k b) -> p k b", b=NB)
            dve.wait_ge(p_pe, 2)
            for k in (0, 4):
                setup(dve.tensor_tensor(ada[:, k:k + 2, :], ada_ps[:, k:k + 2],
                                        b_ada_col[:, 4 + k:6 + k].unsqueeze(2).broadcast_to([128, 2, NB]), ALU.add))
            setup(dve.tensor_scalar(ada[:, 0:2, :], ada[:, 0:2, :], 1.0, None, ALU.add))
            assert done[0] == ADA1
            dve.wait_ge(w_in["qkv"], 16)
            split(w_qkv, raw_qkv[:], WS, 0)
            dve.wait_ge(w_in["consts"], 64)
            setup(dve.tensor_copy(bv_wide[:], b_v[:].unsqueeze(2).broadcast_to([128, J, NB])))
            assert done[0] == BV_WIDE

            def later_setup(turn):
                if turn == 0:
                    late = S[0][:, 0, 0:12 * NB].rearrange("p (k b) -> p k b", b=NB)
                    dve.wait_ge(p_pe, 4)
                    for k in (2, 6):
                        setup(dve.tensor_tensor(ada[:, k:k + 2, :], late[:, k:k + 2],
                                                b_ada_col[:, 4 + k:6 + k].unsqueeze(2).broadcast_to([128, 2, NB]),
                                                ALU.add), now=False)
                    setup(dve.tensor_tensor(ada[:, 8:12, :], late[:, 8:12],
                                            b_ada1[:].unsqueeze(2).broadcast_to([128, 4, NB]), ALU.add))
                    setup(dve.tensor_scalar(ada[:, 2:4, :], ada[:, 2:4, :], 1.0, None, ALU.add), now=False)
                    setup(dve.tensor_scalar(ada[:, 8:10, :], ada[:, 8:10, :], 1.0, None, ALU.add), now=False)
                    setup(dve.tensor_copy(raw_l1[:, :, C:], S[0][:, 0, 12 * NB:12 * NB + J * 128].rearrange(
                        "p (j k) -> p j k", j=J)), now=False)
                    dve.wait_ge(p_pe, 6)
                    setup(dve.tensor_tensor(bproj_v[:], S[0][0:NB, 1, 0:C], b_proj[:], ALU.add))
                    assert done[0] == SLOT_READ
                    for k in range(2):
                        setup(dve.tensor_tensor(gam[:, 2 * k, :], G[0:NB, 1, k * C:(k + 1) * C],
                                                b_ada_row[:, k * C:(k + 1) * C], ALU.add))
                    setup(dve.tensor_tensor(gam[:, 1, :], gam[:, 0, :], bproj_v[:], ALU.mult), now=False)
                    setup(dve.tensor_tensor(gam[:, 3, :], gam[:, 2, :], b_fc2[:], ALU.mult))
                    assert done[0] == GAM_ROWS
                if turn == 1:
                    dve.wait_ge(w_in["mlp"], 48)
                    split(w_fc1, raw_fc1[:], WS, 1)
                if turn == 2:
                    split(w_fc2, raw_fc2[:], 0.5 * WS, 2)
                if turn == 3:
                    dve.wait_ge(w_in["l1"], 80)
                    setup(dve.tensor_copy(winb[:], win[:]))
                    split(w_l1, raw_l1[:], WS, 3)

            def head_scales(b):
                dve.wait_ge(roots_done, ROOT_STEPS * (b + 2))
                wait(dve, sems["A", "tmp"], b)
                if isinstance(b, int) and b == 0:
                    dve.wait_ge(p_act, 2)
                dve.tensor_tensor(qsc[:, 0:H], root[:, 3:3 + H], sm[:], ALU.mult).then_inc(sems["A", "qsc"], 1)
                dve.tensor_copy(qsc[:, H:], root[:, 3 + H:]).then_inc(sems["A", "qsc"], 1)

            def unit_vectors(b):
                dve.wait_ge(sems["A", "qsc"], 2 * (b + 1))
                wait(dve, sems["A", "lo"], 2 * b)
                dve.tensor_tensor(heads16(tmpA[:]), heads16(G[:, BANK["qk"], :]),
                                  qsc[:].unsqueeze(2).broadcast_to([128, 2 * H, D]), ALU.mult
                                  ).then_inc(sems["A", "tmp"], 1)

            def dup_A(b):
                dve.wait_ge(sems["A", "hi"], b + 1)
                dve.tensor_copy(stkA[:, 0, :, 32:48], stkA[:, 0, :, 0:16]).then_inc(sems["A", "dup"], 1)
                dve.tensor_copy(stkA[:, 1, :, 16:32], stkA[:, 1, :, 0:16]).then_inc(sems["A", "dup"], 1)

            width = C + KV * D
            sn = sin_s[:].rearrange("p (h two e) -> p h two e", two=2, e=D // 2)
            r2 = rot2[:].rearrange("p (h two e) -> p h two e", two=2, e=D // 2)

            def values_C(b, par):
                dve.wait_ge(sems["C", "qkv"], b + 1)
                wait(dve, sems["C", "pv"], b - 1)
                dve.tensor_scalar(V["C"][:, par, :, 0:D], heads16(G[:, BANK["qkv"], width:width + KV * D]), 1.0 / WS,
                                  None, ALU.mult).then_inc(sems["C", "v"], 1)

            def rotate_cos(b):
                dve.wait_ge(sems["C", "qkv"], b + 1)
                wait(dve, sems["C", "tmp"], b)
                dve.tensor_tensor(rot1[:], G[:, BANK["qkv"], 0:width], cos_s[:], ALU.mult).then_inc(sems["C", "r1"], 1)

            def rotate_sin(b):
                dve.wait_ge(sems["C", "qkv"], b + 1)
                wait(dve, sems["C", "tmp"], b)
                ps = G[:, BANK["qkv"], 0:width].rearrange("p (h two e) -> p h two e", two=2, e=D // 2)
                for half in range(2):
                    dve.tensor_tensor(r2[:, :, half, :], ps[:, :, 1 - half, :], sn[:, :, half, :], ALU.mult
                                      ).then_inc(sems["C", "r2"], 1)

            def rotated(b):
                dve.wait_ge(sems["C", "r1"], b + 1)
                dve.wait_ge(sems["C", "r2"], 2 * (b + 1))
                wait(dve, sems["C", "lo"], 2 * b)
                dve.tensor_tensor(tmpC[:], rot1[:], rot2[:], ALU.add).then_inc(sems["C", "tmp"], 1)

            def dup_C(b):
                dve.wait_ge(sems["C", "hi"], b + 1)
                dve.tensor_copy(stkC[:, 0:H, 32:48], stkC[:, 0:H, 0:16]).then_inc(sems["C", "dup"], 1)
                dve.tensor_copy(stkC[:, H:, 16:32], stkC[:, H:, 0:16]).then_inc(sems["C", "dup"], 1)

            def maxima(stage, b, k):
                dve.wait_ge(sems[stage, f"s{k}"], b + 1)
                wait(dve, sems[stage, "cl"], b)
                m3 = mx[stage][:].rearrange("p (r t) -> p r t", r=2)
                dve.tensor_reduce(m3[:, :, 4 * k:4 * k + 4], S[k][:].rearrange("p r (t q) -> p r t q", q=128), AX.X,
                                  ALU.max).then_inc(sems[stage, f"m{k}"], 1)

            def shift_high(stage, b):
                for k in range(2):
                    dve.wait_ge(sems[stage, f"m{k}"], b + 1)
                wait(dve, sems[stage, "ct"], b)
                dve.tensor_scalar(cmax[stage][:, :, 0, :], mx[stage][:].rearrange("p (r t) -> p r t", r=2), -1.0 / CSCALE,
                                  None, ALU.mult).then_inc(sems[stage, "ch"], 1)

            def shift_low(stage, b):
                dve.wait_ge(sems[stage, "ch"], b + 1)
                dve.scalar_tensor_tensor(cmax[stage][:, :, 1, :], mx[stage][:].rearrange("p (r t) -> p r t", r=2),
                                         -1.0 / CSCALE, cmax[stage][:, :, 0, :], ALU.mult, ALU.subtract
                                         ).then_inc(sems[stage, "cl"], 1)

            def sum_reciprocal(stage, b):
                dve.wait_ge(sems[stage, "ut"], b + 1)
                wait(dve, sems[stage, "on"], b)
                v = G[:, BANK["ut_" + stage], :].rearrange("p (h w) -> p h w", w=32)
                dve.reciprocal(rcp[stage][:], v[:, :, D]).then_inc(sems[stage, "rcp"], 1)

            def over_sums(stage, b):
                v = G[:, BANK["ut_" + stage], :].rearrange("p (h w) -> p h w", w=32)
                dve.wait_ge(sems[stage, "rcp"], b + 1)
                wait(dve, sems[stage, "ot"], b)
                dve.tensor_tensor(heads16(on[stage][:]), v[:, :, 0:D], rcp[stage][:].unsqueeze(2).broadcast_to([128, H, D]),
                                  ALU.mult).then_inc(sems[stage, "on"], 1)

            def add_attention(b):
                dve.wait_ge(sems["C", "o"], b + 1)
                dve.tensor_tensor(xrow(b), G[:, BANK["o_C"], 0:C], xrow(b), ALU.add).then_inc(sems["C", "res"], 1)

            def gelu_cubic(b):
                dve.wait_ge(sems["M", "sqr"], b + 1)
                wait(dve, sems["M", "glo"], b)
                dve.scalar_tensor_tensor(Z[:], S2[:], 1.0, U[:], ALU.add, ALU.mult).then_inc(sems["M", "z"], 1)

            def gelu_gate(b):
                dve.wait_ge(sems["M", "tanh"], b + 1)
                dve.scalar_tensor_tensor(Z[:], S2[:], 1.0, U[:], ALU.add, ALU.mult).then_inc(sems["M", "gl"], 1)

            def gated(stage, b, use, done_step, scale, par):
                dve.wait_ge(sems[stage, done_step], b + 1)
                dve.wait_ge(gb_in[stage], 16 * (b + 1))
                wait(dve, sems[stage, "res"], b)
                dve.scalar_tensor_tensor(upd[stage][:], G[:, BANK[use], 0:C], scale, gb[stage][:, par, 0, :],
                                         ALU.mult, ALU.mult).then_inc(sems[stage, "upd"], 1)

            def turn_dve(turn, par):
                on_ = stages(turn)
                b = {s: turn - OFF[s] for s in OFF}
                if isinstance(turn, int) and turn == 1:
                    dve.wait_ge(x_in[1], 16)
                if "M2" in on_:
                    gated("M", b["M2"], "fc2", "fc2", 1.0 / WS, parity("M2", par))
                statistics("A1", turn + 1)
                if "A3" in on_:
                    gated("A", b["A3"], "o_A", "o", 1.0, parity("A3", par))
                statistics("C1", turn + 1)
                statistics("M1", turn + 1)
                if "A1" in on_:
                    norm_sums(b["A1"])
                variances(turn)
                newton(turn, 0, 8)
                if "A1" in on_:
                    head_scales(b["A1"])
                    unit_vectors(b["A1"])
                if "C1" in on_:
                    rotate_sin(b["C1"])
                    rotate_cos(b["C1"])
                if "A1" in on_:
                    dup_A(b["A1"])
                if isinstance(turn, int):
                    later_setup(turn)
                if "C1" in on_:
                    rotated(b["C1"])
                if "M1" in on_:
                    gelu_cubic(b["M1"])
                if "C1" in on_:
                    values_C(b["C1"], parity("C1", par))
                    dup_C(b["C1"])
                if "C3" in on_:
                    add_attention(b["C3"])
                if "M1" in on_:
                    gelu_gate(b["M1"])
                if "A1" in on_:
                    maxima("A", b["A1"], 0)
                    maxima("A", b["A1"], 1)
                if "C2" in on_:
                    sum_reciprocal("C", b["C2"])
                    over_sums("C", b["C2"])
                if "A2" in on_:
                    sum_reciprocal("A", b["A2"])
                    over_sums("A", b["A2"])
                if "C1" in on_:
                    maxima("C", b["C1"], 0)
                    maxima("C", b["C1"], 1)
                    shift_high("C", b["C1"])
                if "A1" in on_:
                    shift_high("A", b["A1"])
                if "C1" in on_:
                    shift_low("C", b["C1"])
                if "A1" in on_:
                    shift_low("A", b["A1"])

            turns(dve, turn_dve)

        @block.tensor
        def _(pe):
            pe.wait_ge(w_in["first"], 48)
            pe.wait_ge(p_dve, MASK_ROW)
            pe.transpose(G[0:1, 3, 0:128], msk_row[:], idf[:]).then_inc(p_pe, 1)

            def scales_shifts(dst, ks):
                for k in ks:
                    src, w, col = (csil, w_ada, 2 * C + k * 128) if k < 8 else (cond, w_ada1, (k - 8) * 128)
                    for j in range(J):
                        ins = pe.matmul(dst[:, k * NB:(k + 1) * NB], w[:, j, col:col + 128], src[:, j, :],
                                        start=(j == 0), stop=(j == J - 1))
                return ins

            pe.wait_ge(p_dve, SILU)
            pe.wait_ge(w_in["ada1"], 48)
            scales_shifts(G[:, 1, :], (0, 1, 4, 5)).then_inc(p_pe, 1)
            pe.wait_ge(qb_in, 16)
            pe.wait_ge(p_pool, 7)
            pe.wait_ge(p_dve, CONSTS)

            def later_products():
                pe.wait_ge(w_in["ada"], 96)
                scales_shifts(S[0][:, 0, :], (2, 3, 6, 7, 8, 9, 10, 11)).then_inc(p_pe, 1)
                pe.wait_ge(w_in["kv"], 32)
                for j in range(J):
                    ins = pe.matmul(S[0][:, 0, 12 * NB + j * 128:12 * NB + (j + 1) * 128], w_kd[:, j * 128:(j + 1) * 128],
                                    w_kvu[:], start=True, stop=True)
                ins.then_inc(p_pe, 1)
                pe.wait_ge(p_dve, ADA1)
                for j in range(J):
                    ins = pe.matmul(G[0:NB, 1, :], csil[:, j, :], w_ada[:, j, 0:2 * C], start=(j == 0), stop=(j == J - 1))
                ins.then_inc(p_pe, 1)
                pe.wait_ge(p_dve, BV_WIDE)
                pe.wait_ge(w_in["consts"], 64)
                for j in range(J):
                    ins = pe.matmul(S[0][0:NB, 1, 0:C], bv_wide[:, j, :], w_proj[:, j, :], start=(j == 0), stop=(j == J - 1))
                ins.then_inc(p_pe, 1)

            def tokens_to_channels(stage, b, bank, col):
                pe.wait_ge(sems[stage, "xn"], b + 1)
                for j in range(J):
                    ins = pe.transpose(G[:, bank, col + j * 128:col + (j + 1) * 128],
                                       xn[stage][:, j * 128:(j + 1) * 128], idf[:])
                ins.then_inc(sems[stage, "xt"], 1)

            def passes(x_parts, w_parts):
                return [(x_parts[0], w_parts[0]), (x_parts[1], w_parts[0]), (x_parts[0], w_parts[1])]

            def scores(stage, b, par, k, masked, turn):
                pe.wait_ge(sems[stage, "evq"], b + 1)
                if stage == "C":
                    pe.wait_ge(sems[stage, "evk"], b + 1)
                bank_free(pe, f"s{k}_{stage}", turn)
                if stage == "C":
                    for r in range(2):
                        pe.matmul(S[k][:, r, :], idb[:], winb[:].unsqueeze(1).broadcast_to([128, 4, 128]),
                                  start=True, stop=False, skip_group_check=True)
                elif masked:
                    for r in range(2):
                        pe.matmul(S[k][:, r, :], idf[:], msk_rel[:].unsqueeze(1).broadcast_to([128, 4, 128]),
                                  start=True, stop=False, skip_group_check=True)
                added = masked or stage == "C"
                for t in range(4):
                    for r in range(2):
                        rows = slice(64 * r, 64 * r + 48)
                        tk = KT + (4 * k + t if stage == "A" else k)
                        ins = pe.matmul(S[k][:, r, t * 128:(t + 1) * 128], tiles(stage, par, 4 * k + t, 1)[rows],
                                        tiles(stage, par, tk, 1)[rows], start=not added, stop=True,
                                        skip_group_check=True)
                ins.then_inc(sems[stage, f"s{k}"], 1)

            def shifted(stage, b, par, k, masked, turn):
                pe.wait_ge(c_in[stage], 32 * (b + 1))
                bank_free(pe, f"p{k}_{stage}", turn)
                if stage == "C":
                    for r in range(2):
                        pe.matmul(S[k][:, r, :], winb[:], idb[:].unsqueeze(1).broadcast_to([128, 4, 128]),
                                  start=True, stop=False, skip_group_check=True)
                    for r in range(2):
                        rows = slice(64 * r, 64 * r + 64)
                        ins = pe.matmul(S[k][:, r, :], tiles(stage, par, KT + k, 1)[rows],
                                        tiles(stage, par, 4 * k, 4)[rows], start=False, stop=True,
                                        skip_group_check=True)
                else:
                    if masked:
                        for r in range(2):
                            pe.matmul(S[k][:, r, :], msk_rel[:], idf[:].unsqueeze(1).broadcast_to([128, 4, 128]),
                                      start=True, stop=False, skip_group_check=True)
                    for t in range(4):
                        for r in range(2):
                            rows = slice(64 * r, 64 * r + 64)
                            ins = pe.matmul(S[k][:, r, t * 128:(t + 1) * 128], tiles(stage, par, KT + 4 * k + t, 1)[rows],
                                            tiles(stage, par, 4 * k + t, 1)[rows], start=not masked, stop=True,
                                            skip_group_check=True)
                ins.then_inc(sems[stage, f"p{k}"], 1)

            def output(stage, b, w, turn):
                pe.wait_ge(sems[stage, "oe"], b + 1)
                bank_free(pe, "o_" + stage, turn)
                for j in range(J):
                    ins = pe.matmul(G[:, BANK["o_" + stage], 0:C], oT[stage][:, j, :], w[:, j, :], start=(j == 0), stop=(j == J - 1))
                ins.then_inc(sems[stage, "o"], 1)

            def attention_out(s, b):
                pe.wait_ge(sems[s, "on"], b + 1)
                col = 0 if s == "A" else C
                for j in range(J):
                    ins = pe.transpose(G[:, BANK["ot"], col + j * 128:col + (j + 1) * 128],
                                       on[s][:, j * 128:(j + 1) * 128], idf[:])
                ins.then_inc(sems[s, "ot"], 1)

            def max_to_rows(s, b):
                pe.wait_ge(sems[s, "cl"], b + 1)
                col = 0 if s == "A" else 64
                pe.transpose(G[0:32, BANK["ct"], col:col + 64].bitcast(F16), cmax[s][:].rearrange("p r s t -> p (r s t)"),
                             idh[:]).then_inc(sems[s, "ct"], 1)

            def fc2(b, turn):
                pe.wait_ge(sems["M", "glo"], b + 1)
                if isinstance(b, int) and b == 0:
                    pe.wait_ge(w_split, 6)
                bank_free(pe, "fc2", turn)
                for k in range(NH):
                    for i, (g, w) in enumerate(passes((GH, GLo), w_fc2)):
                        ins = pe.matmul(G[:, BANK["fc2"], 0:C], g[:, k, :], w[:, k, :], start=(k == 0 and i == 0),
                                        stop=(k == NH - 1 and i == 2))
                ins.then_inc(sems["M", "fc2"], 1)

            def fc1(b, turn, half):
                ab = "ab"[half]
                pe.wait_ge(sems["M", "xl"], b + 1)
                if isinstance(b, int) and b == 0:
                    pe.wait_ge(w_split, 4)
                bank_free(pe, "fc1" + ab, turn)
                for k in range(4 * half, 4 * half + 4):
                    for i, (x_, w) in enumerate(passes((xh["M"], xl["M"]), w_fc1)):
                        for j in range(J):
                            ins = pe.matmul(G[:, BANK["fc1" + ab], (k % 4) * 128:(k % 4 + 1) * 128],
                                            w[:, j, k * 128:(k + 1) * 128], x_[:, j, :],
                                            start=(i == 0 and j == 0), stop=(i == 2 and j == J - 1))
                ins.then_inc(sems["M", "fc1" + ab], 1)

            def qkv_A(b, turn):
                pe.wait_ge(sems["A", "xl"], b + 1)
                if isinstance(b, int) and b == 0:
                    pe.wait_ge(w_split, 2)
                bank_free(pe, "qk", turn)
                bank_free(pe, "v", turn)
                for i, (x_, w) in enumerate(passes((xh["A"], xl["A"]), w_qkv)):
                    for j in range(J):
                        pe.matmul(G[:, BANK["v"], 0:C], x_[:, j, :], w[:, j, 2 * C:3 * C], start=(i == 0 and j == 0),
                                  stop=(i == 2 and j == J - 1))
                        ins = pe.matmul(G[:, BANK["qk"], :], x_[:, j, :], w[:, j, 0:2 * C], start=(i == 0 and j == 0),
                                        stop=(i == 2 and j == J - 1), skip_group_check=True)
                        if i == 0 and j == 0:
                            pe.matmul(G[:, BANK["qk"], 0:C], one3[:], qb3[:], start=False, stop=False,
                                      skip_group_check=True)
                ins.then_inc(sems["A", "qkv"], 1)

            def qkv_C(b, turn):
                pe.wait_ge(sems["C", "xl"], b + 1)
                if isinstance(b, int) and b == 0:
                    pe.wait_ge(w_split, 8)
                bank_free(pe, "qkv", turn)
                width = C + 2 * KV * D
                for i, (x_, w) in enumerate(passes((xh["C"], xl["C"]), w_l1)):
                    for j in range(J):
                        ins = pe.matmul(G[:, BANK["qkv"], 0:width], x_[:, j, :], w[:, j, :], start=(i == 0 and j == 0),
                                        stop=(i == 2 and j == J - 1))
                ins.then_inc(sems["C", "qkv"], 1)

            def pv_A(b, par, turn):
                for k in range(2):
                    pe.wait_ge(sems["A", f"e{k}"], b + 1)
                pe.wait_ge(sems["A", "v"], b + 1)
                bank_free(pe, "pv_A", turn)
                for h in range(H):
                    t, j = h // 2, h % 4
                    ins = pe.matmul(G[32 * j:32 * j + 32, BANK["pv_A"], (h // 4) * 128:(h // 4 + 1) * 128],
                                    V["A"][:, par, h, :], P["A"][:, t // 4, h % 2, (t % 4) * 128:(t % 4 + 1) * 128],
                                    start=True, stop=True)
                ins.then_inc(sems["A", "pv"], 1)

            def pv_C(b, par, turn):
                for k in range(2):
                    pe.wait_ge(sems["C", f"e{k}"], b + 1)
                pe.wait_ge(sems["C", "v"], b + 1)
                bank_free(pe, "pv_C", turn)
                for g in range(KV):
                    ins = pe.matmul(G[32 * g:32 * g + 32, BANK["pv_C"], :], V["C"][:, par, g, :],
                                    P["C"][:, g // 2, g % 2, :], start=True, stop=True)
                ins.then_inc(sems["C", "pv"], 1)

            def transpose_A(b, turn):
                pe.wait_ge(sems["A", "lo"], 2 * (b + 1))
                pe.wait_ge(sems["A", "dup"], 2 * (b + 1))
                bank_free(pe, "tr", turn)
                for kq in range(2):
                    for t in range(8):
                        ins = pe.transpose(S[1][:, kq, t * 64:(t + 1) * 64].bitcast(F16),
                                           stkA[:, kq, 2 * t:2 * t + 2, :].rearrange("p h w -> p (h w)"), idh[:])
                ins.then_inc(sems["A", "tr"], 1)

            def transpose_C(b, turn):
                pe.wait_ge(sems["C", "lo"], 2 * (b + 1))
                pe.wait_ge(sems["C", "dup"], 2 * (b + 1))
                bank_free(pe, "tr_q", turn)
                bank_free(pe, "tr_k", turn)
                for t in range((H + KV) // 2):
                    ins = pe.transpose(G[:, BANK["tr_q" if t < 8 else "tr_k"], (t % 8) * 64:(t % 8 + 1) * 64].bitcast(F16),
                                       stkC[:, 2 * t:2 * t + 2, :].rearrange("p h w -> p (h w)"), idh[:])
                ins.then_inc(sems["C", "tr"], 1)

            def transpose_sums(s, b, turn):
                pe.wait_ge(sems[s, "ou"], b + 1)
                bank_free(pe, "ut_" + s, turn)
                for t in range(4):
                    ins = pe.transpose(G[:, BANK["ut_" + s], t * 128:(t + 1) * 128], ou[s][:, t, :], idf[:])
                ins.then_inc(sems[s, "ut"], 1)

            def turn_pe(turn, par, masked):
                on_ = stages(turn)
                if isinstance(turn, int) and turn == 1:
                    pe.wait_ge(p_dve, GAM_ROWS)
                b = {s: turn - OFF[s] for s in OFF}
                if "A1" in on_:
                    bank_free(pe, "xt_A", turn)
                    tokens_to_channels("A", b["A1"], BANK["xt_A"], 0)
                if "A3" in on_ or "C3" in on_:
                    bank_free(pe, "ot", turn)
                if "C3" in on_:
                    attention_out("C", b["C3"])
                if "M1" in on_ or "C1" in on_:
                    bank_free(pe, "xt_MC", turn)
                if "C1" in on_:
                    tokens_to_channels("C", b["C1"], BANK["xt_MC"], C)
                if "M1" in on_:
                    tokens_to_channels("M", b["M1"], BANK["xt_MC"], 0)
                if "A3" in on_:
                    attention_out("A", b["A3"])
                if "M2" in on_:
                    fc2(b["M2"], turn)
                if "A2" in on_ or "C2" in on_:
                    bank_free(pe, "ct", turn)
                if "C2" in on_:
                    max_to_rows("C", b["C2"])
                if "A2" in on_:
                    max_to_rows("A", b["A2"])
                if "A3" in on_:
                    output("A", b["A3"], w_proj, turn)
                if "A1" in on_:
                    qkv_A(b["A1"], turn)
                    if isinstance(turn, int) and turn == 0:
                        later_products()
                if "M1" in on_:
                    fc1(b["M1"], turn, 0)
                if "A2" in on_:
                    shifted("A", b["A2"], parity("A2", par), 1, masked, turn)
                if "M1" in on_:
                    fc1(b["M1"], turn, 1)
                if "A2" in on_:
                    shifted("A", b["A2"], parity("A2", par), 0, masked, turn)
                if "C1" in on_:
                    qkv_C(b["C1"], turn)
                if "C2" in on_:
                    shifted("C", b["C2"], parity("C2", par), 1, masked, turn)
                    shifted("C", b["C2"], parity("C2", par), 0, masked, turn)
                if "C3" in on_:
                    output("C", b["C3"], w_o1, turn)
                if "A2" in on_:
                    pv_A(b["A2"], parity("A2", par), turn)
                if "A1" in on_:
                    transpose_A(b["A1"], turn)
                if "C2" in on_:
                    pv_C(b["C2"], parity("C2", par), turn)
                if "C1" in on_:
                    transpose_C(b["C1"], turn)
                if isinstance(turn, int) and turn == 0:
                    pe.wait_ge(p_dve, SLOT_READ)
                if "A1" in on_:
                    scores("A", b["A1"], parity("A1", par), 0, masked, turn)
                    scores("A", b["A1"], parity("A1", par), 1, masked, turn)
                if "C2" in on_:
                    transpose_sums("C", b["C2"], turn)
                if "A2" in on_:
                    transpose_sums("A", b["A2"], turn)
                if "C1" in on_:
                    scores("C", b["C1"], parity("C1", par), 0, masked, turn)
                    scores("C", b["C1"], parity("C1", par), 1, masked, turn)

            flag = pe.value_load(msk_flag[0:1, 0:1].bitcast(I32))
            with pe.If(flag):
                turns(pe, lambda turn, par: turn_pe(turn, par, True))
            with pe.Else():
                turns(pe, lambda turn, par: turn_pe(turn, par, False))


KT = 8
ROOT_STEPS = 19
SM_MIN = 5
SILU = 8
MASK_ROW = 13
QB_PARTS = 19
CONSTS = 22
ADA1 = 25
BV_WIDE = 26
SLOT_READ = 33
GAM_ROWS = 37


def _tables():
    freqs = (np.float32(1.0) / np.power(np.float32(10000.0), np.arange(0, D, 2, dtype=np.float32) / np.float32(D))
             ).astype(np.float32)
    emb = np.arange(T, dtype=np.float32)[:, None] * freqs[None, :]
    cos = np.concatenate([np.cos(emb), np.cos(emb)], -1).astype(np.float32)
    sin = np.concatenate([-np.sin(emb), np.sin(emb)], -1).astype(np.float32)
    inv = np.float32(1.0 / np.sqrt(D))

    def full(t):
        return np.concatenate([np.tile(t * inv, (1, H)), np.tile(t, (1, KV))], 1).astype(np.float32)

    i = np.arange(T)
    hidden = (np.abs(i[None, :] - i[:, None]) > 32) & ~(i % 64 == 0)[None, :]
    return full(cos) / np.float32(WS), full(sin) / np.float32(WS), np.where(hidden, np.float32(NEG), np.float32(0.0)), np.eye(128, dtype=np.float32)


def kernel(**inputs):
    import concourse.bacc as bacc
    from concourse.bass_utils import run_bass_kernel_spmd

    a = {k: np.asarray(v) for k, v in inputs.items()}

    def chunks(w):
        return np.ascontiguousarray(w.T.reshape(-1, 128, w.shape[0]).transpose(1, 0, 2))

    def col(v):
        return np.ascontiguousarray(v.reshape(-1, 128).T)

    d = np.arange(D)
    q_order = np.concatenate([(4 * (2 * s + r) + i) * D + d for s in range(2) for i in range(4) for r in range(2)])
    o_order = np.concatenate([(4 * g + i) * D + d for i in range(4) for g in range(KV)])
    cos_t, sin_t, window, ident = _tables()
    data = {
        "x": a["x"],
        "cond_t": np.ascontiguousarray(a["cond_2048"].T.reshape(J, 128, NB).transpose(1, 0, 2)),
        "mask": a["mask_1x1xSxS_ff0"].reshape(T, T),
        "wqkv": chunks(a["L0_cond_Wqkv"]),
        "qbias": a["L0_cond_q_bias"].reshape(1, C),
        "vbias": col(a["L0_cond_v_bias"]),
        "sml": a["L0_cond_scale_mul_log"].reshape(1, H),
        "wproj": chunks(a["L0_cond_Wproj"]),
        "bproj": a["L0_cond_bproj"].reshape(1, C),
        "wada": chunks(a["L0_cond_Wada"]),
        "bada_row": np.ascontiguousarray(a["L0_cond_bada"][:2 * C]).reshape(1, 2 * C),
        "bada_col": col(a["L0_cond_bada"]),
        "wfc1": chunks(a["L0_cond_Wfc1"]),
        "bfc1": col(a["L0_cond_bfc1"]),
        "wfc2": chunks(a["L0_cond_Wfc2"]),
        "bfc2": a["L0_cond_bfc2"].reshape(1, C),
        "wada1": chunks(a["L1_cond_W_ada"]),
        "bada1": col(a["L1_cond_b_ada"]),
        "wq1": chunks(a["L1_cond_Wq"][q_order]),
        "wkd": a["L1_cond_Wkd"],
        "wkvu": np.ascontiguousarray(np.concatenate([a["L1_cond_Wku"], a["L1_cond_Wvu"]], 0).T),
        "wo1": chunks(a["L1_cond_Wo"][:, o_order]),
        "ident": ident, "cos_t": cos_t, "sin_t": sin_t, "window": window,
    }
    nc = bacc.Bacc("TRN2", target_bir_lowering=False, num_devices=1)
    arrays, args = {}, {}
    for name, v in data.items():
        v = np.ascontiguousarray(v)
        arrays[f"in_{name}"] = v
        args[name] = nc.dram_tensor(f"in_{name}", v.shape, mybir.dt.from_np(v.dtype), kind="ExternalInput").ap()
    args["out"] = nc.dram_tensor("out_0", (NB, T, C), F32, kind="ExternalOutput").ap()
    block_pair(nc, **args)
    r = run_bass_kernel_spmd(nc, [arrays], core_ids=[0])
    return r.results[0]["out_0"]
```
